# Optimizing a Trainium2 kernel written in Bass

```python
import numpy as np
import jax
import jax.numpy as jnp

def _softmax(x, axis=-1):
    return jax.nn.softmax(x, axis=axis)

def _gelu(x):
    return jax.nn.gelu(x, approximate=True)

def _silu(x):
    return jax.nn.silu(x)

def _sigmoid(x):
    return jax.nn.sigmoid(x)

def _layernorm(x, axis=-1, eps=1e-05):
    m = jnp.mean(x, axis=axis, keepdims=True)
    v = jnp.var(x, axis=axis, keepdims=True)
    return (x - m) / jnp.sqrt(v + eps)

def _scatter_add(tgt, idx, src, axis=0):
    return tgt.at[idx].add(src)

def _segment_sum(src, seg, n):
    return jax.ops.segment_sum(src, seg, n)
kernel_name = 'mk_flamingo_gated_d2_seqx_r4_26088d'

def setup_inputs(seed: int=0):
    np.random.seed(seed)
    _w = jnp.asarray

    def _rec_inputs():
        import jax
        import jax.numpy as jnp
        _rk = jax.random.key(seed)
        x = -0.0003929 + 0.9999 * jax.random.normal(jax.random.fold_in(_rk, 1), (16, 128, 512), jnp.float32)
        _lenS = 128 - jax.random.randint(jax.random.fold_in(_rk, 7), (16,), 0, max(1, 128 // 4) + 1, jnp.int32)
        _lenS2 = 128 - jax.random.randint(jax.random.fold_in(_rk, 8), (16,), 0, max(1, 128 // 4) + 1, jnp.int32)
        _ctx_2048P = jax.random.normal(jax.random.fold_in(_rk, 11), (16, 16, 512), jnp.float32)
        _ctx_2048c = jax.random.dirichlet(jax.random.fold_in(_rk, 511), 0.3 * jnp.ones((16,), jnp.float32), (16, 128))
        _ctx_2048t = jnp.einsum('bsk,bkd->bsd', _ctx_2048c, _ctx_2048P)
        _ctx_2048t = _ctx_2048t * jax.lax.rsqrt(jnp.mean(jnp.square(_ctx_2048t)) + 1e-12) * 0.953939
        ctx_2048 = 1.72703e-05 + 1.00003 * (_ctx_2048t + 0.3 * jax.random.normal(jax.random.fold_in(_rk, 611), (16, 128, 512), jnp.float32))
        _g = jax.random.normal(jax.random.fold_in(_rk, 9001), (2, 2), jnp.float32)
        _g = jnp.sign(_g) * jnp.maximum(jnp.abs(_g), 1.0) + (_g == 0) * 1.0
        g_xattn = _g[0]
        g_ffn = _g[1]
        return (x, ctx_2048, g_xattn, g_ffn)
    x, ctx_2048, g_xattn, g_ffn = _rec_inputs()

    def _L0_xattn_setup():
        import jax, jax.numpy as jnp
        import numpy as np
        DIM = 512
        H = 16
        D = 128
        INNER = H * D
        N_IMG = 257
        EPS = 1e-06

        def rms_norm(x, scale, eps=EPS):
            ms = jnp.mean(jnp.square(x), axis=-1, keepdims=True)
            return x * jax.lax.rsqrt(ms + eps) * scale

        def sdpa(q, k, v):
            scale = 1.0 / jnp.sqrt(jnp.asarray(D, q.dtype))
            scores = jnp.einsum('bshd,blhd->bhsl', q, k) * scale
            attn = jax.nn.softmax(scores, axis=-1)
            return jnp.einsum('bhsl,blhd->bshd', attn, v)
        key = jax.random.key(seed)
        ks = jax.random.split(key, 16)
        std = 1.0 / np.sqrt(DIM)
        inp = {'x': jax.random.normal(ks[0], (2, 1024, DIM), jnp.float32), 'context': jax.random.normal(ks[1], (2, 769, DIM), jnp.float32), 'q_w': jax.random.normal(ks[2], (DIM, INNER), jnp.float32) * std, 'q_b': jnp.zeros((INNER,), jnp.float32), 'k_w': jax.random.normal(ks[3], (DIM, INNER), jnp.float32) * std, 'k_b': jnp.zeros((INNER,), jnp.float32), 'v_w': jax.random.normal(ks[4], (DIM, INNER), jnp.float32) * std, 'v_b': jnp.zeros((INNER,), jnp.float32), 'ki_w': jax.random.normal(ks[5], (DIM, INNER), jnp.float32) * std, 'ki_b': jnp.zeros((INNER,), jnp.float32), 'vi_w': jax.random.normal(ks[6], (DIM, INNER), jnp.float32) * std, 'vi_b': jnp.zeros((INNER,), jnp.float32), 'o_w': jax.random.normal(ks[7], (INNER, DIM), jnp.float32) * std, 'o_b': jnp.zeros((DIM,), jnp.float32), 'nq_s': jnp.ones((INNER,), jnp.float32), 'nkt_s': jnp.ones((INNER,), jnp.float32), 'nki_s': jnp.ones((INNER,), jnp.float32)}
        return inp
    _L0_xattn_all = _L0_xattn_setup()
    _L0_xattn_in = {k: v for k, v in _L0_xattn_all.items() if k in ('q_w', 'q_b', 'k_w', 'k_b', 'v_w', 'v_b', 'ki_w', 'ki_b', 'vi_w', 'vi_b', 'o_w', 'o_b', 'nq_s', 'nkt_s', 'nki_s')}
    del _L0_xattn_all

    def _L0_ffn_setup():
        import jax, jax.numpy as jnp
        import numpy as np
        TOP_K = 2
        key = jax.random.key(seed)
        ks = jax.random.split(key, 6)
        B, S, H, F, E = (1, 512, 512, 352, 8)
        Fs = 2 * F
        std = jnp.float32(0.02)
        return {'hidden_states': jax.random.normal(ks[0], (B, S, H), jnp.float32), 'gate_weight': jax.random.normal(ks[1], (E, H), jnp.float32) * std, 'gate_up_weights': jax.random.normal(ks[2], (E, 2 * F, H), jnp.float32) * std, 'down_weights': jax.random.normal(ks[3], (E, H, F), jnp.float32) * std, 'shared_gate_up': jax.random.normal(ks[4], (2 * Fs, H), jnp.float32) * std, 'shared_down': jax.random.normal(ks[5], (H, Fs), jnp.float32) * std}
    _L0_ffn_all = _L0_ffn_setup()
    _L0_ffn_in = {k: v for k, v in _L0_ffn_all.items() if k in ('gate_weight', 'gate_up_weights', 'down_weights', 'shared_gate_up', 'shared_down')}
    del _L0_ffn_all

    def _L1_xattn_setup():
        import jax, jax.numpy as jnp
        import numpy as np
        B, S, D, H = (4, 1024, 512, 16)
        HD = D // H
        key = jax.random.key(seed)
        ks = jax.random.split(key, 12)
        sc = 1.0 / np.sqrt(D)
        inp = {'q': jax.random.normal(ks[0], (B, S, D), jnp.float32), 'k': jax.random.normal(ks[1], (B, S, D), jnp.float32), 'v': jax.random.normal(ks[2], (B, S, D), jnp.float32), 'Wq': jax.random.normal(ks[3], (D, D), jnp.float32) * sc, 'bq': jnp.zeros((D,), jnp.float32), 'Wk': jax.random.normal(ks[4], (D, D), jnp.float32) * sc, 'bk': jnp.zeros((D,), jnp.float32), 'Wv': jax.random.normal(ks[5], (D, D), jnp.float32) * sc, 'bv': jnp.zeros((D,), jnp.float32), 'Wo': jax.random.normal(ks[6], (D, D), jnp.float32) * sc, 'bo': jnp.zeros((D,), jnp.float32)}
        return inp
    _L1_xattn_all = _L1_xattn_setup()
    _L1_xattn_in = {k: v for k, v in _L1_xattn_all.items() if k in ('Wq', 'bq', 'Wk', 'bk', 'Wv', 'bv', 'Wo', 'bo')}
    del _L1_xattn_all

    def _L1_ffn_setup():
        import jax, jax.numpy as jnp
        import numpy as np
        EPS = 1e-08

        def _bit_quant(w):
            scale = jnp.maximum(jnp.mean(jnp.abs(w)), EPS)
            w_ternary = jnp.clip(jnp.round(w / scale), -1.0, 1.0)
            return w + jax.lax.stop_gradient(w_ternary - w)
        key = jax.random.key(seed)
        k = jax.random.split(key, 5)
        emb, dff = (512, 2048)
        B, S = (4, 512)
        x = jax.random.normal(k[0], (B, S, emb), dtype=jnp.float32)
        w1 = jax.random.normal(k[1], (dff, emb), dtype=jnp.float32) * 0.02
        b1 = jax.random.normal(k[2], (dff,), dtype=jnp.float32) * 0.02
        w2 = jax.random.normal(k[3], (emb, dff), dtype=jnp.float32) * 0.02
        b2 = jax.random.normal(k[4], (emb,), dtype=jnp.float32) * 0.02
        return {'x': x, 'w1': w1, 'b1': b1, 'w2': w2, 'b2': b2}
    _L1_ffn_all = _L1_ffn_setup()
    _L1_ffn_in = {k: v for k, v in _L1_ffn_all.items() if k in ('w1', 'b1', 'w2', 'b2')}
    del _L1_ffn_all
    return {'x': x, 'ctx_2048': ctx_2048, 'g_xattn': g_xattn, 'g_ffn': g_ffn, 'L0_xattn_q_w': _L0_xattn_in['q_w'], 'L0_xattn_q_b': _L0_xattn_in['q_b'], 'L0_xattn_k_w': _L0_xattn_in['k_w'], 'L0_xattn_k_b': _L0_xattn_in['k_b'], 'L0_xattn_v_w': _L0_xattn_in['v_w'], 'L0_xattn_v_b': _L0_xattn_in['v_b'], 'L0_xattn_ki_w': _L0_xattn_in['ki_w'], 'L0_xattn_ki_b': _L0_xattn_in['ki_b'], 'L0_xattn_vi_w': _L0_xattn_in['vi_w'], 'L0_xattn_vi_b': _L0_xattn_in['vi_b'], 'L0_xattn_o_w': _L0_xattn_in['o_w'], 'L0_xattn_o_b': _L0_xattn_in['o_b'], 'L0_xattn_nq_s': _L0_xattn_in['nq_s'], 'L0_xattn_nkt_s': _L0_xattn_in['nkt_s'], 'L0_xattn_nki_s': _L0_xattn_in['nki_s'], 'L0_ffn_gate_weight': _L0_ffn_in['gate_weight'], 'L0_ffn_gate_up_weights': _L0_ffn_in['gate_up_weights'], 'L0_ffn_down_weights': _L0_ffn_in['down_weights'], 'L0_ffn_shared_gate_up': _L0_ffn_in['shared_gate_up'], 'L0_ffn_shared_down': _L0_ffn_in['shared_down'], 'L1_xattn_Wq': _L1_xattn_in['Wq'], 'L1_xattn_bq': _L1_xattn_in['bq'], 'L1_xattn_Wk': _L1_xattn_in['Wk'], 'L1_xattn_bk': _L1_xattn_in['bk'], 'L1_xattn_Wv': _L1_xattn_in['Wv'], 'L1_xattn_bv': _L1_xattn_in['bv'], 'L1_xattn_Wo': _L1_xattn_in['Wo'], 'L1_xattn_bo': _L1_xattn_in['bo'], 'L1_ffn_w1': _L1_ffn_in['w1'], 'L1_ffn_b1': _L1_ffn_in['b1'], 'L1_ffn_w2': _L1_ffn_in['w2'], 'L1_ffn_b2': _L1_ffn_in['b2']}

def reference(x, ctx_2048, g_xattn, g_ffn, L0_xattn_q_w, L0_xattn_q_b, L0_xattn_k_w, L0_xattn_k_b, L0_xattn_v_w, L0_xattn_v_b, L0_xattn_ki_w, L0_xattn_ki_b, L0_xattn_vi_w, L0_xattn_vi_b, L0_xattn_o_w, L0_xattn_o_b, L0_xattn_nq_s, L0_xattn_nkt_s, L0_xattn_nki_s, L0_ffn_gate_weight, L0_ffn_gate_up_weights, L0_ffn_down_weights, L0_ffn_shared_gate_up, L0_ffn_shared_down, L1_xattn_Wq, L1_xattn_bq, L1_xattn_Wk, L1_xattn_bk, L1_xattn_Wv, L1_xattn_bv, L1_xattn_Wo, L1_xattn_bo, L1_ffn_w1, L1_ffn_b1, L1_ffn_w2, L1_ffn_b2):
    import jax
    import jax.numpy as jnp

    def _L0_xattn_ref(x, context, q_w, q_b, k_w, k_b, v_w, v_b, ki_w, ki_b, vi_w, vi_b, o_w, o_b, nq_s, nkt_s, nki_s):
        import jax, jax.numpy as jnp
        import numpy as np
        DIM = 512
        H = 16
        D = 128
        INNER = H * D
        N_IMG = 257
        EPS = 1e-06

        def rms_norm(x, scale, eps=EPS):
            ms = jnp.mean(jnp.square(x), axis=-1, keepdims=True)
            return x * jax.lax.rsqrt(ms + eps) * scale

        def sdpa(q, k, v):
            scale = 1.0 / jnp.sqrt(jnp.asarray(D, q.dtype))
            scores = jnp.einsum('bshd,blhd->bhsl', q, k) * scale
            attn = jax.nn.softmax(scores, axis=-1)
            return jnp.einsum('bhsl,blhd->bshd', attn, v)
        B, S, _ = x.shape
        img_ctx = context[:, :N_IMG]
        txt_ctx = context[:, N_IMG:]
        q = rms_norm(x @ q_w + q_b, nq_s).reshape(B, S, H, D)
        k_txt = rms_norm(txt_ctx @ k_w + k_b, nkt_s).reshape(B, -1, H, D)
        v_txt = (txt_ctx @ v_w + v_b).reshape(B, -1, H, D)
        out_txt = sdpa(q, k_txt, v_txt)
        k_img = rms_norm(img_ctx @ ki_w + ki_b, nki_s).reshape(B, -1, H, D)
        v_img = (img_ctx @ vi_w + vi_b).reshape(B, -1, H, D)
        out_img = sdpa(q, k_img, v_img)
        out = (out_txt + out_img).reshape(B, S, INNER)
        return out @ o_w + o_b

    def _L0_ffn_ref(hidden_states, gate_weight, gate_up_weights, down_weights, shared_gate_up, shared_down):
        import jax, jax.numpy as jnp
        import numpy as np
        TOP_K = 2
        B, S, H = hidden_states.shape
        E, twoF, _ = gate_up_weights.shape
        F = twoF // 2
        T = B * S
        x = hidden_states.reshape(T, H)
        logits = x @ gate_weight.T
        scores = jax.nn.softmax(logits, axis=-1)
        topk_w, topk_idx = jax.lax.top_k(scores, TOP_K)
        combine = jnp.zeros((T, E), x.dtype).at[jnp.arange(T)[:, None], topk_idx].add(topk_w)
        gu = jnp.einsum('th,efh->tef', x, gate_up_weights)
        act = jax.nn.silu(gu[..., :F]) * gu[..., F:]
        y = jnp.einsum('tef,te,ehf->th', act, combine, down_weights)
        Fs = shared_gate_up.shape[0] // 2
        sgu = x @ shared_gate_up.T
        sact = jax.nn.silu(sgu[:, :Fs]) * sgu[:, Fs:]
        y = y + sact @ shared_down.T
        return y.reshape(B, S, H)

    def _L1_xattn_ref(q, k, v, Wq, bq, Wk, bk, Wv, bv, Wo, bo):
        import jax, jax.numpy as jnp
        import numpy as np
        B, S, D, H = (4, 1024, 512, 16)
        HD = D // H
        bs, sl, nf = q.shape
        Q = (q @ Wq.T + bq).reshape(bs, sl, H, HD)
        K = (k @ Wk.T + bk).reshape(bs, sl, H, HD)
        V = (v @ Wv.T + bv).reshape(bs, sl, H, HD)
        score = jnp.einsum('bshd,bsgd->bshg', Q, K)
        weight = jax.nn.softmax(score, axis=-1)
        attn = jnp.einsum('bshg,bsgd->bshd', weight, V).reshape(bs, sl, nf)
        return attn @ Wo.T + bo

    def _L1_ffn_ref(x, w1, b1, w2, b2):
        import jax, jax.numpy as jnp
        import numpy as np
        EPS = 1e-08

        def _bit_quant(w):
            scale = jnp.maximum(jnp.mean(jnp.abs(w)), EPS)
            w_ternary = jnp.clip(jnp.round(w / scale), -1.0, 1.0)
            return w + jax.lax.stop_gradient(w_ternary - w)
        w1q = _bit_quant(w1)
        w2q = _bit_quant(w2)
        h = jnp.einsum('bsd,fd->bsf', x, w1q) + b1
        h = jax.nn.gelu(h, approximate=False)
        return jnp.einsum('bsf,df->bsd', h, w2q) + b2
    x = x + jnp.tanh(g_xattn[0]) * _L0_xattn_ref(_layernorm(x, axis=-1), ctx_2048, L0_xattn_q_w, L0_xattn_q_b, L0_xattn_k_w, L0_xattn_k_b, L0_xattn_v_w, L0_xattn_v_b, L0_xattn_ki_w, L0_xattn_ki_b, L0_xattn_vi_w, L0_xattn_vi_b, L0_xattn_o_w, L0_xattn_o_b, L0_xattn_nq_s, L0_xattn_nkt_s, L0_xattn_nki_s)
    x = x + jnp.tanh(g_ffn[0]) * _L0_ffn_ref(_layernorm(x, axis=-1), L0_ffn_gate_weight, L0_ffn_gate_up_weights, L0_ffn_down_weights, L0_ffn_shared_gate_up, L0_ffn_shared_down)
    x = x + jnp.tanh(g_xattn[1]) * _L1_xattn_ref(_layernorm(x, axis=-1), ctx_2048, ctx_2048, L1_xattn_Wq, L1_xattn_bq, L1_xattn_Wk, L1_xattn_bk, L1_xattn_Wv, L1_xattn_bv, L1_xattn_Wo, L1_xattn_bo)
    x = x + jnp.tanh(g_ffn[1]) * _L1_ffn_ref(_layernorm(x, axis=-1), L1_ffn_w1, L1_ffn_b1, L1_ffn_w2, L1_ffn_b2)
    return x

_drawn_inputs = setup_inputs


def setup_inputs(seed=0):
    import zlib

    import numpy as np

    out = dict(_drawn_inputs(seed))
    spreads = {'g_ffn': (-1.0, 0.2),
     'L0_xattn_q_b': (0.0, 0.275),
     'L0_xattn_k_b': (0.0, 0.1),
     'L0_xattn_v_b': (0.0, 0.1),
     'L0_xattn_ki_b': (0.0, 0.8),
     'L0_xattn_vi_b': (0.0, 0.1),
     'L0_xattn_o_b': (0.0, 0.1),
     'L0_xattn_nq_s': (1.0, 0.2),
     'L0_xattn_nkt_s': (1.0, 0.2),
     'L0_xattn_nki_s': (1.0, 0.2),
     'L1_xattn_bq': (0.0, 1.637),
     'L1_xattn_bk': (0.0, 1.537),
     'L1_xattn_bv': (0.0, 2.0),
     'L1_xattn_bo': (0.0, 2.0)}
    factors = {'L0_ffn_gate_weight': 7.772,
     'L0_ffn_gate_up_weights': 6.835,
     'L0_ffn_down_weights': 6.826,
     'L1_ffn_b1': 51.909,
     'L1_ffn_b2': 200.0,
     'L0_ffn_shared_gate_up': 8.0,
     'L0_ffn_shared_down': 8.0}
    for name, (base, spread) in spreads.items():
        noise = np.random.default_rng([zlib.crc32(name.encode()), seed]).standard_normal(out[name].shape)
        drawn = base * np.exp(spread * noise) if base else spread * noise
        out[name] = jnp.asarray(drawn.astype(out[name].dtype))
    for name, factor in factors.items():
        out[name] = (out[name] * factor).astype(out[name].dtype)
    return out
```

```python
from contextlib import ExitStack

import concourse.bass as bass
from concourse import mybir

P = 128
F32 = mybir.dt.float32
F32R = mybir.dt.float32r
U32 = mybir.dt.uint32
I32 = mybir.dt.int32
ALU = mybir.AluOpType
ACT = mybir.ActivationFunctionType
AX = mybir.AxisListType

BLK = 512
TPB = BLK // P
LN_EPS = 1e-5
RMS_EPS = 1e-6
PASSES = ((0, 0), (0, 1), (1, 0))


def f32(ap):
    return ap.bitcast(F32)


def l0_attention(nc, new_sem, x, ctxT, W, x1):
    T, D = x.shape
    KC = D // P
    H = W["q_w"].shape[1] // P
    NBLK = T // BLK
    G = H // 4
    ORDER = [("k", g) for g in range(G)] + [("v", 0)] + [("q", g) for g in range(G)] + [("v", g) for g in range(1, G)]
    AT = {kg: i for i, kg in enumerate(ORDER)}
    O0 = 3 * G
    NW = 4 * G
    NP = 4 * O0
    NU = TPB * G
    INNER = H * P
    TURN_LAG, AV_LAG = 3, 4

    with ExitStack() as c:
        def sb(name, shape, dt=F32):
            return c.enter_context(nc.sbuf_tensor("a_" + name, shape, dt))

        def sem(name):
            return new_sem("a_" + name)

        def psum(name, shape):
            return c.enter_context(nc.psum_tensor("a_" + name, shape, F32))

        proj = psum("proj", [P, 4, BLK])
        sc_ps = psum("scores", [P, 2, BLK])
        tr_ps = psum("turned", [P, 2, BLK])

        w_raw = sb("w_raw", [P, 2, KC, BLK])
        w_hl = sb("w_hl", [P, 2, 2, KC, BLK], F32R)
        a_hl = sb("a_hl", [P, 2, KC, BLK], F32R)
        c_hl = sb("c_hl", [P, 2, KC, BLK], F32R)
        c_raw = sb("c_raw", [P, 2, BLK])
        kT = sb("kT", [P, H, BLK])
        qT = sb("qT", [P, H, BLK])
        v = sb("v", [P, TPB, INNER])
        probs = sb("probs", [P, 4, 4, P])
        xr = sb("xr", [P, 2, D])
        sq = sb("sq", [P, 2, BLK])
        ssum = sb("ssum", [P, BLK])
        rk = sb("rk", [P, TPB])
        rk_diag = sb("rk_diag", [P, TPB, P])
        rq = sb("rq", [P, TPB])
        ident = sb("ident", [P, P])
        ones = sb("ones", [P, P])
        mhalf = sb("mhalf", [P, 1])
        vecs = sb("vecs", [P, 5, H])
        nqk = sb("nqk", [P, H])
        tg_ob = sb("tg_ob", [P, D])
        gate = sb("gate", [P, 1])
        tg = sb("tg", [P, 1])
        stats = sb("stats", [P, 2, 6])
        mv = sb("mv", [P, 2, 2])
        rstd = sb("rstd", [P, 2, 1])
        mx = sb("mx", [P, 4, 4])
        den = sb("den", [P, 4, 4])
        rden = sb("rden", [P, 4, 4])
        q_b, k_b, v_b, nk, nq = (vecs[:, n, :] for n in range(5))

        const_in = sem("const_in")
        const_made = sem("const_made")
        tg_ready = sem("tg_ready")
        const_done = sem("const_done")
        w_in = [sem(f"w_in{s}") for s in range(2)]
        w_high = sem("w_high")
        w_split = sem("w_split")
        c_in = [sem(f"c_in{s}") for s in range(2)]
        c_high = sem("c_high")
        c_split = sem("c_split")
        x_in = [sem(f"x_in{s}") for s in range(2)]
        r_in = [sem(f"r_in{s}") for s in range(4)]
        ln_stats = sem("ln_stats")
        ln_seen = sem("ln_seen")
        ln_mv = sem("ln_mv")
        ln_eps = sem("ln_eps")
        ln_rstd = sem("ln_rstd")
        ln_done = sem("ln_done")
        h_turned = sem("h_turned")
        h_high = sem("h_high")
        h_split = sem("h_split")
        proj_ready = sem("proj_ready")
        proj_copied = sem("proj_copied")
        proj_squared = sem("proj_squared")
        sq_added = sem("sq_added")
        ss_ready = sem("ss_ready")
        ss_eps = sem("ss_eps")
        ss_pow = sem("ss_pow")
        rk_spread = sem("rk_spread")
        rk_ready = sem("rk_ready")
        k_normed = sem("k_normed")
        s_ready = sem("s_ready")
        s_max = sem("s_max")
        s_sub = sem("s_sub")
        e_ready = sem("e_ready")
        e_sum = sem("e_sum")
        e_rec = sem("e_rec")
        p_ready = sem("p_ready")
        pt_ready = sem("pt_ready")
        pt_copied = sem("pt_copied")
        av_ready = sem("av_ready")
        av_copied = sem("av_copied")
        a_high = sem("a_high")
        a_split = sem("a_split")
        a_used = sem("a_used")
        o_ready = sem("o_ready")
        o_scaled = sem("o_scaled")
        o_done = sem("o_done")
        x_out = [sem(f"x_out{s}") for s in range(4)]

        def by_columns(w):
            return w.rearrange("(k p) (g n) -> g p k n", p=P, n=BLK)

        names = {"k": "ki_w", "v": "vi_w", "q": "q_w"}
        groups = ([by_columns(W[names[kind]])[g] for kind, g in ORDER]
                  + [W["o_w"].rearrange("(g k p) n -> g p k n", p=P, k=4)[g] for g in range(G)])
        x_t = x.rearrange("(b n p) d -> n b p d", p=P, n=TPB)
        x1_t = x1.rearrange("(b n p) d -> n b p d", p=P, n=TPB)
        ctx_t = ctxT.rearrange("(k p) (b t) -> k b p t", p=P, t=BLK)
        residual = [xr[:, 0, :], xr[:, 1, :], sq[:, 0, :], sq[:, 1, :]]
        NA = 4 * G - 1
        NSQ = H - 1

        def square_slot_free(n):
            return 0 if n < 2 else max(1, n - 2)

        block = c.enter_context(nc.Block())

        @block.sync
        def _(sp):
            sp.dma_start(vecs[:], W["vecs"]).then_inc(const_in, 16)
            sp.dma_start(tg_ob[:], W["o_b"].to_broadcast([P, D])).then_inc(const_in, 16)
            sp.dma_start(gate[:], W["gate"].to_broadcast([P, 1])).then_inc(const_in, 16)
            sp.sem_inc(w_split, 2)
            sp.sem_inc(c_split, 2)

            def load_w(n, i):
                sp.wait_ge(w_split, n + 1)
                sp.dma_start(w_raw[:, i % 2], groups[i]).then_inc(w_in[i % 2], 16)

            def load_ctx(n, b, k):
                sp.wait_ge(c_split, n + k + 1)
                sp.dma_start(c_raw[:, k % 2, :], ctx_t[k][b]).then_inc(c_in[k % 2], 16)

            load_ctx(0, 0, 0)
            load_ctx(0, 0, 1)
            load_w(0, 0)
            load_ctx(0, 0, 2)
            load_ctx(0, 0, 3)
            load_w(1, 1)
            with sp.Fori(0, NBLK) as t:
                def load_x(j):
                    if j < 2:
                        sp.wait_ge(x_out[j], 16 * t + 16)
                    else:
                        sp.wait_ge(h_turned, TPB * t + j - 1)
                    sp.dma_start(xr[:, j % 2, :], x_t[j][t]).then_inc(x_in[j % 2], 16)

                load_x(0)
                load_x(1)
                for i in range(NW):
                    load_w(NW * t + i + 2, (i + 2) % NW)
                    if i < 2:
                        load_x(i + 2)
                    if i == O0 - 1:
                        for j in range(TPB):
                            if j < 2:
                                sp.wait_ge(h_turned, TPB * t + TPB)
                            else:
                                sp.wait_ge(sq_added, 2 * NSQ * t + 2 * NSQ + 1)
                            sp.dma_start(residual[j], x_t[j][t]).then_inc(r_in[j], 16)
                    if i in (O0 - 2, O0 - 1):
                        for k in (0, 1) if i == O0 - 2 else (2, 3):
                            load_ctx(KC * t + KC, (t + 1) % NBLK, k)
                for j in range(TPB):
                    sp.wait_ge(o_done, TPB * t + j + 1)
                    sp.dma_start(x1_t[j][t], residual[j]).then_inc(x_out[j], 16)
            for j in range(TPB):
                sp.wait_ge(x_out[j], 16 * NBLK + 16)

        @block.gpsimd
        def _(pool):
            for j in range(TPB):
                pool.sem_inc(x_out[j], 16)
            pool.sem_inc(sq_added, 1)
            pool.sem_inc(ss_ready, 1)
            pool.memset(ones[:], 1.0).then_inc(const_made, 1)
            pool.memset(mhalf[:], -0.5).then_inc(const_made, 1)
            pool.wait_ge(const_made, 2)
            pool.affine_select(out=ident[:], in_=ones[:], compare_op=ALU.is_equal, fill=0.0, base=0,
                               pattern=[[-1, P]], channel_multiplier=1).then_inc(const_made, 1)

            def w_low(n, i):
                pool.wait_ge(w_high, n + 1)
                s = i % 2
                pool.tensor_tensor(w_hl[:, s, 1], w_raw[:, s], f32(w_hl[:, s, 0]), ALU.subtract)\
                    .then_inc(w_split, 1)

            def c_low(n, k):
                pool.wait_ge(c_high, n + k + 1)
                pool.tensor_tensor(c_hl[:, 1, k, :], c_raw[:, k % 2, :], f32(c_hl[:, 0, k, :]), ALU.subtract)\
                    .then_inc(c_split, 1)

            for k in range(KC):
                c_low(0, k)
            w_low(0, 0)
            w_low(1, 1)
            with pool.Fori(0, NBLK) as t:
                def add_square(half, n):
                    if n == 0:
                        return
                    base = 2 * NSQ * t + half * NSQ + 1
                    pool.wait_ge(proj_squared, 2 * H * t + half * H + n + 1)
                    pool.wait_ge(sq_added, base + n - 1)
                    if n == 1:
                        pool.wait_ge(ss_ready, 2 * t + half + 1)
                        first = sq[:, 0, :]
                    else:
                        first = ssum[:]
                    pool.tensor_tensor(ssum[:], first, sq[:, n % 2, :], ALU.add).then_inc(sq_added, 1)

                def power(half, dst, width):
                    pool.wait_ge(ss_eps, 2 * t + half + 1)
                    pool.tensor_tensor(dst, dst, mhalf[:, 0:1].to_broadcast([P, width]), ALU.pow)\
                        .then_inc(ss_pow, 1)

                for i in range(NW):
                    if i < TPB:
                        pool.wait_ge(ln_eps, TPB * t + i + 1)
                        pool.tensor_tensor(rstd[:, i % 2, :], rstd[:, i % 2, :], mhalf[:], ALU.pow)\
                            .then_inc(ln_rstd, 1)
                    if i < O0 and ORDER[i][0] in "kq":
                        for j in range(4):
                            add_square("kq".index(ORDER[i][0]), 4 * ORDER[i][1] + j)
                    if i == AT["v", 0]:
                        power(0, rk[:], TPB)
                    if i == AT["v", 1]:
                        power(1, rq[:], TPB)
                    if i == O0 - 1:
                        w_low(NW * t + i + 2, i + 2)
                        for u in range(NU):
                            pool.wait_ge(e_rec, NU * t + u + 1)
                            pool.tensor_tensor(probs[:, u % 4], probs[:, u % 4],
                                               rden[:, u % 4].unsqueeze(2).to_broadcast([P, 4, P]), ALU.mult)\
                                .then_inc(p_ready, 1)
                            if u % 4 == 3:
                                c_low(KC * t + KC, u // 4)
                    else:
                        w_low(NW * t + i + 2, (i + 2) % NW)

        @block.scalar
        def _(act):
            act.wait_ge(const_in, 16 * 3)
            act.activation(tg[:], gate[:], ACT.Tanh).then_inc(tg_ready, 1)

            def w_high_part(loads, i):
                act.wait_ge(w_in[i % 2], 16 * loads)
                act.activation(w_hl[:, i % 2, 0], w_raw[:, i % 2], ACT.Copy).then_inc(w_high, 1)

            def c_high_part(loads, k):
                act.wait_ge(c_in[k % 2], 16 * loads)
                act.activation(c_hl[:, 0, k, :], c_raw[:, k % 2, :], ACT.Copy).then_inc(c_high, 1)

            for k in range(KC):
                c_high_part(k // 2 + 1, k)
            w_high_part(1, 0)
            w_high_part(1, 1)
            with act.Fori(0, NBLK) as t:
                def square(i, j):
                    half = "kq".index(ORDER[i][0])
                    n = 4 * ORDER[i][1] + j
                    bias = (k_b, q_b)[half][:, n:n + 1]
                    act.wait_ge(proj_ready, NP * t + 4 * i + j + 1)
                    act.wait_ge(sq_added, 2 * NSQ * t + half * NSQ + 1 + square_slot_free(n))
                    if half == 0 and n < 2:
                        act.wait_ge(x_out[2 + n], 16 * t + 16)
                    act.activation(sq[:, n % 2, :], proj[:, j, :], ACT.Square, bias=bias)\
                        .then_inc(proj_squared, 1)

                def h_high_part(j):
                    act.wait_ge(h_turned, TPB * t + j + 1)
                    act.activation(a_hl[:, 0, :, j * P:(j + 1) * P],
                                   tr_ps[:, j % 2, :].rearrange("p (k n) -> p k n", k=KC), ACT.Copy)\
                        .then_inc(h_high, 1)

                def attention():
                    for u in range(NU + AV_LAG):
                        if TURN_LAG <= u < NU + TURN_LAG:
                            m = u - TURN_LAG
                            act.wait_ge(pt_ready, NU * t + m + 1)
                            act.activation(probs[:, m % 4], tr_ps[:, m % 2, :].rearrange("p (h n) -> p h n", h=4),
                                           ACT.Copy).then_inc(pt_copied, 1)
                        if u < NU:
                            b = u % TPB
                            if u == 0:
                                act.wait_ge(ss_pow, 2 * t + 2)
                            act.wait_ge(s_sub, NU * t + u + 1)
                            act.activation(probs[:, u % 4], probs[:, u % 4], ACT.Exp, scale=rq[:, b:b + 1])\
                                .then_inc(e_ready, 1)
                            if u % 4 == 2:
                                act.wait_ge(proj_ready, NP * t + NP)
                                c_high_part(KC // 2 * t + KC // 2 + u // 8 + 1, u // 4)
                        if AV_LAG <= u:
                            m = u - AV_LAG
                            g, b = m // TPB, m % TPB
                            act.wait_ge(av_ready, NU * t + m + 1)
                            act.activation(qT[:, 4 * g:4 * g + 4, b * P:(b + 1) * P],
                                           proj[:, m % 2, :].rearrange("p (h n) -> p h n", h=4), ACT.Copy)\
                                .then_inc(av_copied, 1)

                def a_high_part(n):
                    if n == 0:
                        act.wait_ge(av_copied, NU * t + NU)
                    if n >= 4:
                        act.wait_ge(a_used, NA * t + n - 3)
                    act.activation(a_hl[:, 0, n % 4, :], qT[:, n, :], ACT.Identity, bias=v_b[:, n:n + 1])\
                        .then_inc(a_high, 1)

                for i in range(NW):
                    if i < O0 and ORDER[i][0] in "kq":
                        for j in range(4):
                            square(i, j)
                    if i == O0:
                        for n in range(4):
                            a_high_part(n)
                    if O0 <= i < NW - 1:
                        for n in range(4 * (i - O0) + 4, 4 * (i - O0) + 7):
                            a_high_part(n)
                    if i < O0:
                        act.wait_ge(proj_ready, NP * t + 4 * i + 4)
                    elif i < NW - 1:
                        act.wait_ge(a_used, NA * t + 4 * (i - O0) + 4)
                    else:
                        act.wait_ge(o_ready, TPB * t + TPB)
                    w_high_part(NW // 2 * t + (i + 2) // 2 + 1, i % 2)
                    if O0 <= i < NW - 1:
                        a_high_part(4 * (i - O0) + 7)
                    if i < TPB:
                        h_high_part(i)
                    if i == O0 - 1:
                        attention()

        @block.tensor
        def _(pe):
            pe.wait_ge(const_made, 3)
            with pe.Fori(0, NBLK) as t:
                def project(i):
                    pe.wait_ge(w_split, NW * t + i + 3)
                    w = w_hl[:, i % 2]
                    kind = ORDER[i][0]
                    a = a_hl if kind == "q" else c_hl
                    if i == 0:
                        pe.wait_ge(c_split, KC * t + KC + 2)
                    if i == AT["q", 0]:
                        pe.wait_ge(h_split, TPB * t + TPB)
                    for j in range(4):
                        if i == 0:
                            pe.wait_ge(o_scaled, TPB * t + j + 1)
                        else:
                            pe.wait_ge(proj_copied, NP * t + 4 * (i - 1) + j + 1)
                        for k in range(KC):
                            for n, (wp, ap) in enumerate(PASSES):
                                tok, col = (a[:, ap, k], w[:, wp, k])
                                own = slice(j * P, (j + 1) * P)
                                left, right = (tok[:, own], col) if kind == "v" else (col[:, own], tok)
                                mm = pe.matmul(proj[:, j, :], left, right, start=(k == 0 and n == 0),
                                               stop=(k == KC - 1 and n == 2))
                        mm.then_inc(proj_ready, 1)

                def turn_h(j):
                    pe.wait_ge(ln_done, TPB * t + j + 1)
                    if j >= 2:
                        pe.wait_ge(h_split, TPB * t + j - 1)
                    for k in range(KC):
                        mm = pe.transpose(tr_ps[:, j % 2, k * P:(k + 1) * P], xr[:, j % 2, k * P:(k + 1) * P],
                                          ident[:])
                    mm.then_inc(h_turned, 1)

                def sum_squares(half):
                    pe.wait_ge(sq_added, 2 * NSQ * t + (half + 1) * NSQ + 1)
                    if half == 1:
                        pe.wait_ge(ss_eps, 2 * t + 1)
                    for b in range(TPB):
                        mm = pe.matmul(sc_ps[:, 0, b:b + 1], ssum[:, b * P:(b + 1) * P], ones[:, 0:1],
                                       start=True, stop=True)
                    mm.then_inc(ss_ready, 1)

                def spread_rk():
                    pe.wait_ge(rk_spread, t + 1)
                    for b in range(TPB):
                        mm = pe.matmul(sc_ps[:, 1, b * P:(b + 1) * P], ones[:], rk_diag[:, b, :],
                                       start=True, stop=True)
                    mm.then_inc(rk_ready, 1)

                def scores(u):
                    g, b = u // TPB, u % TPB
                    own = slice(b * P, (b + 1) * P)
                    if u == 0:
                        pe.wait_ge(k_normed, H * t + H)
                        pe.wait_ge(proj_copied, NP * t + 4 * AT["q", G - 1] + 4)
                        pe.wait_ge(ss_eps, 2 * t + 2)
                    if u >= 2:
                        pe.wait_ge(s_sub, NU * t + u - 1)
                    for y in range(4):
                        mm = pe.matmul(sc_ps[:, u % 2, y * P:(y + 1) * P], qT[:, 4 * g + y, own],
                                       kT[:, 4 * g + y, own], start=True, stop=True)
                    mm.then_inc(s_ready, 1)

                def turn_probs(u):
                    pe.wait_ge(p_ready, NU * t + u + 1)
                    if u >= 2:
                        pe.wait_ge(pt_copied, NU * t + u - 1)
                    for y in range(4):
                        mm = pe.transpose(tr_ps[:, u % 2, y * P:(y + 1) * P], probs[:, u % 4, y, :], ident[:])
                    mm.then_inc(pt_ready, 1)

                def weigh_values(u):
                    g, b = u // TPB, u % TPB
                    pe.wait_ge(pt_copied, NU * t + u + 1)
                    if u < 2:
                        pe.wait_ge(proj_copied, NP * t + NP)
                    else:
                        pe.wait_ge(av_copied, NU * t + u - 1)
                    for y in range(4):
                        h = 4 * g + y
                        mm = pe.matmul(proj[:, u % 2, y * P:(y + 1) * P], v[:, b, h * P:(h + 1) * P],
                                       probs[:, u % 4, y, :], start=True, stop=True)
                    mm.then_inc(av_ready, 1)

                def project_out(i):
                    pe.wait_ge(w_split, NW * t + i + 3)
                    for k in range(4):
                        n = 4 * (i - O0) + k
                        pe.wait_ge(a_split, 4 * G * t + n + 1)
                        if n == 0:
                            pe.wait_ge(av_copied, NU * t + NU)
                        for j in range(TPB):
                            for m, (wp, ap) in enumerate(PASSES):
                                mm = pe.matmul(proj[:, j, :], a_hl[:, ap, k, j * P:(j + 1) * P],
                                               w_hl[:, i % 2, wp, k], start=(n == 0 and m == 0),
                                               stop=(n == 4 * G - 1 and m == 2))
                            if n == 4 * G - 1 and j < TPB - 1:
                                mm.then_inc(o_ready, 1)
                        if n < 4 * G - 1:
                            mm.then_inc(a_used, 1)
                        else:
                            mm.then_inc(o_ready, 1)

                for i in range(O0):
                    project(i)
                    if i < TPB:
                        turn_h(i)
                    if i == AT["v", 0]:
                        sum_squares(0)
                    if i == AT["q", 0]:
                        spread_rk()
                    if i == AT["v", 1]:
                        sum_squares(1)
                for u in range(NU + AV_LAG):
                    if u < NU:
                        scores(u)
                    if TURN_LAG <= u < NU + TURN_LAG:
                        turn_probs(u - TURN_LAG)
                    if u >= AV_LAG:
                        weigh_values(u - AV_LAG)
                for i in range(O0, NW):
                    project_out(i)

        @block.vector
        def _(dve):
            dve.sem_inc(o_scaled, TPB)
            dve.wait_ge(const_made, 3)
            dve.wait_ge(const_in, 16 * 3)
            dve.tensor_tensor(nqk[:], nq, nk, ALU.mult).then_inc(const_done, 1)
            dve.wait_ge(tg_ready, 1)
            dve.tensor_scalar(tg_ob[:], tg_ob[:], tg[:], None, ALU.mult).then_inc(const_done, 1)
            dve.wait_ge(const_done, 2)
            with dve.Fori(0, NBLK) as t:
                def normalise_x(j):
                    s = j % 2
                    n = TPB * t + j + 1
                    dve.wait_ge(x_in[s], 16 * (TPB // 2 * t + j // 2 + 1))
                    dve.bn_stats(stats[:, s, :], xr[:, s, :]).then_inc(ln_stats, 1)
                    dve.wait_ge(ln_stats, n)
                    dve.sem_inc(ln_seen, 1)
                    dve.bn_aggr(mv[:, s, :], stats[:, s, :]).then_inc(ln_mv, 1)
                    dve.wait_ge(ln_mv, n)
                    dve.tensor_scalar(rstd[:, s, :], mv[:, s, 1:2], LN_EPS, None, ALU.add).then_inc(ln_eps, 1)
                    dve.wait_ge(ln_rstd, n)
                    dve.tensor_scalar(xr[:, s, :], xr[:, s, :], mv[:, s, 0:1], rstd[:, s, :],
                                      ALU.subtract, ALU.mult).then_inc(ln_done, 1)

                def h_low_part(j):
                    own = slice(j * P, (j + 1) * P)
                    dve.wait_ge(h_high, TPB * t + j + 1)
                    dve.tensor_tensor(a_hl[:, 1, :, own], tr_ps[:, j % 2, :].rearrange("p (k n) -> p k n", k=KC),
                                      f32(a_hl[:, 0, :, own]), ALU.subtract).then_inc(h_split, 1)

                def take(i, j):
                    kind, g = ORDER[i]
                    n = 4 * g + j
                    if kind == "v":
                        dve.wait_ge(proj_ready, NP * t + 4 * i + j + 1)
                    else:
                        dve.wait_ge(proj_squared, 2 * H * t + (H if kind == "q" else 0) + n + 1)
                    src = proj[:, j, :]
                    if kind == "k":
                        ins = dve.tensor_scalar(kT[:, n, :], src, k_b[:, n:n + 1], nqk[:, n:n + 1], ALU.add, ALU.mult)
                    elif kind == "v":
                        ins = dve.tensor_copy(v[:, j, g * BLK:(g + 1) * BLK], src)
                    else:
                        ins = dve.tensor_scalar(qT[:, n, :], src, q_b[:, n:n + 1], None, ALU.add)
                    ins.then_inc(proj_copied, 1)

                def mean_square(half, dst, src, factor):
                    dve.wait_ge(ss_ready, 2 * t + half + 2)
                    dve.tensor_scalar(dst, src, factor / INNER, factor * RMS_EPS, ALU.mult, ALU.add)\
                        .then_inc(ss_eps, 1)

                def diagonal():
                    dve.wait_ge(ss_pow, 2 * t + 1)
                    dve.tensor_tensor(rk_diag[:], ident[:].unsqueeze(1).to_broadcast([P, TPB, P]),
                                      rk[:].unsqueeze(2).to_broadcast([P, TPB, P]), ALU.mult).then_inc(rk_spread, 1)

                def normalise_k(n):
                    if n == 0:
                        dve.wait_ge(rk_ready, t + 1)
                        dve.wait_ge(proj_copied, NP * t + 4 * G)
                    dve.tensor_tensor(kT[:, n, :], kT[:, n, :], sc_ps[:, 1, :], ALU.mult).then_inc(k_normed, 1)

                def attention():
                    for u in range(NU + 1):
                        if u < NU:
                            s = sc_ps[:, u % 2, :].rearrange("p (h n) -> p h n", h=4)
                            dve.wait_ge(s_ready, NU * t + u + 1)
                            dve.tensor_reduce(mx[:, u % 4], s, AX.X, ALU.max).then_inc(s_max, 1)
                            if u >= 4:
                                dve.wait_ge(av_ready, NU * t + u - 3)
                            dve.wait_ge(s_max, NU * t + u + 1)
                            dve.tensor_tensor(probs[:, u % 4], s, mx[:, u % 4].unsqueeze(2).to_broadcast([P, 4, P]),
                                              ALU.subtract).then_inc(s_sub, 1)
                        if u >= 1:
                            m = u - 1
                            dve.wait_ge(e_ready, NU * t + m + 1)
                            dve.tensor_reduce(den[:, m % 4], probs[:, m % 4], AX.X, ALU.add).then_inc(e_sum, 1)
                            dve.wait_ge(e_sum, NU * t + m + 1)
                            dve.reciprocal(rden[:, m % 4], den[:, m % 4]).then_inc(e_rec, 1)

                def a_low_part(n):
                    dve.wait_ge(a_high, 4 * G * t + n + 1)
                    dve.scalar_tensor_tensor(a_hl[:, 1, n % 4, :], qT[:, n, :], v_b[:, n:n + 1],
                                             f32(a_hl[:, 0, n % 4, :]), ALU.add, ALU.subtract).then_inc(a_split, 1)

                for i in range(NW):
                    if i < TPB:
                        normalise_x(i)
                    if i < O0:
                        for j in range(4):
                            take(i, j)
                    if i < TPB:
                        h_low_part(i)
                    if i == AT["v", 0]:
                        mean_square(0, rk[:], sc_ps[:, 0, 0:TPB], 1.0)
                        diagonal()
                    if i < O0 and ORDER[i][0] == "q":
                        for n in range(4 * ORDER[i][1], 4 * ORDER[i][1] + 4):
                            normalise_k(n)
                    if i == AT["v", 1]:
                        mean_square(1, rq[:], sc_ps[:, 0, 0:TPB], float(P))
                    if i == O0 - 1:
                        attention()
                    if i >= O0:
                        for n in range(4 * (i - O0), 4 * (i - O0) + 4):
                            a_low_part(n)
                for j in range(TPB):
                    dve.wait_ge(o_ready, TPB * t + j + 1)
                    dve.wait_ge(r_in[j], 16 * t + 16)
                    dve.scalar_tensor_tensor(residual[j], proj[:, j, :], tg[:], residual[j], ALU.mult, ALU.add)\
                        .then_inc(o_scaled, 1)
                    dve.wait_ge(o_scaled, TPB * t + TPB + j + 1)
                    dve.tensor_tensor(residual[j], residual[j], tg_ob[:], ALU.add).then_inc(o_done, 1)


def most_groups(T, E):
    return (2 * T + E * (BLK - 1)) // BLK


def l0_experts(nc, new_sem, x1, W, x2, rows, slot_token, expert_out):
    T, D = x1.shape
    KC = D // P
    NT = T // P
    NBLK = T // BLK
    E = W["router"].shape[1]
    F = W["down"].shape[1]
    FCH = [(f, min(P, F - f)) for f in range(0, F, P)]
    NF = len(FCH)
    MAXG = most_groups(T, E)
    NPAIR = (MAXG - 1) // 2
    COLS = slot_token.shape[0] // P
    SHARED = 2 * NBLK
    SHARED_RANK = SHARED - 3
    assert MAXG == 2 * NPAIR + 1 and COLS == TPB * MAXG

    with ExitStack() as c:
        def sb(name, shape, dt=F32):
            return c.enter_context(nc.sbuf_tensor("b_" + name, shape, dt))

        def sem(name):
            return new_sem("b_" + name)

        def psum(name, shape):
            return c.enter_context(nc.psum_tensor("b_" + name, shape, F32))

        gu_ps = psum("gate_up", [P, 2, 2, BLK])
        y_ps = psum("y_sum", [P, TPB, BLK])

        h_hl = sb("h_hl", [P, 2, 2, KC, BLK], F32R)
        y = sb("y", [P, NT, D])
        gu_hl = sb("gu_hl", [P, 2, 2, KC, 2 * F], F32R)
        dn_hl = sb("dn_hl", [P, 2, 2, NF, D], F32R)
        gu_raw = sb("gu_raw", [P, 2, 2 * F])
        dn_raw = sb("dn_raw", [P, 2, D])
        hs = sb("hs", [P, TPB, D])
        yg = sb("yg", [P, TPB, D])
        silu = sb("silu", [P, 2, BLK])
        prod = sb("prod", [P, 2, BLK])
        a_hl = sb("a_hl", [P, 2, NF, BLK], F32R)
        ident = sb("ident", [P, P])
        below = sb("below", [P, P])
        ones = sb("ones", [P, P])
        mhalf = sb("mhalf", [P, 1])
        r_raw = sb("r_raw", [P, KC, E])
        r_hl = sb("r_hl", [P, 2, KC, E], F32R)
        gate = sb("gate", [P, 1])
        tg = sb("tg", [P, 1])
        stats = sb("stats", [P, 2, 6])
        mv = sb("mv", [P, 2, 2])
        rstd = sb("rstd", [P, 2, 1])
        back = sb("back", [P, 1, E])
        logit = sb("logit", [P, NT, E])
        prob = sb("prob", [P, NT, E])
        left = sb("left", [P, NT, E])
        hit = sb("hit", [P, NT, E])
        pick = sb("pick", [P, 2, NT, E])
        top = sb("top", [P, NT, 1])
        weight = sb("weight", [P, 2, NT, 1])
        taken = sb("taken", [P, E, 1])
        groups = sb("groups", [P, 1, E])
        ends = sb("ends", [P, 1, E])
        base = sb("base", [P, 1, E])
        group_no = sb("group_no", [P, MAXG, 1])
        before = sb("before", [P, MAXG, E])
        passed = sb("passed", [P, MAXG, 1])
        expert = sb("expert", [P, MAXG], I32)
        slot_f = sb("slot_f", [P, 2, NT, 1])
        slot_i = sb("slot_i", [P, 2 * NT], I32)
        slot_p = sb("slot_p", [P, 2 * NT], I32)
        slot_c = sb("slot_c", [P, 2 * NT], I32)
        place = sb("place", [P, 2 * NT], I32)
        token = sb("token", [P, NT], I32)
        token0 = sb("token0", [P, COLS], I32)
        wanted = sb("wanted", [P, COLS + TPB], I32)
        wanted_now = sb("wanted_now", [P, 2, TPB], I32)

        const_in = sem("const_in")
        const_made = sem("const_made")
        tg_ready = sem("tg_ready")
        token0_out = sem("token0_out")
        x_in = [sem(f"x_in{n}") for n in range(NBLK)]
        ln_stats = sem("ln_stats")
        ln_mv = sem("ln_mv")
        ln_eps = sem("ln_eps")
        ln_rstd = sem("ln_rstd")
        ln_done = sem("ln_done")
        rows_out = [sem(f"rows_out{j}") for j in range(TPB)]
        rows_in = [sem(f"rows_in{j}") for j in range(TPB)]
        h_turned = sem("h_turned")
        h_high = sem("h_high")
        h_split = sem("h_split")
        r_high = sem("r_high")
        r_split = sem("r_split")
        logits_ready = sem("logits_ready")
        logits_taken = sem("logits_taken")
        route = sem("route")
        exp_ready = sem("exp_ready")
        picks_ready = sem("picks_ready")
        rank_ready = sem("rank_ready")
        rank_taken = sem("rank_taken")
        places_ready = sem("places_ready")
        experts_ready = sem("experts_ready")
        tokens_out = sem("tokens_out")
        wanted_in = sem("wanted_in")
        wanted_ready = sem("wanted_ready")
        gather_free = sem("gather_free")
        gu_in = [sem(f"gu_in{s}") for s in range(2)]
        gu_high = sem("gu_high")
        gu_split = sem("gu_split")
        dn_in = [sem(f"dn_in{s}") for s in range(2)]
        dn_high = sem("dn_high")
        dn_split = sem("dn_split")
        gu_ready = sem("gu_ready")
        silu_ready = sem("silu_ready")
        prod_ready = sem("prod_ready")
        a_high = sem("a_high")
        a_split = sem("a_split")
        y_ready = sem("y_ready")
        y_taken = sem("y_taken")
        yg_out = sem("yg_out")
        got = [sem(f"got{j}") for j in range(TPB)]
        routed_added = sem("routed_added")
        x_out = sem("x_out")

        x1_t = x1.rearrange("(b n p) d -> b p n d", p=P, n=TPB)
        x2_t = x2.rearrange("(b n p) d -> b p n d", p=P, n=TPB)
        gu_t = W["gate_up"].rearrange("e (k p) f -> k e p f", p=P)
        slot_token_t = slot_token.rearrange("(p c) o -> p (c o)", p=P)
        expert_out_t = expert_out.rearrange("(p g j) d -> g p (j d)", p=P, j=TPB)

        block = c.enter_context(nc.Block())


        @block.sync
        def _(sp):
            def load_weights(m, e, s):
                for k in range(KC):
                    sp.wait_ge(gu_split, KC * m + k + 1)
                    sp.dma_start(gu_raw[:, k % 2, :], gu_t[k][e]).then_inc(gu_in[k % 2], 16)
                    if k < NF:
                        start, width = FCH[k]
                        slot = (NF * s + k) % 2
                        sp.wait_ge(dn_split, NF * m + k + 1)
                        sp.dma_start(dn_raw[0:width, slot, :], W["down"][e, start:start + width, :])\
                            .then_inc(dn_in[slot], 16)

            for b in range(NBLK):
                sp.dma_start(y[:, b * TPB:(b + 1) * TPB, :], x1_t[b]).then_inc(x_in[b], 16)
                if b == 0:
                    sp.dma_start(gate[:], W["gate"].to_broadcast([P, 1])).then_inc(const_in, 16)
                    sp.dma_start(r_raw[:], W["router"].rearrange("(k p) e -> p k e", p=P)).then_inc(const_in, 16)
                    sp.sem_inc(gu_split, 2)
                    sp.sem_inc(dn_split, 2)
                    load_weights(0, E, 0)
            sp.wait_ge(const_made, 7)
            sp.dma_start(slot_token_t, token0[:]).then_inc(token0_out, 16)
            for n in range(NT):
                if n == TPB:
                    load_weights(1, E + 1, 1)
                sp.wait_ge(ln_done, n + 1)
                sp.dma_start(rows[n * P:(n + 1) * P, :], hs[:, n % TPB, :]).then_inc(rows_out[n % TPB], 16)
            sp.wait_ge(experts_ready, 1)

            def load_group_weights(g, s):
                e = sp.value_load(expert[0:1, bass.ds(g, 1)], min_val=0, max_val=E - 1)
                for k in range(KC):
                    sp.wait_ge(gu_split, KC * (g + 2) + k + 1)
                    sp.dma_start(gu_raw[:, k % 2, :], gu_t[k][bass.ds(e, 1)].rearrange("a p f -> (a p) f"))\
                        .then_inc(gu_in[k % 2], 16)
                    if k < NF:
                        start, width = FCH[k]
                        slot = (NF * s + k) % 2
                        sp.wait_ge(dn_split, NF * (g + 2) + k + 1)
                        sp.dma_start(dn_raw[0:width, slot, :],
                                     W["down"][bass.ds(e, 1), start:start + width, :].rearrange("a p f -> (a p) f"))\
                            .then_inc(dn_in[slot], 16)

            sp.wait_ge(tokens_out, 2 * NT * 16)
            sp.dma_start(wanted[:, 0:COLS], slot_token_t).then_inc(wanted_in, 16)
            load_group_weights(0, 0)
            with sp.Fori(0, NPAIR) as t:
                load_group_weights(2 * t + 1, 1)
                load_group_weights(2 * t + 2, 0)
            for b in range(NBLK):
                sp.wait_ge(routed_added, 2 * TPB * (b + 1))
                sp.dma_start(x2_t[b], y[:, b * TPB:(b + 1) * TPB, :]).then_inc(x_out, 16)
            for j in range(TPB):
                sp.wait_ge(rows_out[j], 16 * NBLK)
            sp.wait_ge(x_out, 16 * NBLK)

        @block.gpsimd
        def _(pool):
            pool.memset(ones[:], 1.0).then_inc(const_made, 1)
            pool.memset(mhalf[:], -0.5).then_inc(const_made, 1)
            pool.memset(token0[:], 0).then_inc(const_made, 1)
            pool.memset(wanted[:, COLS:COLS + TPB], 0).then_inc(const_made, 1)
            pool.iota(back[:, 0, :], pattern=[[1, E]], base=-E, channel_multiplier=0,
                      allow_small_or_imprecise_dtypes=True).then_inc(const_made, 1)
            pool.iota(group_no[:, :, 0], pattern=[[1, MAXG]], base=0, channel_multiplier=0,
                      allow_small_or_imprecise_dtypes=True).then_inc(const_made, 1)
            pool.iota(token[:], pattern=[[P, NT]], base=0, channel_multiplier=1).then_inc(const_made, 1)
            pool.wait_ge(const_made, 7)
            pool.affine_select(out=ident[:], in_=ones[:], compare_op=ALU.is_equal, fill=0.0, base=0,
                               pattern=[[-1, P]], channel_multiplier=1).then_inc(const_made, 1)
            pool.affine_select(out=below[:], in_=ones[:], compare_op=ALU.is_ge, fill=0.0, base=-1,
                               pattern=[[1, P]], channel_multiplier=-1).then_inc(const_made, 1)

            def power(n):
                pool.wait_ge(ln_eps, n + 1)
                pool.tensor_tensor(rstd[:, n % 2, :], rstd[:, n % 2, :], mhalf[:], ALU.pow).then_inc(ln_rstd, 1)

            def powers(b):
                for j in range(TPB):
                    power(TPB * b + j)

            def low_parts(m, s, chunks):
                for k in chunks:
                    pool.wait_ge(gu_high, KC * m + k + 1)
                    pool.tensor_tensor(gu_hl[:, s, 1, k, :], gu_raw[:, k % 2, :], f32(gu_hl[:, s, 0, k, :]),
                                       ALU.subtract).then_inc(gu_split, 1)
                    if k < NF:
                        w = FCH[k][1]
                        pool.wait_ge(dn_high, NF * m + k + 1)
                        pool.tensor_tensor(dn_hl[0:w, s, 1, k, :], dn_raw[0:w, (NF * s + k) % 2, :],
                                           f32(dn_hl[0:w, s, 0, k, :]), ALU.subtract).then_inc(dn_split, 1)

            def a_low(step, par, f):
                w = FCH[f][1]
                pool.wait_ge(a_high, NF * step + f + 1)
                pool.tensor_tensor(a_hl[0:w, 1, f, :], prod[0:w, (NF * par + f) % 2, :], f32(a_hl[0:w, 0, f, :]),
                                   ALU.subtract).then_inc(a_split, 1)

            def gather_rows(g, s):
                if isinstance(g, int) and g == 0:
                    pool.wait_ge(wanted_in, 16)
                    for j in range(TPB):
                        pool.wait_ge(rows_out[j], 16 * NBLK)
                pool.wait_ge(h_turned, TPB * (g + NBLK))
                pool.sem_inc(gather_free, 1)
                pool.tensor_copy(wanted_now[:, s, :], wanted[:, bass.ds(TPB * g, TPB)]).then_inc(wanted_ready, 1)
                pool.wait_ge(wanted_ready, g + 1)
                pool.sem_inc(gather_free, 1)
                for j in range(TPB):
                    pool.indirect_dma_start(hs[:, j, :], None, rows,
                                            bass.IndirectOffsetOnAxis(ap=wanted_now[:, s, j:j + 1], axis=0))\
                        .then_inc(rows_in[j], 16)

            pool.sem_inc(a_split, 2)
            pool.sem_inc(prod_ready, 2)
            powers(0)
            low_parts(0, 0, range(KC))
            powers(1)
            low_parts(1, 1, range(KC))
            for step in range(SHARED - 1):
                for f in range(NF):
                    a_low(step, step % 2, f)
                    if f == 0 and step in (1, 3):
                        powers(step // 2 + 2)
                    if step == 5 and f == 0:
                        pool.wait_ge(token0_out, 16)
                        pool.wait_ge(places_ready, 1)
                    if (step, f) in ((5, 0), (5, 1), (5, 2), (6, 0), (6, 1), (6, 2)):
                        part = NF * (step - 5) + f
                        each = -(-2 * NT // (2 * NF))
                        for n in range(part * each, min(2 * NT, (part + 1) * each)):
                            pool.indirect_dma_start(slot_token, bass.IndirectOffsetOnAxis(ap=place[:, n:n + 1], axis=0),
                                                    token[:, n % NT:n % NT + 1], None).then_inc(tokens_out, 16)
            gather_rows(0, 0)

            def group_step(step, par, g, s):
                a_low(step, par, 0)
                low_parts(g + 2, s, range(2))
                a_low(step, par, 1)
                gather_rows(g + 1, 1 - s)
                low_parts(g + 2, s, range(2, KC - 1))
                a_low(step, par, 2)
                low_parts(g + 2, s, range(KC - 1, KC))

            group_step(SHARED - 1, 1, 0, 0)
            with pool.Fori(0, NPAIR) as t:
                for i in range(2):
                    group_step(SHARED + 2 * t + i, i, 2 * t + i + 1, 1 - i)
            for f in range(NF):
                a_low(SHARED + MAXG - 1, 0, f)

            pool.wait_ge(yg_out, 16 * MAXG + 16)
            for j in range(TPB):
                pool.wait_ge(rows_in[j], 16 * (MAXG + 1))
            for n in range(NT):
                for r in range(2):
                    q = 2 * n + r
                    if q >= TPB:
                        pool.wait_ge(routed_added, q - TPB + 1)
                    pool.indirect_dma_start(hs[:, q % TPB, :], None, expert_out,
                                            bass.IndirectOffsetOnAxis(ap=place[:, r * NT + n:r * NT + n + 1], axis=0))\
                        .then_inc(got[q % TPB], 16)

        @block.scalar
        def _(act):
            act.wait_ge(const_in, 32)
            act.activation(tg[:], gate[:], ACT.Tanh).then_inc(tg_ready, 1)
            act.activation(r_hl[:, 0], r_raw[:], ACT.Copy).then_inc(r_high, 1)

            def high_parts(m, half_m, s, chunks):
                for k in chunks:
                    act.wait_ge(gu_in[k % 2], 16 * (KC // 2 * m + k // 2 + 1))
                    act.activation(gu_hl[:, s, 0, k, :], gu_raw[:, k % 2, :], ACT.Copy).then_inc(gu_high, 1)
                    if k < NF:
                        w = FCH[k][1]
                        act.wait_ge(dn_in[(NF * s + k) % 2], 16 * (NF * half_m + (NF * s + k) // 2 + 1))
                        act.activation(dn_hl[0:w, s, 0, k, :], dn_raw[0:w, (NF * s + k) % 2, :], ACT.Copy)\
                            .then_inc(dn_high, 1)

            def h_high_parts(u, s):
                for j in range(TPB):
                    act.wait_ge(h_turned, TPB * u + j + 1)
                    act.activation(h_hl[:, s, 0, :, j * P:(j + 1) * P],
                                   y_ps[:, j, :].rearrange("p (k n) -> p k n", k=KC), ACT.Copy).then_inc(h_high, 1)

            def gate_part(step, par, f):
                w = FCH[f][1]
                n = (NF * par + f) % 2
                act.wait_ge(gu_ready, NF * step + f + 1)
                act.wait_ge(prod_ready, NF * step + f - 1 + 2)
                act.activation(silu[0:w, n, :], gu_ps[0:w, n, 0, :], ACT.Silu).then_inc(silu_ready, 1)

            def a_high_part(step, par, f):
                w = FCH[f][1]
                act.wait_ge(prod_ready, NF * step + f + 1 + 2)
                act.activation(a_hl[0:w, 0, f, :], prod[0:w, (NF * par + f) % 2, :], ACT.Copy).then_inc(a_high, 1)

            def chunk(step, par, f):
                gate_part(step, par, f)
                a_high_part(step, par, f)

            h_high_parts(0, 0)
            high_parts(0, 0, 0, range(KC))
            high_parts(1, 0, 1, range(2))
            for step in range(SHARED - 1):
                for f in range(NF):
                    chunk(step, step % 2, f)
                    if step == 0 and f == 1:
                        high_parts(1, 0, 1, range(2, KC))
                    if f == 0 and step % 2 == 0 and step // 2 + 1 < NBLK:
                        h_high_parts(step // 2 + 1, (step // 2 + 1) % 2)
                    if f == 1 and step == 2 * (NBLK - 2):
                        act.wait_ge(route, 2)
                        act.activation(left[:], left[:], ACT.Exp).then_inc(exp_ready, 1)

            def store_group(g):
                act.wait_ge(y_taken, TPB * (SHARED + g + 1))
                act.dma_start(expert_out_t[g] if isinstance(g, int) else
                              expert_out_t[bass.ds(g, 1)].rearrange("a p f -> (a p) f"),
                              yg[:].rearrange("p j d -> p (j d)")).then_inc(yg_out, 16)

            def group_step(step, par, g, half_m, s):
                chunk(step, par, 0)
                act.wait_ge(y_ready, TPB * step)
                high_parts(g + 2, half_m, s, range(2))
                h_high_parts(g + NBLK, s)
                chunk(step, par, 1)
                high_parts(g + 2, half_m, s, range(2, KC - 1))
                chunk(step, par, 2)
                high_parts(g + 2, half_m, s, range(KC - 1, KC))

            group_step(SHARED - 1, 1, 0, 1, 0)
            with act.Fori(0, NPAIR) as t:
                for i in range(2):
                    group_step(SHARED + 2 * t + i, i, 2 * t + i + 1, t + 1 + i, 1 - i)
                    store_group(2 * t + i)
            for f in range(NF):
                chunk(SHARED + MAXG - 1, 0, f)
            store_group(MAXG - 1)

        @block.tensor
        def _(pe):
            pe.wait_ge(const_made, 9)

            def turn(u, ready):
                for j in range(TPB):
                    ready(j)
                    for k in range(KC):
                        mm = pe.transpose(y_ps[:, j, k * P:(k + 1) * P], hs[:, j, k * P:(k + 1) * P], ident[:])
                    mm.then_inc(h_turned, 1)

            def turn_block(b, step):
                def ready(j):
                    pe.wait_ge(ln_done, TPB * b + j + 1)
                    if step:
                        pe.wait_ge(y_taken, TPB * (step - 1) + j + 1)
                    elif b:
                        pe.wait_ge(logits_taken, 1)
                turn(b, ready)

            def turn_group(g, step):
                def ready(j):
                    pe.wait_ge(rows_in[j], 16 * (g + 1))
                    pe.wait_ge(y_taken, TPB * (step - 1) + j + 1)
                turn(NBLK + g, ready)

            def logits(b):
                pe.wait_ge(h_split, TPB * (b + 1))
                for j in range(TPB):
                    for k in range(KC):
                        for m, (wp, ap) in enumerate(PASSES):
                            mm = pe.matmul(y_ps[:, 0, j * E:(j + 1) * E], h_hl[:, b % 2, ap, k, j * P:(j + 1) * P],
                                           r_hl[:, wp, k, :], start=(k == 0 and m == 0), stop=(k == KC - 1 and m == 2))
                mm.then_inc(logits_ready, 1)

            def gate_up(step, par, s, hslot, f):
                start, w = FCH[f]
                n = (NF * par + f) % 2
                pe.wait_ge(prod_ready, NF * step + f - 1 + 2)
                for part in range(2):
                    cols = slice(part * F + start, part * F + start + w)
                    for k in range(KC):
                        for m, (wp, ap) in enumerate(PASSES):
                            mm = pe.matmul(gu_ps[0:w, n, part, :], gu_hl[:, s, wp, k, cols], h_hl[:, hslot, ap, k, :],
                                           start=(k == 0 and m == 0), stop=(k == KC - 1 and m == 2))
                mm.then_inc(gu_ready, 1)

            def down(step, s, f, freed):
                w = FCH[f][1]
                pe.wait_ge(a_split, NF * step + f + 1 + 2)
                for j in range(TPB):
                    if f == 0:
                        freed(j)
                    for m, (wp, ap) in enumerate(PASSES):
                        mm = pe.matmul(y_ps[:, j, :], a_hl[0:w, ap, f, j * P:(j + 1) * P], dn_hl[0:w, s, wp, f, :],
                                       start=(f == 0 and m == 0), stop=(f == NF - 1 and m == 2))
                    if f == NF - 1:
                        mm.then_inc(y_ready, 1)

            def ranks():
                pe.wait_ge(picks_ready, 2)
                pe.wait_ge(y_taken, TPB * SHARED_RANK)
                both = hit[:].rearrange("p n e -> p (n e)")
                pe.matmul(y_ps[:, 0, 0:NT * E], below[:], both, start=True, stop=False)
                for n in range(1, NT):
                    pe.matmul(y_ps[:, 0, n * E:NT * E], ones[:], both[:, 0:(NT - n) * E], start=False,
                              stop=(n == NT - 1))
                pe.matmul(y_ps[:, 1, 0:E], ones[:], taken[:, :, 0], start=True, stop=True).then_inc(rank_ready, 1)

            pe.wait_ge(r_split, 1)
            turn_block(0, 0)
            logits(0)
            for step in range(SHARED):
                b, s = step // 2, step % 2
                if b == 0:
                    pe.wait_ge(gu_split, KC * (s + 1) + 2)
                gate_up(step, s, s, b % 2, 0)
                ahead = s == 0 and b + 1 < NBLK
                if ahead:
                    if step == 0:
                        pe.wait_ge(logits_taken, 1)
                    turn_block(b + 1, step)
                if step == SHARED_RANK:
                    ranks()
                if step == SHARED - 1:
                    turn_group(0, step)
                gate_up(step, s, s, b % 2, 1)
                if ahead:
                    logits(b + 1)
                gate_up(step, s, s, b % 2, 2)
                if b == 0:
                    pe.wait_ge(dn_split, NF * (s + 1) + 2)

                def freed(j):
                    if ahead:
                        pe.wait_ge(h_split, TPB * (b + 1) + j + 1)
                        pe.wait_ge(logits_taken, b + 2)
                    elif step == SHARED_RANK:
                        pe.wait_ge(rank_taken, 1)
                    elif step == SHARED - 1:
                        pe.wait_ge(h_split, TPB * NBLK + j + 1)
                    if not ahead and step:
                        pe.wait_ge(y_taken, TPB * (step - 1) + j + 1)

                for f in range(NF):
                    down(step, s, f, freed)

            def group(g, s):
                step = SHARED + g
                last = isinstance(g, int)
                pe.wait_ge(gu_split, KC * (g + 3) + 2)
                pe.wait_ge(h_split, TPB * (NBLK + g + 1))
                gate_up(step, s, s, s, 0)
                if not last:
                    turn_group(g + 1, step)
                gate_up(step, s, s, s, 1)
                gate_up(step, s, s, s, 2)
                pe.wait_ge(dn_split, NF * (g + 3) + 2)

                def freed(j):
                    if last:
                        pe.wait_ge(y_taken, TPB * (step - 1) + j + 1)
                    else:
                        pe.wait_ge(h_split, TPB * (NBLK + g + 1) + j + 1)

                for f in range(NF):
                    down(step, s, f, freed)

            with pe.Fori(0, NPAIR) as t:
                for i in range(2):
                    group(2 * t + i, i)
            group(MAXG - 1, 0)

        @block.vector
        def _(dve):
            def statistics(n):
                s = n % 2
                dve.wait_ge(x_in[n // TPB], 16)
                dve.bn_stats(stats[:, s, :], y[:, n, :]).then_inc(ln_stats, 1)
                dve.wait_ge(ln_stats, n + 1)
                dve.bn_aggr(mv[:, s, :], stats[:, s, :]).then_inc(ln_mv, 1)
                dve.wait_ge(ln_mv, n + 1)
                dve.tensor_scalar(rstd[:, s, :], mv[:, s, 1:2], LN_EPS, None, ALU.add).then_inc(ln_eps, 1)

            def normalise(n):
                s = n % 2
                dve.wait_ge(ln_rstd, n + 1)
                if n >= TPB:
                    dve.wait_ge(h_turned, n - TPB + 1)
                    dve.wait_ge(rows_out[n % TPB], 16 * (n // TPB))
                dve.tensor_scalar(hs[:, n % TPB, :], y[:, n, :], mv[:, s, 0:1], rstd[:, s, :], ALU.subtract, ALU.mult)\
                    .then_inc(ln_done, 1)

            def layer_norm(b):
                for j in range(TPB + 1):
                    if j < TPB:
                        statistics(TPB * b + j)
                    if j >= 1:
                        normalise(TPB * b + j - 1)

            def h_low_parts(u, s):
                for j in range(TPB):
                    dve.wait_ge(h_high, TPB * u + j + 1)
                    dve.tensor_tensor(h_hl[:, s, 1, :, j * P:(j + 1) * P],
                                      y_ps[:, j, :].rearrange("p (k n) -> p k n", k=KC),
                                      f32(h_hl[:, s, 0, :, j * P:(j + 1) * P]), ALU.subtract).then_inc(h_split, 1)

            def take_logits(b):
                dve.wait_ge(logits_ready, b + 1)
                dve.tensor_copy(logit[:, b * TPB:(b + 1) * TPB, :],
                                y_ps[:, 0, 0:TPB * E].rearrange("p (n e) -> p n e", e=E)).then_inc(logits_taken, 1)

            steps = [0]

            def step_done(ins):
                steps[0] += 1
                ins.then_inc(route, 1)
                dve.wait_ge(route, steps[0])

            every = [P, NT, E]
            spread = back[:].to_broadcast(every)

            def choose():
                dve.wait_ge(logits_taken, NBLK)
                step_done(dve.tensor_reduce(top[:], logit[:], AX.X, ALU.max))
                step_done(dve.tensor_tensor(left[:], logit[:], top[:].to_broadcast(every), ALU.subtract))
                dve.wait_ge(exp_ready, 1)
                step_done(dve.tensor_reduce(top[:], left[:], AX.X, ALU.add))
                step_done(dve.reciprocal(top[:], top[:]))
                step_done(dve.tensor_tensor(prob[:], left[:], top[:].to_broadcast(every), ALU.mult))
                for r in range(2):
                    rest = (prob, left)[r]
                    step_done(dve.tensor_reduce(weight[:, r], rest[:], AX.X, ALU.max))
                    step_done(dve.tensor_tensor(hit[:], rest[:], weight[:, r].to_broadcast(every), ALU.is_equal))
                    step_done(dve.tensor_tensor(hit[:], hit[:], spread, ALU.mult))
                    step_done(dve.tensor_reduce(top[:], hit[:], AX.X, ALU.min))
                    step_done(dve.tensor_tensor(pick[:, r], spread, top[:].to_broadcast(every), ALU.is_equal))
                    if r == 0:
                        step_done(dve.scalar_tensor_tensor(left[:], pick[:, 0], -2.0, prob[:], ALU.mult, ALU.add))
                dve.tensor_tensor(hit[:], pick[:, 0], pick[:, 1], ALU.add).then_inc(picks_ready, 1)
                dve.wait_ge(picks_ready, 1)
                dve.tensor_reduce(taken[:], hit[:].rearrange("p n e -> p e n"), AX.X, ALU.add).then_inc(picks_ready, 1)
                dve.wait_ge(tg_ready, 1)
                step_done(dve.tensor_scalar(weight[:], weight[:], tg[:], None, ALU.mult))

            def assign():
                dve.wait_ge(rank_ready, 1)
                count = y_ps[:, 1:2, 0:E]
                step_done(dve.tensor_scalar(groups[:], count, 0.0, None, ALU.is_gt))
                for k in range(1, NBLK):
                    step_done(dve.scalar_tensor_tensor(groups[:], count, float(BLK * k), groups[:], ALU.is_gt, ALU.add))
                step_done(dve.tensor_copy(ends[:], groups[:]))
                for e in range(1, E):
                    step_done(dve.tensor_tensor(ends[:, :, e:e + 1], ends[:, :, e:e + 1], ends[:, :, e - 1:e], ALU.add))
                step_done(dve.tensor_tensor(base[:], ends[:], groups[:], ALU.subtract))
                step_done(dve.tensor_scalar(base[:], base[:], float(BLK), None, ALU.mult))
                step_done(dve.tensor_tensor(left[:], y_ps[:, 0, 0:NT * E].rearrange("p (n e) -> p n e", e=E),
                                            base[:].to_broadcast(every), ALU.add))
                dve.sem_inc(rank_taken, 1)
                for r in range(2):
                    step_done(dve.tensor_tensor(hit[:], pick[:, r], left[:], ALU.mult))
                    step_done(dve.tensor_reduce(slot_f[:, r], hit[:], AX.X, ALU.add))
                step_done(dve.tensor_copy(slot_i[:], slot_f[:].rearrange("p r n o -> p (r n o)")))
                step_done(dve.tensor_scalar(slot_p[:], slot_i[:], P - 1, None, ALU.bitwise_and))
                step_done(dve.tensor_scalar(slot_c[:], slot_i[:], P.bit_length() - 1, None, ALU.logical_shift_right))
                dve.scalar_tensor_tensor(place[:], slot_p[:], float(COLS), slot_c[:], ALU.mult, ALU.add).then_inc(places_ready, 1)
                lot = [P, MAXG, E]
                step_done(dve.tensor_tensor(before[:], ends[:].to_broadcast(lot), group_no[:].to_broadcast(lot),
                                            ALU.is_le))
                step_done(dve.tensor_reduce(passed[:], before[:], AX.X, ALU.add))
                dve.tensor_scalar(expert[:], passed[:, :, 0], float(E - 1), None, ALU.min).then_inc(experts_ready, 1)

            def product(step, par, f):
                w = FCH[f][1]
                n = (NF * par + f) % 2
                dve.wait_ge(silu_ready, NF * step + f + 1)
                dve.wait_ge(a_split, NF * step + f + 1)
                dve.tensor_tensor(prod[0:w, n, :], silu[0:w, n, :], gu_ps[0:w, n, 1, :], ALU.mult)\
                    .then_inc(prod_ready, 1)

            dve.wait_ge(const_made, 7)
            layer_norm(0)
            dve.wait_ge(r_high, 1)
            dve.tensor_tensor(r_hl[:, 1], r_raw[:], f32(r_hl[:, 0]), ALU.subtract).then_inc(r_split, 1)
            h_low_parts(0, 0)
            layer_norm(1)
            take_logits(0)
            dve.wait_ge(tg_ready, 1)
            for step in range(SHARED):
                b, s = step // 2, step % 2
                product(step, s, 0)
                if s == 0 and b + 1 < NBLK:
                    h_low_parts(b + 1, (b + 1) % 2)
                elif s == 1 and b + 2 < NBLK:
                    layer_norm(b + 2)
                elif step == SHARED_RANK:
                    assign()
                elif step == SHARED - 1:
                    h_low_parts(NBLK, 0)
                product(step, s, 1)
                if s == 0 and b + 1 < NBLK:
                    take_logits(b + 1)
                if step == SHARED_RANK - 1:
                    choose()
                product(step, s, 2)
                for j in range(TPB):
                    tile = TPB * b + j
                    dve.wait_ge(y_ready, TPB * step + j + 1)
                    dve.scalar_tensor_tensor(y[:, tile, :], y_ps[:, j, :], tg[:], y[:, tile, :], ALU.mult, ALU.add)\
                        .then_inc(y_taken, 1)

            def take_group(g):
                for j in range(TPB):
                    if j == 0:
                        dve.wait_ge(yg_out, 16 * g + 16)
                    dve.wait_ge(y_ready, TPB * (SHARED + g) + j + 1)
                    dve.tensor_copy(yg[:, j, :], y_ps[:, j, :]).then_inc(y_taken, 1)

            dve.sem_inc(yg_out, 16)
            with dve.Fori(0, NPAIR) as t:
                for i in range(2):
                    product(SHARED + 2 * t + i, i, 0)
                    h_low_parts(NBLK + 2 * t + i + 1, 1 - i)
                    product(SHARED + 2 * t + i, i, 1)
                    product(SHARED + 2 * t + i, i, 2)
                    take_group(2 * t + i)
            for f in range(NF):
                product(SHARED + MAXG - 1, 0, f)
            take_group(MAXG - 1)
            for n in range(NT):
                for r in range(2):
                    q = 2 * n + r
                    dve.wait_ge(got[q % TPB], 16 * (q // TPB + 1))
                    if r == 1:
                        dve.wait_ge(routed_added, q)
                    dve.scalar_tensor_tensor(y[:, n, :], hs[:, q % TPB, :], weight[:, r, n], y[:, n, :],
                                             ALU.mult, ALU.add).then_inc(routed_added, 1)


def l1_projections(nc, new_sem, x2, ctxT, W, qT, kT, v):
    T, D = x2.shape
    KC = D // P
    NBLK = T // BLK
    NO = 3 * KC
    RING = 4

    with ExitStack() as c:
        def sb(name, shape, dt=F32):
            return c.enter_context(nc.sbuf_tensor("p_" + name, shape, dt))

        def sem(name):
            return new_sem("p_" + name)

        def psum(name, shape):
            return c.enter_context(nc.psum_tensor("p_" + name, shape, F32))

        proj = psum("proj", [P, 4, BLK])
        tr_ps = psum("turned", [P, 2, BLK])
        w_raw = sb("w_raw", [P, 3, KC, D])
        w_hl = sb("w_hl", [P, 3, 2, KC, D], F32R)
        c_raw = sb("c_raw", [P, 2, BLK])
        c_hl = sb("c_hl", [P, 2, KC, BLK], F32R)
        a_hl = sb("a_hl", [P, 2, KC, BLK], F32R)
        xr = sb("xr", [P, 2, D])
        outs = sb("outs", [P, RING, BLK])
        bias = sb("bias", [P, 2, KC])
        v_b = sb("v_b", [P, D])
        ident = sb("ident", [P, P])
        ones = sb("ones", [P, P])
        mhalf = sb("mhalf", [P, 1])
        stats = sb("stats", [P, 2, 6])
        mv = sb("mv", [P, 2, 2])
        rstd = sb("rstd", [P, 2, 1])

        const_in = sem("const_in")
        const_made = sem("const_made")
        w_in = [sem(f"w_in{n}") for n in range(3)]
        w_high = sem("w_high")
        w_split = sem("w_split")
        c_in = [sem(f"c_in{s}") for s in range(2)]
        c_high = sem("c_high")
        c_split = sem("c_split")
        x_in = [sem(f"x_in{s}") for s in range(2)]
        ln_stats = sem("ln_stats")
        ln_seen = sem("ln_seen")
        ln_mv = sem("ln_mv")
        ln_eps = sem("ln_eps")
        ln_rstd = sem("ln_rstd")
        ln_done = sem("ln_done")
        h_turned = sem("h_turned")
        h_high = sem("h_high")
        h_split = sem("h_split")
        proj_ready = sem("proj_ready")
        kq_taken = sem("kq_taken")
        v_taken = sem("v_taken")
        stored = [sem(f"stored{s}") for s in range(RING)]

        x_t = x2.rearrange("(b n p) d -> n b p d", p=P, n=TPB)
        ctx_t = ctxT.rearrange("(k p) (b t) -> k b p t", p=P, t=BLK)
        k_out, q_out = (a.rearrange("(k p) (b t) -> k b p t", p=P, t=BLK) for a in (kT, qT))
        v_out = v.rearrange("(b n p) d -> n b p d", p=P, n=TPB)

        block = c.enter_context(nc.Block())

        @block.sync
        def _(sp):
            sp.dma_start(bias[:], W["kq_bias"]).then_inc(const_in, 16)
            sp.dma_start(v_b[:], W["bv"].to_broadcast([P, D])).then_inc(const_in, 16)
            sp.sem_inc(c_split, 2)
            for s in range(RING):
                sp.sem_inc(stored[s], 16)

            def load_ctx(n, b, k):
                sp.wait_ge(c_split, n + k + 1)
                sp.dma_start(c_raw[:, k % 2, :], ctx_t[k][b]).then_inc(c_in[k % 2], 16)

            load_ctx(0, 0, 0)
            load_ctx(0, 0, 1)
            for n, name in enumerate(("wk", "wv", "wq")):
                sp.dma_start(w_raw[:, n], W[name].rearrange("(k p) n -> p k n", p=P)).then_inc(w_in[n], 16)
                if n == 0:
                    load_ctx(0, 0, 2)
                    load_ctx(0, 0, 3)
            with sp.Fori(0, NBLK) as t:
                def load_x(j):
                    if j >= 2:
                        sp.wait_ge(h_turned, TPB * t + j - 1)
                    sp.dma_start(xr[:, j % 2, :], x_t[j][t]).then_inc(x_in[j % 2], 16)

                def store(i):
                    if KC <= i < 2 * KC:
                        sp.wait_ge(v_taken, KC * t + i - KC + 1)
                    else:
                        sp.wait_ge(kq_taken, KC + 2 * KC * t + (i if i < KC else i - KC) + 1)
                    dst = (k_out, v_out, q_out)[i // KC][i % KC][t]
                    sp.dma_start(dst, outs[:, i % RING, :]).then_inc(stored[i % RING], 16)

                load_x(0)
                load_x(1)
                for i in range(NO):
                    store(i)
                    if i < 2:
                        load_x(i + 2)
                    if i == 2 * KC:
                        for k in range(KC):
                            load_ctx(KC * t + KC, (t + 1) % NBLK, k)
            for s in range(RING):
                sp.wait_ge(stored[s], 16 + 16 * NBLK * (NO // RING))

        @block.gpsimd
        def _(pool):
            pool.memset(ones[:], 1.0).then_inc(const_made, 1)
            pool.memset(mhalf[:], -0.5).then_inc(const_made, 1)
            pool.wait_ge(const_made, 2)
            pool.affine_select(out=ident[:], in_=ones[:], compare_op=ALU.is_equal, fill=0.0, base=0,
                               pattern=[[-1, P]], channel_multiplier=1).then_inc(const_made, 1)

            def c_low(n, k):
                pool.wait_ge(c_high, n + k + 1)
                pool.tensor_tensor(c_hl[:, 1, k, :], c_raw[:, k % 2, :], f32(c_hl[:, 0, k, :]), ALU.subtract)\
                    .then_inc(c_split, 1)

            for k in range(KC):
                c_low(0, k)
            with pool.Fori(0, NBLK) as t:
                for j in range(TPB):
                    pool.wait_ge(ln_eps, TPB * t + j + 1)
                    pool.tensor_tensor(rstd[:, j % 2, :], rstd[:, j % 2, :], mhalf[:], ALU.pow).then_inc(ln_rstd, 1)
                for k in range(KC):
                    c_low(KC * t + KC, k)

        @block.scalar
        def _(act):
            def c_high_part(loads, k):
                act.wait_ge(c_in[k % 2], 16 * loads)
                act.activation(c_hl[:, 0, k, :], c_raw[:, k % 2, :], ACT.Copy).then_inc(c_high, 1)

            def w_high_part(n):
                act.wait_ge(w_in[n], 16)
                for k in range(KC):
                    act.activation(w_hl[:, n, 0, k, :], w_raw[:, n, k, :], ACT.Copy).then_inc(w_high, 1)

            act.sem_inc(kq_taken, KC)
            c_high_part(1, 0)
            c_high_part(1, 1)
            w_high_part(0)
            c_high_part(2, 2)
            c_high_part(2, 3)
            act.wait_ge(const_in, 32)
            w_high_part(1)
            w_high_part(2)
            with act.Fori(0, NBLK) as t:
                def take(i):
                    half = 0 if i < KC else 1
                    act.wait_ge(proj_ready, NO * t + i + 1)
                    act.wait_ge(stored[i % RING], 16 * (NO // RING * t + i // RING + 1))
                    act.activation(outs[:, i % RING, :], proj[:, i % 4, :], ACT.Identity,
                                   bias=bias[:, half, i % KC:i % KC + 1]).then_inc(kq_taken, 1)

                for i in range(KC):
                    take(i)
                    act.wait_ge(h_turned, TPB * t + i + 1)
                    act.activation(a_hl[:, 0, :, i * P:(i + 1) * P],
                                   tr_ps[:, i % 2, :].rearrange("p (k n) -> p k n", k=KC), ACT.Copy)\
                        .then_inc(h_high, 1)
                act.wait_ge(proj_ready, NO * t + 2 * KC)
                for k in range(KC):
                    take(2 * KC + k)
                    c_high_part(KC // 2 * t + KC // 2 + k // 2 + 1, k)

        @block.tensor
        def _(pe):
            pe.wait_ge(const_made, 3)
            with pe.Fori(0, NBLK) as t:
                def project(i):
                    which, j = i // KC, i % KC
                    if i % KC == 0:
                        pe.wait_ge(w_split, KC * (which + 1))
                    if i == 0:
                        pe.wait_ge(c_split, KC * t + KC + 2)
                    if i == 2 * KC:
                        pe.wait_ge(h_split, TPB * t + TPB)
                    if which == 1:
                        pe.wait_ge(kq_taken, KC + 2 * KC * t + j + 1)
                    elif which == 2:
                        pe.wait_ge(v_taken, KC * t + j + 1)
                    else:
                        pe.wait_ge(kq_taken, 2 * KC * t + j + 1)
                    a = a_hl if which == 2 else c_hl
                    own = slice(j * P, (j + 1) * P)
                    for k in range(KC):
                        for n, (wp, ap) in enumerate(PASSES):
                            tok, col = a[:, ap, k], w_hl[:, which, wp, k]
                            left, right = (tok[:, own], col) if which == 1 else (col[:, own], tok)
                            mm = pe.matmul(proj[:, j, :], left, right, start=(k == 0 and n == 0),
                                           stop=(k == KC - 1 and n == 2))
                    mm.then_inc(proj_ready, 1)

                def turn_h(j):
                    pe.wait_ge(ln_done, TPB * t + j + 1)
                    if j >= 2:
                        pe.wait_ge(h_split, TPB * t + j - 1)
                    for k in range(KC):
                        mm = pe.transpose(tr_ps[:, j % 2, k * P:(k + 1) * P], xr[:, j % 2, k * P:(k + 1) * P],
                                          ident[:])
                    mm.then_inc(h_turned, 1)

                for i in range(NO):
                    project(i)
                    if i < TPB:
                        turn_h(i)

        @block.vector
        def _(dve):
            dve.wait_ge(const_in, 32)
            for n in range(3):
                for k in range(KC):
                    dve.wait_ge(w_high, KC * n + k + 1)
                    dve.tensor_tensor(w_hl[:, n, 1, k, :], w_raw[:, n, k, :], f32(w_hl[:, n, 0, k, :]), ALU.subtract)\
                        .then_inc(w_split, 1)
            with dve.Fori(0, NBLK) as t:
                def normalise_x(j):
                    s = j % 2
                    n = TPB * t + j + 1
                    dve.wait_ge(x_in[s], 16 * (TPB // 2 * t + j // 2 + 1))
                    dve.bn_stats(stats[:, s, :], xr[:, s, :]).then_inc(ln_stats, 1)
                    dve.wait_ge(ln_stats, n)
                    dve.sem_inc(ln_seen, 1)
                    dve.bn_aggr(mv[:, s, :], stats[:, s, :]).then_inc(ln_mv, 1)
                    dve.wait_ge(ln_mv, n)
                    dve.tensor_scalar(rstd[:, s, :], mv[:, s, 1:2], LN_EPS, None, ALU.add).then_inc(ln_eps, 1)
                    dve.wait_ge(ln_rstd, n)
                    dve.tensor_scalar(xr[:, s, :], xr[:, s, :], mv[:, s, 0:1], rstd[:, s, :],
                                      ALU.subtract, ALU.mult).then_inc(ln_done, 1)

                for j in range(TPB):
                    normalise_x(j)
                    own = slice(j * P, (j + 1) * P)
                    dve.wait_ge(h_high, TPB * t + j + 1)
                    dve.tensor_tensor(a_hl[:, 1, :, own], tr_ps[:, j % 2, :].rearrange("p (k n) -> p k n", k=KC),
                                      f32(a_hl[:, 0, :, own]), ALU.subtract).then_inc(h_split, 1)
                for j in range(KC):
                    i = KC + j
                    dve.wait_ge(proj_ready, NO * t + i + 1)
                    dve.wait_ge(stored[i % RING], 16 * (NO // RING * t + i // RING + 1))
                    dve.tensor_tensor(outs[:, i % RING, :], proj[:, j, :], v_b[:], ALU.add).then_inc(v_taken, 1)


def l1_attention(nc, new_sem, qT, kT, v, aT):
    D, T = qT.shape
    HD = 32
    H = D // HD
    NBLK = T // BLK
    NQ = P // HD
    TQ = BLK // NQ
    TOK = P // H
    UN = 4
    NJ = TQ // TOK // UN
    NU = NJ * NQ
    NV = BLK // TOK
    TURN_LAG, AV_LAG = 3, 4
    BIG = 1e30

    with ExitStack() as c:
        def sb(name, shape, dt=F32):
            return c.enter_context(nc.sbuf_tensor("t_" + name, shape, dt))

        def sem(name):
            return new_sem("t_" + name)

        def psum(name, shape):
            return c.enter_context(nc.psum_tensor("t_" + name, shape, F32))

        sc_ps = psum("scores", [P, 2, UN, P])
        tr_ps = psum("turned", [P, 2, UN, P])
        av_ps = psum("out", [P, 2, UN, P])
        q_sb = sb("q", [P, H, TQ])
        q_laid = sb("q_laid", [P, 2, NJ * UN, H, TOK])
        k_sb = sb("k", [P, 2, H, TQ])
        v_sb = sb("v", [P, 2, NV, HD])
        o_sb = sb("o", [P, 2, H, TQ])
        probs = sb("probs", [P, 4, UN, P])
        mask = sb("mask", [P, H, TOK])
        diff = sb("diff", [P, TOK], mybir.dt.int32)
        same = sb("same", [P, TOK], mybir.dt.int32)
        flag = sb("flag", [P, 1, TOK])
        ident = sb("ident", [P, P])
        ones = sb("ones", [P, P])
        mx = sb("mx", [P, 4, UN])
        den = sb("den", [P, 4, UN])
        rden = sb("rden", [P, 4, UN])

        const_made = sem("const_made")
        masked = sem("masked")
        q_in = sem("q_in")
        k_in = [sem(f"k_in{s}") for s in range(2)]
        q_moved = sem("q_moved")
        v_in = [sem(f"v_in{s}") for s in range(2)]
        s_ready = sem("s_ready")
        s_masked = sem("s_masked")
        s_max = sem("s_max")
        s_sub = sem("s_sub")
        e_ready = sem("e_ready")
        e_sum = sem("e_sum")
        e_rec = sem("e_rec")
        p_ready = sem("p_ready")
        pt_ready = sem("pt_ready")
        pt_copied = sem("pt_copied")
        av_ready = sem("av_ready")
        o_copied = sem("o_copied")
        o_out = [sem(f"o_out{s}") for s in range(2)]

        def by_quadrant(a):
            return a.rearrange("(h d) (b q t) -> q b d h t", d=HD, q=NQ, t=TQ)

        q_src, k_src, a_out = by_quadrant(qT), by_quadrant(kT), by_quadrant(aT)
        v_src = v.rearrange("(b n t) (h d) -> h b t n d", t=TOK, n=NV, d=HD)
        IN_QK, IN_V = NQ * 16, H * 16

        block = c.enter_context(nc.Block())

        def load(eng, n, b, s):
            eng.wait_ge(q_moved, n + 1)
            for q in range(NQ):
                rows = slice(q * HD, (q + 1) * HD)
                eng.dma_start(q_sb[rows], q_src[q][b]).then_inc(q_in, 16)
                eng.dma_start(k_sb[rows, s], k_src[q][b]).then_inc(k_in[s], 16)
            for h in range(H):
                eng.dma_start(v_sb[h * TOK:(h + 1) * TOK, s], v_src[h][b]).then_inc(v_in[s], 16)

        @block.sync
        def _(sp):
            for s in range(2):
                sp.sem_inc(o_out[s], 16 * NQ)
            sp.sem_inc(q_moved, 1)
            load(sp, 0, 0, 0)
            with sp.Fori(0, NBLK // 2) as t:
                def store(s, blocks, b):
                    sp.wait_ge(o_copied, 2 + NJ * blocks)
                    for q in range(NQ):
                        rows = slice(q * HD, (q + 1) * HD)
                        sp.dma_start(a_out[q][b], o_sb[rows, s]).then_inc(o_out[s], 16)

                load(sp, 2 * t + 1, 2 * t + 1, 1)
                store(0, 2 * t + 1, 2 * t)
                load(sp, 2 * t + 2, (2 * t + 2) % NBLK, 0)
                store(1, 2 * t + 2, 2 * t + 1)
            for s in range(2):
                sp.wait_ge(o_out[s], 16 * NQ * (NBLK // 2 + 1))
            sp.wait_ge(q_in, IN_QK * (NBLK + 1))
            sp.wait_ge(k_in[0], IN_QK * (NBLK // 2 + 1))
            sp.wait_ge(v_in[0], IN_V * (NBLK // 2 + 1))

        @block.gpsimd
        def _(pool):
            pool.memset(ones[:], 1.0).then_inc(const_made, 1)
            pool.iota(diff[:], pattern=[[-1, TOK]], base=TOK, channel_multiplier=1).then_inc(const_made, 1)
            pool.wait_ge(const_made, 2)
            pool.affine_select(out=ident[:], in_=ones[:], compare_op=ALU.is_equal, fill=0.0, base=0,
                               pattern=[[-1, P]], channel_multiplier=1).then_inc(const_made, 1)
            with pool.Fori(0, NBLK // 2) as t:
                for u in range(2 * NU):
                    pool.wait_ge(e_rec, 2 * NU * t + u + 1)
                    pool.tensor_tensor(probs[:, u % 4], probs[:, u % 4],
                                       rden[:, u % 4].unsqueeze(2).to_broadcast([P, UN, P]), ALU.mult)\
                        .then_inc(p_ready, 1)

        @block.scalar
        def _(act):
            act.sem_inc(o_copied, 2)
            act.sem_inc(av_ready, 4)
            with act.Fori(0, NBLK // 2) as t:
                def move_queries(s):
                    act.wait_ge(q_in, IN_QK * (2 * t + s + 1))
                    act.activation(q_laid[:, s], q_sb[:].rearrange("p h (n t) -> p n h t", t=TOK), ACT.Copy)\
                        .then_inc(q_moved, 1)

                move_queries(0)
                for u in range(2 * NU + AV_LAG):
                    if u == NU - 4:
                        move_queries(1)
                    if TURN_LAG <= u < 2 * NU + TURN_LAG:
                        m = u - TURN_LAG
                        act.wait_ge(pt_ready, 2 * NU * t + m + 1)
                        act.activation(probs[:, m % 4], tr_ps[:, m % 2], ACT.Copy).then_inc(pt_copied, 1)
                    if u < 2 * NU:
                        act.wait_ge(s_sub, 2 * NU * t + u + 1)
                        act.activation(probs[:, u % 4], probs[:, u % 4], ACT.Exp).then_inc(e_ready, 1)
                    m = u - AV_LAG
                    if m >= 0 and m % NQ == NQ - 1:
                        n, s = m // NQ, m // NU
                        jj = n % NJ
                        if jj == 0:
                            act.wait_ge(o_out[s], 16 * NQ * (t + 1))
                        act.wait_ge(av_ready, 4 + 2 * NU * t + m + 1)
                        dst = o_sb[:, s, :, jj * UN * TOK:(jj + 1) * UN * TOK].rearrange("p h (y t) -> p y h t", t=TOK)
                        src = av_ps[:, n % 2].rearrange("p y (h t) -> p y h t", t=TOK)
                        act.activation(dst, src, ACT.Copy).then_inc(o_copied, 1)

        @block.tensor
        def _(pe):
            pe.wait_ge(const_made, 3)
            with pe.Fori(0, NBLK // 2) as t:
                def place(u):
                    return u // NU, u % NU // NQ, u % NQ

                def scores(u):
                    s, jj, q = place(u)
                    if u % NU == 0:
                        pe.wait_ge(k_in[s], IN_QK * (t + 1))
                        pe.wait_ge(q_moved, 1 + 2 * t + s + 1)
                    pe.wait_ge(s_masked, 2 * NU * t + u + 1)
                    rows = slice(q * HD, (q + 1) * HD)
                    for y in range(UN):
                        toks = slice((jj * UN + y) * TOK, (jj * UN + y + 1) * TOK)
                        mm = pe.matmul(sc_ps[:, u % 2, y, :], q_laid[rows, s, jj * UN + y].rearrange("p h t -> p (h t)"),
                                       k_sb[rows, s, :, toks],
                                       start=True, stop=True)
                    mm.then_inc(s_ready, 1)

                def turn(u):
                    pe.wait_ge(p_ready, 2 * NU * t + u + 1)
                    if u >= 2:
                        pe.wait_ge(pt_copied, 2 * NU * t + u - 1)
                    for y in range(UN):
                        mm = pe.transpose(tr_ps[:, u % 2, y, :], probs[:, u % 4, y, :], ident[:])
                    mm.then_inc(pt_ready, 1)

                def weigh(u):
                    s, jj, q = place(u)
                    n = u // NQ
                    if u % NU == 0:
                        pe.wait_ge(v_in[s], IN_V * (t + 1))
                    pe.wait_ge(pt_copied, 2 * NU * t + u + 1)
                    if q == 0:
                        pe.wait_ge(o_copied, 2 * NJ * t + n + 1)
                    for y in range(UN):
                        mm = pe.matmul(av_ps[q * HD:(q + 1) * HD, n % 2, y, :],
                                       v_sb[:, s, (q * NJ + jj) * UN + y, :], probs[:, u % 4, y, :],
                                       start=True, stop=True)
                    mm.then_inc(av_ready, 1)

                for u in range(2 * NU + AV_LAG):
                    if u < 2 * NU:
                        scores(u)
                    if TURN_LAG <= u < 2 * NU + TURN_LAG:
                        turn(u - TURN_LAG)
                    if u >= AV_LAG:
                        weigh(u - AV_LAG)

        @block.vector
        def _(dve):
            dve.wait_ge(const_made, 2)
            dve.tensor_scalar(same[:], diff[:], TOK - 1, None, ALU.bitwise_and).then_inc(masked, 1)
            dve.wait_ge(masked, 1)
            dve.tensor_scalar(flag[:, 0, :], same[:], 0.0, None, ALU.is_equal).then_inc(masked, 1)
            dve.wait_ge(masked, 2)
            dve.tensor_scalar(mask[:], flag[:].to_broadcast([P, H, TOK]), 1.0, BIG, ALU.subtract, ALU.mult)\
                .then_inc(masked, 1)
            dve.wait_ge(masked, 3)
            dve.sem_inc(s_masked, 2)
            with dve.Fori(0, NBLK // 2) as t:
                for u in range(2 * NU + 1):
                    n = 2 * NU * t + u + 1
                    r = u % 4
                    if u < 2 * NU:
                        dve.wait_ge(s_ready, n)
                        dve.wait_ge(av_ready, n)
                        dve.tensor_tensor(probs[:, r], sc_ps[:, u % 2],
                                          mask[:].rearrange("p h t -> p (h t)").unsqueeze(1)
                                          .to_broadcast([P, UN, P]), ALU.add).then_inc(s_masked, 1)
                        dve.wait_ge(s_masked, n + 2)
                        dve.tensor_reduce(mx[:, r], probs[:, r], AX.X, ALU.max).then_inc(s_max, 1)
                        dve.wait_ge(s_max, n)
                        dve.tensor_tensor(probs[:, r], probs[:, r], mx[:, r].unsqueeze(2).to_broadcast([P, UN, P]),
                                          ALU.subtract).then_inc(s_sub, 1)
                    if u >= 1:
                        r = (u - 1) % 4
                        dve.wait_ge(e_ready, n - 1)
                        dve.tensor_reduce(den[:, r], probs[:, r], AX.X, ALU.add).then_inc(e_sum, 1)
                        dve.wait_ge(e_sum, n - 1)
                        dve.reciprocal(rden[:, r], den[:, r]).then_inc(e_rec, 1)


def l1_output_ffn(nc, new_sem, x2, aT, W, out):
    T, D = x2.shape
    KC = D // P
    NT = T // P
    NBLK = T // BLK
    F = W["w1T"].shape[1]
    NG = F // BLK
    FC = BLK // P
    HALF = 2 * BLK
    NPC = KC * F // HALF
    PASSES2 = (0, 1)

    with ExitStack() as c:
        def sb(name, shape, dt=F32):
            return c.enter_context(nc.sbuf_tensor("f_" + name, shape, dt))

        def sem(name):
            return new_sem("f_" + name)

        def psum(name, shape):
            return c.enter_context(nc.psum_tensor("f_" + name, shape, F32))

        h_ps = psum("hidden", [P, 2, BLK])
        y_ps = psum("totals", [P, TPB, BLK])
        m_ps = psum("means", [P, 2])

        h_hl = sb("h_hl", [P, 2, KC, T], F32R)
        y = sb("y", [P, NT, D])
        w_t = sb("w_t", [P, 2 * NG, KC, BLK], F32R)
        WO = 2 * NG - 2
        w_raw = sb("w_raw", [P, 2, HALF])
        w_neg = sb("w_neg", [P, HALF])
        a_raw = sb("a_raw", [P, 2, BLK])
        a_hl = sb("a_hl", [P, 2, KC, BLK], F32R)
        act_sb = sb("act_sb", [P, 2, BLK])
        hs = sb("hs", [P, 2, D])
        ident = sb("ident", [P, P])
        ones = sb("ones", [P, P])
        mhalf = sb("mhalf", [P, 1])
        tg_bo = sb("tg_bo", [P, D])
        tg_b2 = sb("tg_b2", [P, D])
        b1 = sb("b1", [P, F // P])
        gates = sb("gates", [P, 2])
        tgs = sb("tgs", [P, 2])
        sums = sb("sums", [P, 2, NPC])
        sum2 = sb("sum2", [P, 2])
        mean = sb("mean", [P, 2])
        thr = sb("thr", [P, 2, 2])
        stats = sb("stats", [P, 2, 6])
        mv = sb("mv", [P, 2, 2])
        rstd = sb("rstd", [P, 2, 1])

        const_in = sem("const_in")
        const_made = sem("const_made")
        tg_ready = sem("tg_ready")
        const_done = sem("const_done")
        x_in = [sem(f"x_in{n}") for n in range(NBLK)]
        wo_in = [sem(f"wo_in{s}") for s in range(2)]
        wo_high = sem("wo_high")
        wo_split = sem("wo_split")
        w_in = [sem(f"w_in{s}") for s in range(2)]
        w_used = sem("w_used")
        sums_ready = sem("sums_ready")
        mean_ready = sem("mean_ready")
        thr_step = sem("thr_step")
        neg_ready = sem("neg_ready")
        a_in = [sem(f"a_in{s}") for s in range(2)]
        a_high = sem("a_high")
        a_split = sem("a_split")
        o_ready = sem("o_ready")
        o_added = sem("o_added")
        x3_ready = sem("x3_ready")
        ln_stats = sem("ln_stats")
        ln_mv = sem("ln_mv")
        ln_eps = sem("ln_eps")
        ln_rstd = sem("ln_rstd")
        ln_done = sem("ln_done")
        h_turned = sem("h_turned")
        h_high = sem("h_high")
        h_split = sem("h_split")
        hid_ready = sem("hid_ready")
        gelu_ready = sem("gelu_ready")
        g_high = sem("g_high")
        g_split = sem("g_split")
        y_ready = sem("y_ready")
        y_added = sem("y_added")
        y_done = sem("y_done")
        x_out = sem("x_out")

        x2_t = x2.rearrange("(b n p) d -> b p n d", p=P, n=TPB)
        out_t = out.rearrange("(b n p) d -> n b p d", p=P, n=TPB)
        a_t = aT.rearrange("(k p) (b t) -> k b p t", p=P, t=BLK)
        wo_t = W["woT"].rearrange("(k p) (c n) -> k c p n", p=P, n=BLK)
        w1_t = W["w1T"].rearrange("(k p) (g n) -> g p k n", p=P, n=BLK)
        w2_t = W["w2T"].rearrange("(g k p) n -> g p k n", p=P, k=KC)

        def piece(n):
            if n < 2 * NPC:
                w, m = (w1_t, w2_t)[n // NPC], n % NPC
                g, half = m // 2, m % 2
            else:
                m = n - 2 * NPC
                g, half = m // 4, m % 2
                w = (w1_t, w2_t)[m // 2 % 2]
            return w[g][:, 2 * half:2 * half + 2, :]

        def piece_dst(m):
            g, which, half = m // 4, m // 2 % 2, m % 2
            return which, w_t[:, 2 * g + which, 2 * half:2 * half + 2, :].rearrange("p k n -> p (k n)")

        block = c.enter_context(nc.Block())

        @block.sync
        def _(sp):
            sp.dma_start(gates[:], W["gates"].to_broadcast([P, 2])).then_inc(const_in, 16)
            sp.dma_start(tg_bo[:], W["bo"].to_broadcast([P, D])).then_inc(const_in, 16)
            sp.dma_start(tg_b2[:], W["b2"].to_broadcast([P, D])).then_inc(const_in, 16)
            sp.dma_start(b1[:], W["b1"]).then_inc(const_in, 16)
            for k in range(KC):
                if k >= 2:
                    sp.wait_ge(wo_split, k - 1)
                sp.dma_start(a_raw[:, k % 2, :], wo_t[k][0]).then_inc(wo_in[k % 2], 16)

            def load_piece(n):
                if n >= 2:
                    sp.wait_ge(w_used, n - 1)
                sp.dma_start(w_raw[:, n % 2, :].rearrange("p (k n) -> p k n", k=2), piece(n)).then_inc(w_in[n % 2], 16)

            def load_output(b):
                sp.dma_start(y[:, b * TPB:(b + 1) * TPB, :], x2_t[b]).then_inc(x_in[b], 16)
                for k in range(KC):
                    if KC * b + k >= 2:
                        sp.wait_ge(a_split, KC * b + k - 1)
                    sp.dma_start(a_raw[:, k % 2, :], a_t[k][b]).then_inc(a_in[k % 2], 16)

            sp.wait_ge(wo_split, KC)
            load_output(0)
            for n in range(4 * NPC):
                load_piece(n)
                if n < NT and n % TPB == 1 and n // TPB + 1 < NBLK:
                    load_output(n // TPB + 1)
            with sp.Fori(0, NBLK) as t:
                for j in range(TPB):
                    sp.wait_ge(y_done, TPB * t + j + 1)
                    sp.dma_start(out_t[j][t], y[:, bass.ds(TPB * t + j, 1), :]).then_inc(x_out, 16)
            sp.wait_ge(x_out, 16 * NT)

        @block.gpsimd
        def _(pool):
            pool.memset(ones[:], 1.0).then_inc(const_made, 1)
            pool.memset(mhalf[:], -0.5).then_inc(const_made, 1)
            pool.wait_ge(const_made, 2)
            pool.affine_select(out=ident[:], in_=ones[:], compare_op=ALU.is_equal, fill=0.0, base=0,
                               pattern=[[-1, P]], channel_multiplier=1).then_inc(const_made, 1)
            pool.sem_inc(g_split, 2)
            pool.sem_inc(gelu_ready, 2)

            def a_low(n):
                pool.wait_ge(a_high, n + 1)
                pool.tensor_tensor(a_hl[:, 1, n % KC, :], a_raw[:, n % 2, :], f32(a_hl[:, 0, n % KC, :]), ALU.subtract)\
                    .then_inc(a_split, 1)

            for n in range(KC):
                a_low(n)
            for n in range(NT):
                pool.wait_ge(ln_eps, n + 1)
                pool.tensor_tensor(rstd[:, n % 2, :], rstd[:, n % 2, :], mhalf[:], ALU.pow).then_inc(ln_rstd, 1)
                if n % TPB == TPB - 1 and n < NT - 1:
                    for k in range(KC):
                        a_low(n + 1 + k)
            with pool.Fori(0, NBLK) as t:
                for m in range(NG * FC):
                    pool.wait_ge(g_high, NG * FC * t + m + 1)
                    pool.tensor_tensor(a_hl[:, 1, m % FC, :], act_sb[:, m % 2, :], f32(a_hl[:, 0, m % FC, :]),
                                       ALU.subtract).then_inc(g_split, 1)

        @block.scalar
        def _(act):
            act.wait_ge(const_in, 64)
            act.activation(tgs[:], gates[:], ACT.Tanh).then_inc(tg_ready, 1)
            for k in range(KC):
                act.wait_ge(wo_in[k % 2], 16 * (k // 2 + 1))
                act.activation(w_t[:, WO, k, :], a_raw[:, k % 2, :], ACT.Copy).then_inc(wo_high, 1)

            def a_high_part(n):
                act.wait_ge(a_in[n % 2], 16 * (n // 2 + 1))
                if n >= KC:
                    act.wait_ge(o_ready, n // KC * TPB)
                act.activation(a_hl[:, 0, n % KC, :], a_raw[:, n % 2, :], ACT.Copy).then_inc(a_high, 1)

            def piece_sum(n):
                act.wait_ge(w_in[n % 2], 16 * (n // 2 + 1))
                act.activation(w_raw[:, n % 2, :], w_raw[:, n % 2, :], ACT.Abs,
                               accum_out=sums[:, n // NPC, n % NPC:n % NPC + 1]).then_inc(w_used, 1)
                if n == 2 * NPC - 1:
                    act.wait_ge(w_used, 2 * NPC)
                    act.drain().then_inc(sums_ready, 1)

            for n in range(KC):
                a_high_part(n)
            for n in range(NT):
                act.wait_ge(h_turned, n + 1)
                act.activation(h_hl[:, 0, :, n * P:(n + 1) * P],
                               y_ps[:, 2 + n % 2, :].rearrange("p (k n) -> p k n", k=KC), ACT.Copy).then_inc(h_high, 1)
                piece_sum(n)
                if n % TPB == 1 and n < NT - TPB:
                    for k in range(KC):
                        a_high_part(KC * (n // TPB + 1) + k)
            with act.Fori(0, NBLK) as t:
                for m in range(NG * FC):
                    n = NG * FC * t + m
                    act.wait_ge(hid_ready, n + 1)
                    act.wait_ge(g_split, n + 1)
                    act.activation(act_sb[:, m % 2, :], h_ps[:, m % 2, :], ACT.Gelu, bias=b1[:, m:m + 1])\
                        .then_inc(gelu_ready, 1)
                    act.wait_ge(gelu_ready, n + 1 + 2)
                    act.activation(a_hl[:, 0, m % FC, :], act_sb[:, m % 2, :], ACT.Copy).then_inc(g_high, 1)

        @block.tensor
        def _(pe):
            pe.wait_ge(const_made, 3)
            pe.wait_ge(wo_split, KC)

            def project_out(n):
                pe.wait_ge(a_split, KC * (n // TPB + 1))
                if n >= 2:
                    pe.wait_ge(o_added, n - 1)
                own = slice(n % TPB * P, (n % TPB + 1) * P)
                for k in range(KC):
                    for m, (wp, ap) in enumerate(PASSES):
                        mm = pe.matmul(y_ps[:, n % 2, :], a_hl[:, ap, k, own], w_t[:, WO + wp, k, :],
                                       start=(k == 0 and m == 0), stop=(k == KC - 1 and m == 2))
                mm.then_inc(o_ready, 1)

            def turn(n):
                pe.wait_ge(ln_done, n + 1)
                if n >= 2:
                    pe.wait_ge(h_split, n - 1)
                for k in range(KC):
                    mm = pe.transpose(y_ps[:, 2 + n % 2, k * P:(k + 1) * P], hs[:, n % 2, k * P:(k + 1) * P], ident[:])
                mm.then_inc(h_turned, 1)

            for n in range(NT + 2):
                if n < NT:
                    project_out(n)
                if n >= 2:
                    turn(n - 2)
            pe.wait_ge(sums_ready, 1)
            pe.wait_ge(thr_step, 1)
            pe.matmul(m_ps[:], ones[:], sum2[:], start=True, stop=True).then_inc(mean_ready, 1)
            pe.wait_ge(h_split, NT)
            with pe.Fori(0, NBLK) as t:
                def hidden(m):
                    g, f = m // FC, m % FC
                    if f == 0:
                        pe.wait_ge(w_used, 2 * NPC + 4 * g + 2)
                    pe.wait_ge(gelu_ready, NG * FC * t + m + 1)
                    for k in range(KC):
                        for ap in PASSES2:
                            mm = pe.matmul(h_ps[:, m % 2, :], w_t[:, 2 * g, k, f * P:(f + 1) * P],
                                           h_hl[:, ap, k, bass.ds(BLK * t, BLK)],
                                           start=(k == 0 and ap == 0), stop=(k == KC - 1 and ap == 1))
                    mm.then_inc(hid_ready, 1)

                def down(m):
                    g, f = m // FC, m % FC
                    if f == 0:
                        pe.wait_ge(w_used, 2 * NPC + 4 * g + 4)
                    pe.wait_ge(g_split, 2 + NG * FC * t + m + 1)
                    for j in range(TPB):
                        if m == 0:
                            pe.wait_ge(y_added, TPB * t + j + 1)
                        for ap in PASSES2:
                            mm = pe.matmul(y_ps[:, j, :], a_hl[:, ap, f, j * P:(j + 1) * P], w_t[:, 2 * g + 1, f, :],
                                           start=(m == 0 and ap == 0), stop=(m == NG * FC - 1 and ap == 1))
                        if m == NG * FC - 1:
                            mm.then_inc(y_ready, 1)

                for g in range(NG):
                    for f in range(FC):
                        hidden(FC * g + f)
                    for f in range(FC):
                        down(FC * g + f)

        @block.vector
        def _(dve):
            for k in range(KC):
                dve.wait_ge(wo_high, k + 1)
                dve.tensor_tensor(w_t[:, WO + 1, k, :], a_raw[:, k % 2, :], f32(w_t[:, WO, k, :]), ALU.subtract)\
                    .then_inc(wo_split, 1)
            dve.wait_ge(const_in, 64)
            dve.wait_ge(tg_ready, 1)
            dve.tensor_scalar(tg_bo[:], tg_bo[:], tgs[:, 0:1], None, ALU.mult).then_inc(const_done, 1)
            dve.tensor_scalar(tg_b2[:], tg_b2[:], tgs[:, 1:2], None, ALU.mult).then_inc(const_done, 1)
            dve.wait_ge(const_done, 2)

            def add_output(n):
                s = n % 2
                dve.wait_ge(x_in[n // TPB], 16)
                dve.wait_ge(o_ready, n + 1)
                dve.scalar_tensor_tensor(y[:, n, :], y_ps[:, s, :], tgs[:, 0:1], y[:, n, :], ALU.mult, ALU.add)\
                    .then_inc(o_added, 1)
                dve.wait_ge(o_added, n + 1)
                dve.tensor_tensor(y[:, n, :], y[:, n, :], tg_bo[:], ALU.add).then_inc(x3_ready, 1)
                dve.wait_ge(x3_ready, n + 1)
                dve.bn_stats(stats[:, s, :], y[:, n, :]).then_inc(ln_stats, 1)
                dve.wait_ge(ln_stats, n + 1)
                dve.bn_aggr(mv[:, s, :], stats[:, s, :]).then_inc(ln_mv, 1)
                dve.wait_ge(ln_mv, n + 1)
                dve.tensor_scalar(rstd[:, s, :], mv[:, s, 1:2], LN_EPS, None, ALU.add).then_inc(ln_eps, 1)

            def normalise(n):
                s = n % 2
                dve.wait_ge(ln_rstd, n + 1)
                if n >= 2:
                    dve.wait_ge(h_turned, n - 1)
                dve.tensor_scalar(hs[:, s, :], y[:, n, :], mv[:, s, 0:1], rstd[:, s, :], ALU.subtract, ALU.mult)\
                    .then_inc(ln_done, 1)

            def h_low_part(n):
                own = slice(n * P, (n + 1) * P)
                dve.wait_ge(h_high, n + 1)
                dve.tensor_tensor(h_hl[:, 1, :, own], y_ps[:, 2 + n % 2, :].rearrange("p (k n) -> p k n", k=KC),
                                  f32(h_hl[:, 0, :, own]), ALU.subtract).then_inc(h_split, 1)

            for n in range(NT + 2):
                if n < NT:
                    add_output(n)
                if n >= 2:
                    h_low_part(n - 2)
                if n < NT:
                    normalise(n)

            dve.wait_ge(sums_ready, 1)
            dve.tensor_reduce(sum2[:], sums[:], AX.X, ALU.add).then_inc(thr_step, 1)
            dve.wait_ge(mean_ready, 1)
            dve.tensor_scalar(mean[:], m_ps[:], 1.0 / (D * F), 1e-8, ALU.mult, ALU.max).then_inc(thr_step, 1)
            dve.wait_ge(thr_step, 2)
            dve.tensor_scalar(thr[:, :, 0], mean[:], 0.5, None, ALU.mult).then_inc(thr_step, 1)
            dve.tensor_scalar(thr[:, :, 1], mean[:], -0.5, None, ALU.mult).then_inc(thr_step, 1)
            dve.wait_ge(thr_step, 4)
            for m in range(2 * NPC):
                n = 2 * NPC + m
                which, dst = piece_dst(m)
                raw = w_raw[:, n % 2, :]
                dve.wait_ge(w_in[n % 2], 16 * (n // 2 + 1))
                if m >= 1:
                    dve.wait_ge(w_used, n)
                dve.tensor_scalar(w_neg[:], raw, thr[:, which, 1:2], None, ALU.is_lt).then_inc(neg_ready, 1)
                dve.wait_ge(neg_ready, m + 1)
                dve.scalar_tensor_tensor(dst, raw, thr[:, which, 0:1], w_neg[:], ALU.is_gt, ALU.subtract)\
                    .then_inc(w_used, 1)
            dve.sem_inc(y_added, TPB)
            with dve.Fori(0, NBLK) as t:
                for j in range(TPB):
                    tile = y[:, bass.ds(TPB * t + j, 1), :].rearrange("p a d -> p (a d)")
                    dve.wait_ge(y_ready, TPB * t + j + 1)
                    dve.scalar_tensor_tensor(tile, y_ps[:, j, :], tgs[:, 1:2], tile, ALU.mult, ALU.add)\
                        .then_inc(y_added, 1)
                    dve.wait_ge(y_added, TPB * t + TPB + j + 1)
                    dve.tensor_tensor(tile, tile, tg_b2[:], ALU.add).then_inc(y_done, 1)


def build(nc, a, out):
    T, D = a["x"].shape

    def scratch(name, shape, dt=F32):
        return nc.dram_tensor(name, shape, dt, kind="Internal").ap()

    x1, x2, v = (scratch(n, [T, D]) for n in ("x1", "x2", "l1_v"))
    qT, kT, aT = (scratch(n, [D, T]) for n in ("l1_qT", "l1_kT", "l1_aT"))

    slots = most_groups(T, a["b_router"].shape[1]) * BLK
    rows, expert_out = scratch("l0_rows", [T, D]), scratch("l0_expert_out", [slots, D])
    slot_token = scratch("l0_slot_token", [slots, 1], I32)

    def part(prefix):
        return {k[len(prefix):]: ap for k, ap in a.items() if k.startswith(prefix)}

    def stage(run, *args):
        with ExitStack() as sems:
            own = []

            def new_sem(name):
                own.append(sems.enter_context(nc.semaphore(name)))
                return own[-1]

            run(nc, new_sem, *args)
            nc.all_engine_barrier()
            for s in own:
                nc.gpsimd.sem_clear(s)
            nc.all_engine_barrier()

    stage(l0_attention, a["x"], a["ctxT"], part("a_"), x1)
    stage(l0_experts, x1, part("b_"), x2, rows, slot_token, expert_out)
    stage(l1_projections, x2, a["ctxT"], part("c_"), qT, kT, v)
    stage(l1_attention, qT, kT, v, aT)
    stage(l1_output_ffn, x2, aT, part("d_"), out)


def lay_out(i):
    import numpy as np

    def chunks(a):
        return a.reshape(-1, P).T

    B, S, D = i["x"].shape
    F = i["L0_ffn_down_weights"].shape[2]
    x = i["x"].reshape(B * S, D)
    ctx = i["ctx_2048"].reshape(B * S, D)
    shared_gu = i["L0_ffn_shared_gate_up"]
    halves = shared_gu.reshape(2, -1, F, D).transpose(1, 0, 2, 3).reshape(-1, 2 * F, D)
    g_x, g_f = i["g_xattn"], i["g_ffn"]
    a = {
        "x": x, "ctxT": ctx.T,
        "a_ki_w": i["L0_xattn_ki_w"], "a_vi_w": i["L0_xattn_vi_w"], "a_q_w": i["L0_xattn_q_w"],
        "a_o_w": i["L0_xattn_o_w"], "a_o_b": i["L0_xattn_o_b"][None], "a_gate": g_x[None, 0:1],
        "a_vecs": np.stack([chunks(i["L0_xattn_" + n]) for n in ("q_b", "ki_b", "vi_b", "nki_s", "nq_s")], 1),
        "b_gate_up": np.concatenate([i["L0_ffn_gate_up_weights"], halves]).transpose(0, 2, 1),
        "b_down": np.concatenate([i["L0_ffn_down_weights"].transpose(0, 2, 1),
                                  i["L0_ffn_shared_down"].T.reshape(-1, F, D)]),
        "b_router": i["L0_ffn_gate_weight"].T, "b_gate": g_f[None, 0:1],
        "c_wk": i["L1_xattn_Wk"].T, "c_wv": i["L1_xattn_Wv"].T, "c_wq": i["L1_xattn_Wq"].T,
        "c_kq_bias": np.stack([chunks(i["L1_xattn_bk"]), chunks(i["L1_xattn_bq"])], 1),
        "c_bv": i["L1_xattn_bv"][None],
        "d_woT": i["L1_xattn_Wo"].T, "d_bo": i["L1_xattn_bo"][None],
        "d_w1T": i["L1_ffn_w1"].T, "d_b1": chunks(i["L1_ffn_b1"]),
        "d_w2T": i["L1_ffn_w2"].T, "d_b2": i["L1_ffn_b2"][None],
        "d_gates": np.concatenate([g_x[1:2], g_f[1:2]])[None],
    }
    return {k: np.ascontiguousarray(v) for k, v in a.items()}


def kernel(**inputs):
    import numpy as np
    import concourse.bacc as bacc
    from concourse.bass_utils import run_bass_kernel_spmd

    nc = bacc.Bacc("TRN2", target_bir_lowering=False, num_devices=1)
    arrays = lay_out({k: np.asarray(v) for k, v in inputs.items()})
    aps = {k: nc.dram_tensor("in_" + k, v.shape, mybir.dt.from_np(v.dtype), kind="ExternalInput").ap()
           for k, v in arrays.items()}
    shape = inputs["x"].shape
    out = nc.dram_tensor("out", shape, F32, kind="ExternalOutput").ap()
    build(nc, aps, out.rearrange("b s d -> (b s) d"))
    r = run_bass_kernel_spmd(nc, [{"in_" + k: v for k, v in arrays.items()}], core_ids=[0])
    return r.results[0]["out"]
```

```python
from contextlib import ExitStack

import concourse.bass as bass
from concourse import mybir

P = 128
F32 = mybir.dt.float32
F32R = mybir.dt.float32r
I32 = mybir.dt.int32
ALU = mybir.AluOpType
ACT = mybir.ActivationFunctionType
AX = mybir.AxisListType

BLK = 512
TPB = BLK // P
LN_EPS = 1e-5
RMS_EPS = 1e-6
PASSES = ((0, 0), (0, 1), (1, 0))


def f32(ap):
    return ap.bitcast(F32)


def l0_attention(nc, new_sem, x, ctxT, W, x1):
    T, D = x.shape
    KC = D // P
    H = W["q_w"].shape[1] // P
    NBLK = T // BLK
    G = H // 4
    ORDER = [("k", g) for g in range(G)] + [("v", 0)] + [("q", g) for g in range(G)] + [("v", g) for g in range(1, G)]
    AT = {kg: i for i, kg in enumerate(ORDER)}
    O0 = 3 * G
    NW = 4 * G
    NP = 4 * O0
    NU = TPB * G
    INNER = H * P
    EARLY = 10
    TURN_LAG, AV_LAG = 3, 4

    with ExitStack() as c:
        def sb(name, shape, dt=F32):
            return c.enter_context(nc.sbuf_tensor("a_" + name, shape, dt))

        def sem(name):
            return new_sem("a_" + name)

        def psum(name, shape):
            return c.enter_context(nc.psum_tensor("a_" + name, shape, F32))

        proj = psum("proj", [P, 4, BLK])
        sc_ps = psum("scores", [P, 2, BLK])
        tr_ps = psum("turned", [P, 2, BLK])

        w_raw = sb("w_raw", [P, 2, KC, BLK])
        w_hl = sb("w_hl", [P, 2, 2, KC, BLK], F32R)
        a_hl = sb("a_hl", [P, 2, KC, BLK], F32R)
        c_hl = sb("c_hl", [P, 2, KC, BLK], F32R)
        c_raw = sb("c_raw", [P, 2, BLK])
        kT = sb("kT", [P, H, BLK])
        qT = sb("qT", [P, H, BLK])
        v = sb("v", [P, TPB, INNER])
        probs = sb("probs", [P, 4, 4, P])
        xr = sb("xr", [P, 2, D])
        sq = sb("sq", [P, 2, BLK])
        ssum = sb("ssum", [P, BLK])
        rk = sb("rk", [P, TPB])
        rk_diag = sb("rk_diag", [P, TPB, P])
        rq = sb("rq", [P, TPB])
        ident = sb("ident", [P, P])
        ones = sb("ones", [P, P])
        mhalf = sb("mhalf", [P, 1])
        vecs = sb("vecs", [P, 5, H])
        nqk = sb("nqk", [P, H])
        tg_ob = sb("tg_ob", [P, D])
        gate = sb("gate", [P, 1])
        tg = sb("tg", [P, 1])
        stats = sb("stats", [P, 2, 6])
        mv = sb("mv", [P, 2, 2])
        rstd = sb("rstd", [P, 2, 1])
        mx = sb("mx", [P, 4, 4])
        den = sb("den", [P, 4, 4])
        rden = sb("rden", [P, 4, 4])
        q_b, k_b, v_b, nk, nq = (vecs[:, n, :] for n in range(5))

        const_in = sem("const_in")
        const_made = sem("const_made")
        tg_ready = sem("tg_ready")
        const_done = sem("const_done")
        w_in = [sem(f"w_in{s}") for s in range(2)]
        w_high = sem("w_high")
        w_split = sem("w_split")
        c_in = [sem(f"c_in{s}") for s in range(2)]
        c_high = sem("c_high")
        c_split = sem("c_split")
        x_in = [sem(f"x_in{s}") for s in range(2)]
        r_in = [sem(f"r_in{s}") for s in range(4)]
        ln_stats = sem("ln_stats")
        ln_seen = sem("ln_seen")
        ln_mv = sem("ln_mv")
        ln_eps = sem("ln_eps")
        ln_rstd = sem("ln_rstd")
        ln_done = sem("ln_done")
        h_turned = sem("h_turned")
        h_high = sem("h_high")
        h_split = sem("h_split")
        proj_ready = sem("proj_ready")
        proj_copied = sem("proj_copied")
        proj_squared = sem("proj_squared")
        sq_added = sem("sq_added")
        ss_ready = sem("ss_ready")
        ss_eps = sem("ss_eps")
        ss_pow = sem("ss_pow")
        rk_spread = sem("rk_spread")
        rk_ready = sem("rk_ready")
        k_normed = sem("k_normed")
        s_ready = sem("s_ready")
        s_max = sem("s_max")
        s_sub = sem("s_sub")
        e_ready = sem("e_ready")
        e_sum = sem("e_sum")
        e_rec = sem("e_rec")
        p_ready = sem("p_ready")
        pt_ready = sem("pt_ready")
        pt_copied = sem("pt_copied")
        av_ready = sem("av_ready")
        av_copied = sem("av_copied")
        a_high = sem("a_high")
        a_split = sem("a_split")
        a_used = sem("a_used")
        o_ready = sem("o_ready")
        o_scaled = sem("o_scaled")
        o_done = sem("o_done")
        x_out = [sem(f"x_out{s}") for s in range(4)]

        def by_columns(w):
            return w.rearrange("(k p) (g n) -> g p k n", p=P, n=BLK)

        names = {"k": "ki_w", "v": "vi_w", "q": "q_w"}
        groups = ([by_columns(W[names[kind]])[g] for kind, g in ORDER]
                  + [W["o_w"].rearrange("(g k p) n -> g p k n", p=P, k=4)[g] for g in range(G)])
        x_t = x.rearrange("(b n p) d -> n b p d", p=P, n=TPB)
        x1_t = x1.rearrange("(b n p) d -> n b p d", p=P, n=TPB)
        ctx_t = ctxT.rearrange("(k p) (b t) -> k b p t", p=P, t=BLK)
        residual = [xr[:, 0, :], xr[:, 1, :], sq[:, 0, :], sq[:, 1, :]]
        NA = 4 * G - 1
        NSQ = H - 1

        def square_slot_free(n):
            return 0 if n < 2 else max(1, n - 2)

        block = c.enter_context(nc.Block())

        @block.sync
        def _(sp):
            sp.dma_start(vecs[:], W["vecs"]).then_inc(const_in, 16)
            sp.dma_start(tg_ob[:], W["o_b"].to_broadcast([P, D])).then_inc(const_in, 16)
            sp.dma_start(gate[:], W["gate"].to_broadcast([P, 1])).then_inc(const_in, 16)
            sp.sem_inc(w_split, 2)
            sp.sem_inc(c_split, 2)

            def load_w(n, i):
                sp.wait_ge(w_split, n + 1)
                sp.dma_start(w_raw[:, i % 2], groups[i]).then_inc(w_in[i % 2], 16)

            def load_ctx(n, b, k):
                sp.wait_ge(c_split, n + k + 1)
                sp.dma_start(c_raw[:, k % 2, :], ctx_t[k][b]).then_inc(c_in[k % 2], 16)

            load_ctx(0, 0, 0)
            load_ctx(0, 0, 1)
            load_w(0, 0)
            load_ctx(0, 0, 2)
            load_ctx(0, 0, 3)
            load_w(1, 1)
            with sp.Fori(0, NBLK) as t:
                def load_x(j):
                    if j < 2:
                        sp.wait_ge(x_out[j], 16 * t + 16)
                    else:
                        sp.wait_ge(h_turned, TPB * t + j - 1)
                    sp.dma_start(xr[:, j % 2, :], x_t[j][t]).then_inc(x_in[j % 2], 16)

                load_x(0)
                load_x(1)
                for i in range(NW):
                    load_w(NW * t + i + 2, (i + 2) % NW)
                    if i < 2:
                        load_x(i + 2)
                    if i == O0 - 1:
                        for j in range(TPB):
                            if j < 2:
                                sp.wait_ge(h_turned, TPB * t + TPB)
                            else:
                                sp.wait_ge(sq_added, 2 * NSQ * t + 2 * NSQ + 1)
                            sp.dma_start(residual[j], x_t[j][t]).then_inc(r_in[j], 16)
                    if i in (O0 - 2, O0 - 1):
                        for k in (0, 1) if i == O0 - 2 else (2, 3):
                            load_ctx(KC * t + KC, (t + 1) % NBLK, k)
                for j in range(TPB):
                    sp.wait_ge(o_done, TPB * t + j + 1)
                    sp.dma_start(x1_t[j][t], residual[j]).then_inc(x_out[j], 16)
            for j in range(TPB):
                sp.wait_ge(x_out[j], 16 * NBLK + 16)

        @block.gpsimd
        def _(pool):
            for j in range(TPB):
                pool.sem_inc(x_out[j], 16)
            pool.sem_inc(sq_added, 1)
            pool.sem_inc(ss_ready, 1)
            pool.memset(ones[:], 1.0).then_inc(const_made, 1)
            pool.memset(mhalf[:], -0.5).then_inc(const_made, 1)
            pool.wait_ge(const_made, 2)
            pool.affine_select(out=ident[:], in_=ones[:], compare_op=ALU.is_equal, fill=0.0, base=0,
                               pattern=[[-1, P]], channel_multiplier=1).then_inc(const_made, 1)

            def w_low(n, i):
                pool.wait_ge(w_high, n + 1)
                s = i % 2
                pool.tensor_tensor(w_hl[:, s, 1], w_raw[:, s], f32(w_hl[:, s, 0]), ALU.subtract)\
                    .then_inc(w_split, 1)

            def c_low(n, k):
                pool.wait_ge(c_high, n + k + 1)
                pool.tensor_tensor(c_hl[:, 1, k, :], c_raw[:, k % 2, :], f32(c_hl[:, 0, k, :]), ALU.subtract)\
                    .then_inc(c_split, 1)

            for k in range(KC):
                c_low(0, k)
            pool.wait_ge(w_split, 3)
            w_low(1, 1)
            with pool.Fori(0, NBLK) as t:
                def add_square(half, n):
                    if n == 0:
                        return
                    base = 2 * NSQ * t + half * NSQ + 1
                    pool.wait_ge(proj_squared, 2 * H * t + half * H + n + 1)
                    pool.wait_ge(sq_added, base + n - 1)
                    if n == 1:
                        pool.wait_ge(ss_ready, 2 * t + half + 1)
                        first = sq[:, 0, :]
                    else:
                        first = ssum[:]
                    pool.tensor_tensor(ssum[:], first, sq[:, n % 2, :], ALU.add).then_inc(sq_added, 1)

                def power(half, dst, width):
                    pool.wait_ge(ss_eps, 2 * t + half + 1)
                    pool.tensor_tensor(dst, dst, mhalf[:, 0:1].to_broadcast([P, width]), ALU.pow)\
                        .then_inc(ss_pow, 1)

                for i in range(NW):
                    if i < TPB:
                        pool.wait_ge(ln_eps, TPB * t + i + 1)
                        pool.tensor_tensor(rstd[:, i % 2, :], rstd[:, i % 2, :], mhalf[:], ALU.pow)\
                            .then_inc(ln_rstd, 1)
                    if i < O0 and ORDER[i][0] in "kq":
                        for j in range(4):
                            add_square("kq".index(ORDER[i][0]), 4 * ORDER[i][1] + j)
                    if i == AT["v", 0]:
                        power(0, rk[:], TPB)
                    if i == AT["v", 1]:
                        power(1, rq[:], TPB)
                    if i == O0 - 1:
                        for u in range(NU):
                            pool.wait_ge(e_rec, NU * t + u + 1)
                            pool.tensor_tensor(probs[:, u % 4], probs[:, u % 4],
                                               rden[:, u % 4].unsqueeze(2).to_broadcast([P, 4, P]), ALU.mult)\
                                .then_inc(p_ready, 1)
                            if u % 4 == 3:
                                c_low(KC * t + KC, u // 4)
                        w_low(NW * t + i + 2, i + 2)
                    else:
                        w_low(NW * t + i + 2, (i + 2) % NW)

        @block.scalar
        def _(act):
            act.wait_ge(const_in, 16 * 3)
            act.activation(tg[:], gate[:], ACT.Tanh).then_inc(tg_ready, 1)

            def w_high_part(loads, i):
                act.wait_ge(w_in[i % 2], 16 * loads)
                act.activation(w_hl[:, i % 2, 0], w_raw[:, i % 2], ACT.Copy).then_inc(w_high, 1)

            def c_high_part(loads, k):
                act.wait_ge(c_in[k % 2], 16 * loads)
                act.activation(c_hl[:, 0, k, :], c_raw[:, k % 2, :], ACT.Copy).then_inc(c_high, 1)

            for k in range(KC):
                c_high_part(k // 2 + 1, k)
            w_high_part(1, 0)
            w_high_part(1, 1)
            with act.Fori(0, NBLK) as t:
                def square(i, j):
                    half = "kq".index(ORDER[i][0])
                    n = 4 * ORDER[i][1] + j
                    bias = (k_b, q_b)[half][:, n:n + 1]
                    act.wait_ge(proj_ready, NP * t + 4 * i + j + 1)
                    act.wait_ge(sq_added, 2 * NSQ * t + half * NSQ + 1 + square_slot_free(n))
                    if half == 0 and n < 2:
                        act.wait_ge(x_out[2 + n], 16 * t + 16)
                    act.activation(sq[:, n % 2, :], proj[:, j, :], ACT.Square, bias=bias)\
                        .then_inc(proj_squared, 1)

                def h_high_part(j):
                    act.wait_ge(h_turned, TPB * t + j + 1)
                    act.activation(a_hl[:, 0, :, j * P:(j + 1) * P],
                                   tr_ps[:, j % 2, :].rearrange("p (k n) -> p k n", k=KC), ACT.Copy)\
                        .then_inc(h_high, 1)

                def a_high_part(n):
                    if n % 4 == 0:
                        act.wait_ge(av_copied, NU * t + TPB * (n // 4 + 1))
                    if n >= 4:
                        act.wait_ge(a_used, NA * t + n - 3)
                    act.activation(a_hl[:, 0, n % 4, :], qT[:, n, :], ACT.Identity, bias=v_b[:, n:n + 1])\
                        .then_inc(a_high, 1)

                def attention():
                    for u in range(NU + AV_LAG):
                        if TURN_LAG <= u < NU + TURN_LAG:
                            m = u - TURN_LAG
                            act.wait_ge(pt_ready, NU * t + m + 1)
                            act.activation(probs[:, m % 4], tr_ps[:, m % 2, :].rearrange("p (h n) -> p h n", h=4),
                                           ACT.Copy).then_inc(pt_copied, 1)
                        if u < NU:
                            b = u % TPB
                            if u == 0:
                                act.wait_ge(ss_pow, 2 * t + 2)
                            act.wait_ge(s_sub, NU * t + u + 1)
                            act.activation(probs[:, u % 4], probs[:, u % 4], ACT.Exp, scale=rq[:, b:b + 1])\
                                .then_inc(e_ready, 1)
                            if u % 4 == 3:
                                act.wait_ge(proj_ready, NP * t + NP)
                                c_high_part(KC // 2 * t + KC // 2 + u // 8 + 1, u // 4)
                        if AV_LAG <= u:
                            m = u - AV_LAG
                            g, b = m // TPB, m % TPB
                            act.wait_ge(av_ready, NU * t + m + 1)
                            act.activation(qT[:, 4 * g:4 * g + 4, b * P:(b + 1) * P],
                                           proj[:, m % 2, :].rearrange("p (h n) -> p h n", h=4), ACT.Copy)\
                                .then_inc(av_copied, 1)
                        if EARLY <= u < EARLY + 4:
                            a_high_part(u - EARLY)

                for i in range(NW):
                    if i < O0 and ORDER[i][0] in "kq":
                        for j in range(4):
                            square(i, j)
                    if i == O0:
                        w_high_part(NW // 2 * t + (i + 1) // 2 + 1, (i + 1) % 2)
                    if O0 <= i < NW - 1:
                        for n in range(4 * (i - O0) + 4, 4 * (i - O0) + 7):
                            a_high_part(n)
                    if i < O0 - 1:
                        act.wait_ge(proj_ready, NP * t + 4 * i + 4)
                    elif O0 <= i < NW - 1:
                        act.wait_ge(a_used, NA * t + 4 * (i - O0) + 4)
                    elif i == NW - 1:
                        act.wait_ge(o_ready, TPB * t + TPB)
                    if i != O0 - 1:
                        w_high_part(NW // 2 * t + (i + 2) // 2 + 1, i % 2)
                    if O0 <= i < NW - 1:
                        a_high_part(4 * (i - O0) + 7)
                    if i < TPB:
                        h_high_part(i)
                    if i == O0 - 1:
                        attention()

        @block.tensor
        def _(pe):
            pe.wait_ge(const_made, 3)
            with pe.Fori(0, NBLK) as t:
                def project(i, tiles=range(4)):
                    pe.wait_ge(w_split, NW * t + i + 3)
                    w = w_hl[:, i % 2]
                    kind = ORDER[i][0]
                    a = a_hl if kind == "q" else c_hl
                    if i == 0:
                        pe.wait_ge(c_split, KC * t + KC + 2)
                    if i == AT["q", 0]:
                        pe.wait_ge(h_split, TPB * t + TPB)
                    for j in tiles:
                        if i == 0:
                            pe.wait_ge(o_scaled, TPB * t + j + 1)
                        else:
                            pe.wait_ge(proj_copied, NP * t + 4 * (i - 1) + j + 1)
                        for k in range(KC):
                            for n, (wp, ap) in enumerate(PASSES):
                                tok, col = (a[:, ap, k], w[:, wp, k])
                                own = slice(j * P, (j + 1) * P)
                                left, right = (tok[:, own], col) if kind == "v" else (col[:, own], tok)
                                mm = pe.matmul(proj[:, j, :], left, right, start=(k == 0 and n == 0),
                                               stop=(k == KC - 1 and n == 2))
                        mm.then_inc(proj_ready, 1)

                def turn_h(j):
                    pe.wait_ge(ln_done, TPB * t + j + 1)
                    if j >= 2:
                        pe.wait_ge(h_split, TPB * t + j - 1)
                    for k in range(KC):
                        mm = pe.transpose(tr_ps[:, j % 2, k * P:(k + 1) * P], xr[:, j % 2, k * P:(k + 1) * P],
                                          ident[:])
                    mm.then_inc(h_turned, 1)

                def sum_squares(half):
                    pe.wait_ge(sq_added, 2 * NSQ * t + (half + 1) * NSQ + 1)
                    if half == 1:
                        pe.wait_ge(ss_eps, 2 * t + 1)
                    for b in range(TPB):
                        mm = pe.matmul(sc_ps[:, 0, b:b + 1], ssum[:, b * P:(b + 1) * P], ones[:, 0:1],
                                       start=True, stop=True)
                    mm.then_inc(ss_ready, 1)

                def spread_rk():
                    pe.wait_ge(rk_spread, t + 1)
                    for b in range(TPB):
                        mm = pe.matmul(sc_ps[:, 1, b * P:(b + 1) * P], ones[:], rk_diag[:, b, :],
                                       start=True, stop=True)
                    mm.then_inc(rk_ready, 1)

                def scores(u):
                    g, b = u // TPB, u % TPB
                    own = slice(b * P, (b + 1) * P)
                    if u == 0:
                        pe.wait_ge(k_normed, H * t + H)
                        pe.wait_ge(proj_copied, NP * t + 4 * AT["q", G - 1] + 4)
                        pe.wait_ge(ss_eps, 2 * t + 2)
                    if u >= 2:
                        pe.wait_ge(s_sub, NU * t + u - 1)
                    for y in range(4):
                        mm = pe.matmul(sc_ps[:, u % 2, y * P:(y + 1) * P], qT[:, 4 * g + y, own],
                                       kT[:, 4 * g + y, own], start=True, stop=True)
                    mm.then_inc(s_ready, 1)

                def turn_probs(u):
                    pe.wait_ge(p_ready, NU * t + u + 1)
                    if u >= 2:
                        pe.wait_ge(pt_copied, NU * t + u - 1)
                    for y in range(4):
                        mm = pe.transpose(tr_ps[:, u % 2, y * P:(y + 1) * P], probs[:, u % 4, y, :], ident[:])
                    mm.then_inc(pt_ready, 1)

                def weigh_values(u):
                    g, b = u // TPB, u % TPB
                    pe.wait_ge(pt_copied, NU * t + u + 1)
                    if u < 2:
                        pe.wait_ge(proj_copied, NP * t + NP)
                    else:
                        pe.wait_ge(av_copied, NU * t + u - 1)
                    for y in range(4):
                        h = 4 * g + y
                        mm = pe.matmul(proj[:, u % 2, y * P:(y + 1) * P], v[:, b, h * P:(h + 1) * P],
                                       probs[:, u % 4, y, :], start=True, stop=True)
                    mm.then_inc(av_ready, 1)

                def project_out(i, k, tiles):
                    n = 4 * (i - O0) + k
                    pe.wait_ge(w_split, NW * t + i + 3)
                    pe.wait_ge(a_split, 4 * G * t + n + 1)
                    for j in tiles:
                        if n == 0 and j < 2:
                            pe.wait_ge(av_copied, NU * t + NU)
                        for m, (wp, ap) in enumerate(PASSES):
                            mm = pe.matmul(proj[:, j, :], a_hl[:, ap, k, j * P:(j + 1) * P],
                                           w_hl[:, i % 2, wp, k], start=(n == 0 and m == 0),
                                           stop=(n == 4 * G - 1 and m == 2))
                        if n == 4 * G - 1:
                            mm.then_inc(o_ready, 1)
                        elif j == tiles[-1] and 0 in tiles:
                            mm.then_inc(a_used, 1)

                for i in range(O0 - 1):
                    project(i)
                    if i < TPB:
                        turn_h(i)
                    if i == AT["v", 0]:
                        sum_squares(0)
                    if i == AT["q", 0]:
                        spread_rk()
                    if i == AT["v", 1]:
                        sum_squares(1)
                for u in range(NU + AV_LAG):
                    if u < NU:
                        scores(u)
                    if u < 4:
                        project(O0 - 1, (u,))
                    if TURN_LAG <= u < NU + TURN_LAG:
                        turn_probs(u - TURN_LAG)
                    if u >= AV_LAG:
                        weigh_values(u - AV_LAG)
                    if u >= NU:
                        project_out(O0, u - NU, (2, 3))
                for i in range(O0, NW):
                    for k in range(4):
                        project_out(i, k, (0, 1) if i == O0 else (0, 1, 2, 3))

        @block.vector
        def _(dve):
            dve.sem_inc(o_scaled, TPB)
            dve.wait_ge(const_made, 3)
            dve.wait_ge(const_in, 16 * 3)
            dve.tensor_tensor(nqk[:], nq, nk, ALU.mult).then_inc(const_done, 1)
            dve.wait_ge(tg_ready, 1)
            dve.tensor_scalar(tg_ob[:], tg_ob[:], tg[:], None, ALU.mult).then_inc(const_done, 1)
            dve.wait_ge(const_done, 2)
            dve.wait_ge(w_high, 1)
            dve.tensor_tensor(w_hl[:, 0, 1], w_raw[:, 0], f32(w_hl[:, 0, 0]), ALU.subtract).then_inc(w_split, 1)
            with dve.Fori(0, NBLK) as t:
                def normalise_x(j):
                    s = j % 2
                    n = TPB * t + j + 1
                    dve.wait_ge(x_in[s], 16 * (TPB // 2 * t + j // 2 + 1))
                    dve.bn_stats(stats[:, s, :], xr[:, s, :]).then_inc(ln_stats, 1)
                    dve.wait_ge(ln_stats, n)
                    dve.sem_inc(ln_seen, 1)
                    dve.bn_aggr(mv[:, s, :], stats[:, s, :]).then_inc(ln_mv, 1)
                    dve.wait_ge(ln_mv, n)
                    dve.tensor_scalar(rstd[:, s, :], mv[:, s, 1:2], LN_EPS, None, ALU.add).then_inc(ln_eps, 1)
                    dve.wait_ge(ln_rstd, n)
                    dve.tensor_scalar(xr[:, s, :], xr[:, s, :], mv[:, s, 0:1], rstd[:, s, :],
                                      ALU.subtract, ALU.mult).then_inc(ln_done, 1)

                def h_low_part(j):
                    own = slice(j * P, (j + 1) * P)
                    dve.wait_ge(h_high, TPB * t + j + 1)
                    dve.tensor_tensor(a_hl[:, 1, :, own], tr_ps[:, j % 2, :].rearrange("p (k n) -> p k n", k=KC),
                                      f32(a_hl[:, 0, :, own]), ALU.subtract).then_inc(h_split, 1)

                def take(i, j):
                    kind, g = ORDER[i]
                    n = 4 * g + j
                    if kind == "v":
                        dve.wait_ge(proj_ready, NP * t + 4 * i + j + 1)
                    else:
                        dve.wait_ge(proj_squared, 2 * H * t + (H if kind == "q" else 0) + n + 1)
                    src = proj[:, j, :]
                    if kind == "k":
                        ins = dve.tensor_scalar(kT[:, n, :], src, k_b[:, n:n + 1], nqk[:, n:n + 1], ALU.add, ALU.mult)
                    elif kind == "v":
                        ins = dve.tensor_copy(v[:, j, g * BLK:(g + 1) * BLK], src)
                    else:
                        ins = dve.tensor_scalar(qT[:, n, :], src, q_b[:, n:n + 1], None, ALU.add)
                    ins.then_inc(proj_copied, 1)

                def mean_square(half, dst, src, factor):
                    dve.wait_ge(ss_ready, 2 * t + half + 2)
                    dve.tensor_scalar(dst, src, factor / INNER, factor * RMS_EPS, ALU.mult, ALU.add)\
                        .then_inc(ss_eps, 1)

                def diagonal():
                    dve.wait_ge(ss_pow, 2 * t + 1)
                    dve.tensor_tensor(rk_diag[:], ident[:].unsqueeze(1).to_broadcast([P, TPB, P]),
                                      rk[:].unsqueeze(2).to_broadcast([P, TPB, P]), ALU.mult).then_inc(rk_spread, 1)

                def normalise_k(n):
                    if n == 0:
                        dve.wait_ge(rk_ready, t + 1)
                        dve.wait_ge(proj_copied, NP * t + 4 * G)
                    dve.tensor_tensor(kT[:, n, :], kT[:, n, :], sc_ps[:, 1, :], ALU.mult).then_inc(k_normed, 1)

                def a_low_part(n):
                    dve.wait_ge(a_high, 4 * G * t + n + 1)
                    dve.scalar_tensor_tensor(a_hl[:, 1, n % 4, :], qT[:, n, :], v_b[:, n:n + 1],
                                             f32(a_hl[:, 0, n % 4, :]), ALU.add, ALU.subtract).then_inc(a_split, 1)

                def attention():
                    for u in range(NU + 1):
                        if 1 <= u <= 4:
                            take(O0 - 1, u - 1)
                        if u < NU:
                            s = sc_ps[:, u % 2, :].rearrange("p (h n) -> p h n", h=4)
                            dve.wait_ge(s_ready, NU * t + u + 1)
                            dve.tensor_reduce(mx[:, u % 4], s, AX.X, ALU.max).then_inc(s_max, 1)
                            if u >= 4:
                                dve.wait_ge(av_ready, NU * t + u - 3)
                            dve.wait_ge(s_max, NU * t + u + 1)
                            dve.tensor_tensor(probs[:, u % 4], s, mx[:, u % 4].unsqueeze(2).to_broadcast([P, 4, P]),
                                              ALU.subtract).then_inc(s_sub, 1)
                        if u >= 1:
                            m = u - 1
                            dve.wait_ge(e_ready, NU * t + m + 1)
                            dve.tensor_reduce(den[:, m % 4], probs[:, m % 4], AX.X, ALU.add).then_inc(e_sum, 1)
                            dve.wait_ge(e_sum, NU * t + m + 1)
                            dve.reciprocal(rden[:, m % 4], den[:, m % 4]).then_inc(e_rec, 1)
                        if EARLY < u <= EARLY + 4:
                            a_low_part(u - EARLY - 1)

                for i in range(NW):
                    if i < TPB:
                        normalise_x(i)
                    if i < O0 - 1:
                        for j in range(4):
                            take(i, j)
                    if i < TPB:
                        h_low_part(i)
                    if i == AT["v", 0]:
                        mean_square(0, rk[:], sc_ps[:, 0, 0:TPB], 1.0)
                        diagonal()
                    if i < O0 and ORDER[i][0] == "q":
                        for n in range(4 * ORDER[i][1], 4 * ORDER[i][1] + 4):
                            normalise_k(n)
                    if i == AT["v", 1]:
                        mean_square(1, rq[:], sc_ps[:, 0, 0:TPB], float(P))
                    if i == O0 - 1:
                        attention()
                    if i > O0:
                        for n in range(4 * (i - O0), 4 * (i - O0) + 4):
                            a_low_part(n)
                for j in range(TPB):
                    dve.wait_ge(o_ready, TPB * t + j + 1)
                    dve.wait_ge(r_in[j], 16 * t + 16)
                    dve.scalar_tensor_tensor(residual[j], proj[:, j, :], tg[:], residual[j], ALU.mult, ALU.add)\
                        .then_inc(o_scaled, 1)
                    dve.wait_ge(o_scaled, TPB * t + TPB + j + 1)
                    dve.tensor_tensor(residual[j], residual[j], tg_ob[:], ALU.add).then_inc(o_done, 1)


def most_groups(T, E):
    return (2 * T + E * (BLK - 1)) // BLK


def l0_experts(nc, new_sem, x1, W, x_shared, rows, slot_token, expert_out, place, weight):
    T, D = x1.shape
    KC = D // P
    NT = T // P
    NBLK = T // BLK
    E = W["router"].shape[1]
    F = W["down"].shape[1]
    FCH = [(f, min(P, F - f)) for f in range(0, F, P)]
    NF = len(FCH)
    MAXG = most_groups(T, E)
    NPAIR = (MAXG - 1) // 2
    COLS = slot_token.shape[0] // P
    SHARED = 2 * NBLK
    SHARED_RANK = SHARED - 3
    SCATTERED = (0, 5, 5, 19, 24, 28, 32)
    assert MAXG == 2 * NPAIR + 1 and COLS == TPB * MAXG

    with ExitStack() as c:
        def sb(name, shape, dt=F32):
            return c.enter_context(nc.sbuf_tensor("b_" + name, shape, dt))

        def sem(name):
            return new_sem("b_" + name)

        def psum(name, shape):
            return c.enter_context(nc.psum_tensor("b_" + name, shape, F32))

        gu_ps = psum("gate_up", [P, 2, 2, BLK])
        y_ps = psum("y_sum", [P, TPB, BLK])

        h_hl = sb("h_hl", [P, 2, 2, KC, BLK], F32R)
        y = sb("y", [P, NT, D])
        gu_hl = sb("gu_hl", [P, 2, 2, KC, 2 * F], F32R)
        dn_hl = sb("dn_hl", [P, 2, 2, NF, D], F32R)
        gu_raw = sb("gu_raw", [P, 2, 2 * F])
        dn_raw = sb("dn_raw", [P, 2, D])
        hs = sb("hs", [P, TPB, D])
        yg = sb("yg", [P, TPB, D])
        silu = sb("silu", [P, 2, BLK])
        prod = sb("prod", [P, 2, BLK])
        a_hl = sb("a_hl", [P, 2, NF, BLK], F32R)
        ident = sb("ident", [P, P])
        below = sb("below", [P, P])
        ones = sb("ones", [P, P])
        mhalf = sb("mhalf", [P, 1])
        r_raw = sb("r_raw", [P, KC, E])
        r_hl = sb("r_hl", [P, 2, KC, E], F32R)
        gate = sb("gate", [P, 1])
        tg = sb("tg", [P, 1])
        stats = sb("stats", [P, 2, 6])
        mv = sb("mv", [P, 2, 2])
        rstd = sb("rstd", [P, 2, 1])
        back = sb("back", [P, 1, E])
        logit = sb("logit", [P, NT, E])
        prob = sb("prob", [P, NT, E])
        left = sb("left", [P, NT, E])
        hit = sb("hit", [P, NT, E])
        pick = sb("pick", [P, 2, NT, E])
        top = sb("top", [P, NT, 1])
        taken = sb("taken", [P, E, 1])
        groups = sb("groups", [P, 1, E])
        ends = sb("ends", [P, 1, E])
        base = sb("base", [P, 1, E])
        group_no = sb("group_no", [P, MAXG, 1])
        before = sb("before", [P, MAXG, E])
        passed = sb("passed", [P, MAXG, 1])
        expert = sb("expert", [P, MAXG], I32)
        slot_f = sb("slot_f", [P, 2, NT, 1])
        slot_i = sb("slot_i", [P, 2 * NT], I32)
        slot_p = sb("slot_p", [P, 2 * NT], I32)
        slot_c = sb("slot_c", [P, 2 * NT], I32)
        token = sb("token", [P, NT], I32)
        token0 = sb("token0", [P, COLS], I32)
        wanted = sb("wanted", [P, COLS + TPB], I32)
        wanted_now = sb("wanted_now", [P, 2, TPB], I32)

        const_in = sem("const_in")
        const_made = sem("const_made")
        tg_ready = sem("tg_ready")
        token0_out = sem("token0_out")
        x_tile_in = [sem(f"x_tile_in{j}") for j in range(TPB)]
        x_in = {b: sem(f"x_in{b}") for b in range(1, NBLK)}
        ln_stats = sem("ln_stats")
        ln_mv = sem("ln_mv")
        ln_eps = sem("ln_eps")
        ln_rstd = sem("ln_rstd")
        ln_done = sem("ln_done")
        rows_out = [sem(f"rows_out{j}") for j in range(TPB)]
        rows_in = [sem(f"rows_in{j}") for j in range(TPB)]
        h_turned = sem("h_turned")
        h_high = sem("h_high")
        h_split = sem("h_split")
        r_high = sem("r_high")
        r_split = sem("r_split")
        logits_ready = sem("logits_ready")
        logits_taken = sem("logits_taken")
        route = sem("route")
        exp_ready = sem("exp_ready")
        picks_ready = sem("picks_ready")
        rank_ready = sem("rank_ready")
        rank_taken = sem("rank_taken")
        places_ready = sem("places_ready")
        experts_ready = sem("experts_ready")
        tokens_out = sem("tokens_out")
        wanted_in = sem("wanted_in")
        wanted_ready = sem("wanted_ready")
        gather_free = sem("gather_free")
        gu_in = [sem(f"gu_in{s}") for s in range(2)]
        gu_high = sem("gu_high")
        gu_split = sem("gu_split")
        dn_in = [sem(f"dn_in{s}") for s in range(2)]
        dn_high = sem("dn_high")
        dn_split = sem("dn_split")
        gu_ready = sem("gu_ready")
        silu_ready = sem("silu_ready")
        prod_ready = sem("prod_ready")
        a_high = sem("a_high")
        a_split = sem("a_split")
        y_ready = sem("y_ready")
        y_taken = sem("y_taken")
        yg_out = sem("yg_out")
        yg_last_out = sem("yg_last_out")
        x_out = sem("x_out")

        x1_t = x1.rearrange("(b n p) d -> b p n d", p=P, n=TPB)
        x_shared_t = x_shared.rearrange("(b n p) d -> b p n d", p=P, n=TPB)
        gu_t = W["gate_up"].rearrange("e (k p) f -> k e p f", p=P)
        slot_token_t = slot_token.rearrange("(p c) o -> p (c o)", p=P)
        expert_out_t = expert_out.rearrange("(p g j) d -> g p (j d)", p=P, j=TPB)

        block = c.enter_context(nc.Block())


        @block.sync
        def _(sp):
            def load_weights(m, e, s):
                for k in range(KC):
                    sp.wait_ge(gu_split, KC * m + k + 1)
                    sp.dma_start(gu_raw[:, k % 2, :], gu_t[k][e]).then_inc(gu_in[k % 2], 16)
                    if k < NF:
                        start, width = FCH[k]
                        slot = (NF * s + k) % 2
                        sp.wait_ge(dn_split, NF * m + k + 1)
                        sp.dma_start(dn_raw[0:width, slot, :], W["down"][e, start:start + width, :])\
                            .then_inc(dn_in[slot], 16)

            for b in range(NBLK):
                if b:
                    sp.dma_start(y[:, b * TPB:(b + 1) * TPB, :], x1_t[b]).then_inc(x_in[b], 16)
                else:
                    for j in range(TPB):
                        sp.dma_start(y[:, j, :], x1[j * P:(j + 1) * P, :]).then_inc(x_tile_in[j], 16)
                    sp.dma_start(gate[:], W["gate"].to_broadcast([P, 1])).then_inc(const_in, 16)
                    sp.dma_start(r_raw[:], W["router"].rearrange("(k p) e -> p k e", p=P)).then_inc(const_in, 16)
                    sp.sem_inc(gu_split, 2)
                    sp.sem_inc(dn_split, 2)
                    load_weights(0, E, 0)
            sp.wait_ge(const_made, 7)
            sp.dma_start(slot_token_t, token0[:]).then_inc(token0_out, 16)
            for n in range(NT):
                if n == TPB:
                    load_weights(1, E + 1, 1)
                sp.wait_ge(ln_done, n + 1)
                sp.dma_start(rows[n * P:(n + 1) * P, :], hs[:, n % TPB, :]).then_inc(rows_out[n % TPB], 16)
            def store_block(b):
                sp.wait_ge(y_taken, 2 * TPB * (b + 1))
                sp.dma_start(x_shared_t[b], y[:, b * TPB:(b + 1) * TPB, :]).then_inc(x_out, 16)

            for b in range(NBLK - 1):
                store_block(b)
            sp.wait_ge(experts_ready, 1)

            def load_group_weights(g, s):
                e = sp.value_load(expert[0:1, bass.ds(g, 1)], min_val=0, max_val=E - 1)
                for k in range(KC):
                    sp.wait_ge(gu_split, KC * (g + 2) + k + 1)
                    sp.dma_start(gu_raw[:, k % 2, :], gu_t[k][bass.ds(e, 1)].rearrange("a p f -> (a p) f"))\
                        .then_inc(gu_in[k % 2], 16)
                    if k < NF:
                        start, width = FCH[k]
                        slot = (NF * s + k) % 2
                        sp.wait_ge(dn_split, NF * (g + 2) + k + 1)
                        sp.dma_start(dn_raw[0:width, slot, :],
                                     W["down"][bass.ds(e, 1), start:start + width, :].rearrange("a p f -> (a p) f"))\
                            .then_inc(dn_in[slot], 16)

            sp.wait_ge(tokens_out, 2 * NT * 16)
            sp.dma_start(wanted[:, 0:COLS], slot_token_t).then_inc(wanted_in, 16)
            load_group_weights(0, 0)
            store_block(NBLK - 1)
            with sp.Fori(0, NPAIR) as t:
                load_group_weights(2 * t + 1, 1)
                load_group_weights(2 * t + 2, 0)
            sp.wait_ge(yg_out, 16 * (MAXG - 1) + 16)
            sp.wait_ge(yg_last_out, 16 * TPB)
            for j in range(TPB):
                sp.wait_ge(rows_out[j], 16 * NBLK)
            sp.wait_ge(x_out, 16 * NBLK)

        @block.gpsimd
        def _(pool):
            pool.memset(ones[:], 1.0).then_inc(const_made, 1)
            pool.memset(mhalf[:], -0.5).then_inc(const_made, 1)
            pool.memset(token0[:], 0).then_inc(const_made, 1)
            pool.memset(wanted[:, COLS:COLS + TPB], 0).then_inc(const_made, 1)
            pool.iota(back[:, 0, :], pattern=[[1, E]], base=-E, channel_multiplier=0,
                      allow_small_or_imprecise_dtypes=True).then_inc(const_made, 1)
            pool.iota(group_no[:, :, 0], pattern=[[1, MAXG]], base=0, channel_multiplier=0,
                      allow_small_or_imprecise_dtypes=True).then_inc(const_made, 1)
            pool.iota(token[:], pattern=[[P, NT]], base=0, channel_multiplier=1).then_inc(const_made, 1)
            pool.wait_ge(const_made, 7)
            pool.affine_select(out=ident[:], in_=ones[:], compare_op=ALU.is_equal, fill=0.0, base=0,
                               pattern=[[-1, P]], channel_multiplier=1).then_inc(const_made, 1)
            pool.affine_select(out=below[:], in_=ones[:], compare_op=ALU.is_ge, fill=0.0, base=-1,
                               pattern=[[1, P]], channel_multiplier=-1).then_inc(const_made, 1)

            def power(n):
                pool.wait_ge(ln_eps, n + 1)
                pool.tensor_tensor(rstd[:, n % 2, :], rstd[:, n % 2, :], mhalf[:], ALU.pow).then_inc(ln_rstd, 1)

            def powers(b):
                for j in range(TPB):
                    power(TPB * b + j)

            def low_parts(m, s, chunks):
                for k in chunks:
                    pool.wait_ge(gu_high, KC * m + k + 1)
                    pool.tensor_tensor(gu_hl[:, s, 1, k, :], gu_raw[:, k % 2, :], f32(gu_hl[:, s, 0, k, :]),
                                       ALU.subtract).then_inc(gu_split, 1)
                    if k < NF:
                        w = FCH[k][1]
                        pool.wait_ge(dn_high, NF * m + k + 1)
                        pool.tensor_tensor(dn_hl[0:w, s, 1, k, :], dn_raw[0:w, (NF * s + k) % 2, :],
                                           f32(dn_hl[0:w, s, 0, k, :]), ALU.subtract).then_inc(dn_split, 1)

            def a_low(step, par, f):
                w = FCH[f][1]
                pool.wait_ge(a_high, NF * step + f + 1)
                pool.tensor_tensor(a_hl[0:w, 1, f, :], prod[0:w, (NF * par + f) % 2, :], f32(a_hl[0:w, 0, f, :]),
                                   ALU.subtract).then_inc(a_split, 1)

            def gather_rows(g, s):
                if isinstance(g, int) and g == 0:
                    pool.wait_ge(wanted_in, 16)
                    for j in range(TPB):
                        pool.wait_ge(rows_out[j], 16 * NBLK)
                pool.wait_ge(h_turned, TPB * (g + NBLK))
                pool.sem_inc(gather_free, 1)
                pool.tensor_copy(wanted_now[:, s, :], wanted[:, bass.ds(TPB * g, TPB)]).then_inc(wanted_ready, 1)
                pool.wait_ge(wanted_ready, g + 1)
                pool.sem_inc(gather_free, 1)
                for j in range(TPB):
                    pool.indirect_dma_start(hs[:, j, :], None, rows,
                                            bass.IndirectOffsetOnAxis(ap=wanted_now[:, s, j:j + 1], axis=0))\
                        .then_inc(rows_in[j], 16)

            pool.sem_inc(a_split, 2)
            pool.sem_inc(prod_ready, 2)
            powers(0)
            low_parts(0, 0, range(KC))
            powers(1)
            low_parts(1, 1, range(KC))
            for step in range(SHARED - 1):
                for f in range(NF):
                    a_low(step, step % 2, f)
                    if f == 0 and step in (1, 3):
                        powers(step // 2 + 2)
                    if step == SHARED_RANK and f == 0:
                        pool.wait_ge(token0_out, 16)
                        pool.wait_ge(places_ready, 1)
                    if step >= SHARED_RANK:
                        part = NF * (step - SHARED_RANK) + f
                        for n in range(2 * NT * SCATTERED[part] // SCATTERED[-1],
                                       2 * NT * SCATTERED[part + 1] // SCATTERED[-1]):
                            pool.indirect_dma_start(
                                slot_token, bass.IndirectOffsetOnAxis(ap=place[:, n // NT, n % NT:n % NT + 1], axis=0),
                                token[:, n % NT:n % NT + 1], None).then_inc(tokens_out, 16)
            gather_rows(0, 0)

            def group_step(step, par, g, s):
                a_low(step, par, 0)
                low_parts(g + 2, s, range(2))
                a_low(step, par, 1)
                low_parts(g + 2, s, range(2, KC - 1))
                a_low(step, par, 2)
                gather_rows(g + 1, 1 - s)

            group_step(SHARED - 1, 1, 0, 0)
            with pool.Fori(0, NPAIR) as t:
                for i in range(2):
                    group_step(SHARED + 2 * t + i, i, 2 * t + i + 1, 1 - i)
            for f in range(NF):
                a_low(SHARED + MAXG - 1, 0, f)

            for j in range(TPB):
                pool.wait_ge(rows_in[j], 16 * (MAXG + 1))

        @block.scalar
        def _(act):
            act.wait_ge(const_in, 32)
            act.activation(tg[:], gate[:], ACT.Tanh).then_inc(tg_ready, 1)
            act.activation(r_hl[:, 0], r_raw[:], ACT.Copy).then_inc(r_high, 1)

            def high_parts(m, half_m, s, chunks):
                for k in chunks:
                    act.wait_ge(gu_in[k % 2], 16 * (KC // 2 * m + k // 2 + 1))
                    act.activation(gu_hl[:, s, 0, k, :], gu_raw[:, k % 2, :], ACT.Copy).then_inc(gu_high, 1)
                    if k < NF:
                        w = FCH[k][1]
                        act.wait_ge(dn_in[(NF * s + k) % 2], 16 * (NF * half_m + (NF * s + k) // 2 + 1))
                        act.activation(dn_hl[0:w, s, 0, k, :], dn_raw[0:w, (NF * s + k) % 2, :], ACT.Copy)\
                            .then_inc(dn_high, 1)

            def h_high_parts(u, s):
                for j in range(TPB):
                    act.wait_ge(h_turned, TPB * u + j + 1)
                    act.activation(h_hl[:, s, 0, :, j * P:(j + 1) * P],
                                   y_ps[:, j, :].rearrange("p (k n) -> p k n", k=KC), ACT.Copy).then_inc(h_high, 1)

            def gate_part(step, par, f):
                w = FCH[f][1]
                n = (NF * par + f) % 2
                act.wait_ge(gu_ready, NF * step + f + 1)
                act.wait_ge(prod_ready, NF * step + f - 1 + 2)
                act.activation(silu[0:w, n, :], gu_ps[0:w, n, 0, :], ACT.Silu).then_inc(silu_ready, 1)

            def a_high_part(step, par, f):
                w = FCH[f][1]
                act.wait_ge(prod_ready, NF * step + f + 1 + 2)
                act.activation(a_hl[0:w, 0, f, :], prod[0:w, (NF * par + f) % 2, :], ACT.Copy).then_inc(a_high, 1)

            def chunk(step, par, f):
                gate_part(step, par, f)
                a_high_part(step, par, f)

            h_high_parts(0, 0)
            high_parts(0, 0, 0, range(KC))
            high_parts(1, 0, 1, range(2))
            for step in range(SHARED - 1):
                for f in range(NF):
                    chunk(step, step % 2, f)
                    if step == 0 and f == 1:
                        high_parts(1, 0, 1, range(2, KC))
                    if f == (step == 0) and step % 2 == 0 and step // 2 + 1 < NBLK:
                        h_high_parts(step // 2 + 1, (step // 2 + 1) % 2)
                    if f == 1 and step == 2 * (NBLK - 2):
                        act.wait_ge(route, 2)
                        act.activation(left[:], left[:], ACT.Exp).then_inc(exp_ready, 1)

            def store_group(g):
                act.wait_ge(y_taken, TPB * (SHARED + g + 1))
                act.dma_start(expert_out_t[bass.ds(g, 1)].rearrange("a p f -> (a p) f"),
                              yg[:].rearrange("p j d -> p (j d)")).then_inc(yg_out, 16)

            def group_step(step, par, g, half_m, s):
                chunk(step, par, 0)
                act.wait_ge(y_ready, TPB * step)
                high_parts(g + 2, half_m, s, range(2))
                h_high_parts(g + NBLK, s)
                chunk(step, par, 1)
                high_parts(g + 2, half_m, s, range(2, KC - 1))
                chunk(step, par, 2)
                high_parts(g + 2, half_m, s, range(KC - 1, KC))

            group_step(SHARED - 1, 1, 0, 1, 0)
            with act.Fori(0, NPAIR) as t:
                for i in range(2):
                    group_step(SHARED + 2 * t + i, i, 2 * t + i + 1, t + 1 + i, 1 - i)
                    store_group(2 * t + i)
            for f in range(NF):
                chunk(SHARED + MAXG - 1, 0, f)
            for j in range(TPB):
                act.wait_ge(y_taken, TPB * (SHARED + MAXG - 1) + j + 1)
                act.dma_start(expert_out_t[MAXG - 1][:, j * D:(j + 1) * D], yg[:, j, :]).then_inc(yg_last_out, 16)

        @block.tensor
        def _(pe):
            pe.wait_ge(const_made, 9)

            def turn(u, ready):
                for j in range(TPB):
                    ready(j)
                    for k in range(KC):
                        mm = pe.transpose(y_ps[:, j, k * P:(k + 1) * P], hs[:, j, k * P:(k + 1) * P], ident[:])
                    mm.then_inc(h_turned, 1)

            def turn_block(b, step):
                def ready(j):
                    pe.wait_ge(ln_done, TPB * b + j + 1)
                    if step:
                        pe.wait_ge(y_taken, TPB * (step - 1) + j + 1)
                    elif b:
                        pe.wait_ge(logits_taken, 1)
                turn(b, ready)

            def turn_group(g, step):
                def ready(j):
                    pe.wait_ge(rows_in[j], 16 * (g + 1))
                    pe.wait_ge(y_taken, TPB * (step - 1) + j + 1)
                turn(NBLK + g, ready)

            def logits(b):
                pe.wait_ge(h_split, TPB * (b + 1))
                for j in range(TPB):
                    for k in range(KC):
                        for m, (wp, ap) in enumerate(PASSES):
                            mm = pe.matmul(y_ps[:, 0, j * E:(j + 1) * E], h_hl[:, b % 2, ap, k, j * P:(j + 1) * P],
                                           r_hl[:, wp, k, :], start=(k == 0 and m == 0), stop=(k == KC - 1 and m == 2))
                mm.then_inc(logits_ready, 1)

            def gate_up(step, par, s, hslot, f):
                start, w = FCH[f]
                n = (NF * par + f) % 2
                pe.wait_ge(prod_ready, NF * step + f - 1 + 2)
                for part in range(2):
                    cols = slice(part * F + start, part * F + start + w)
                    for k in range(KC):
                        for m, (wp, ap) in enumerate(PASSES):
                            mm = pe.matmul(gu_ps[0:w, n, part, :], gu_hl[:, s, wp, k, cols], h_hl[:, hslot, ap, k, :],
                                           start=(k == 0 and m == 0), stop=(k == KC - 1 and m == 2))
                mm.then_inc(gu_ready, 1)

            def down(step, s, f, freed):
                w = FCH[f][1]
                pe.wait_ge(a_split, NF * step + f + 1 + 2)
                for j in range(TPB):
                    if f == 0:
                        freed(j)
                    for m, (wp, ap) in enumerate(PASSES):
                        mm = pe.matmul(y_ps[:, j, :], a_hl[0:w, ap, f, j * P:(j + 1) * P], dn_hl[0:w, s, wp, f, :],
                                       start=(f == 0 and m == 0), stop=(f == NF - 1 and m == 2))
                    if f == NF - 1:
                        mm.then_inc(y_ready, 1)

            def ranks():
                pe.wait_ge(picks_ready, 2)
                pe.wait_ge(y_taken, TPB * SHARED_RANK)
                both = hit[:].rearrange("p n e -> p (n e)")
                pe.matmul(y_ps[:, 0, 0:NT * E], below[:], both, start=True, stop=False)
                for n in range(1, NT):
                    pe.matmul(y_ps[:, 0, n * E:NT * E], ones[:], both[:, 0:(NT - n) * E], start=False,
                              stop=(n == NT - 1))
                pe.matmul(y_ps[:, 1, 0:E], ones[:], taken[:, :, 0], start=True, stop=True).then_inc(rank_ready, 1)

            pe.wait_ge(r_split, 1)
            turn_block(0, 0)
            logits(0)
            for step in range(SHARED):
                b, s = step // 2, step % 2
                if b == 0:
                    pe.wait_ge(gu_split, KC * (s + 1) + 2)
                gate_up(step, s, s, b % 2, 0)
                ahead = s == 0 and b + 1 < NBLK
                if step == 0:
                    gate_up(step, s, s, b % 2, 1)
                    pe.wait_ge(logits_taken, 1)
                if ahead:
                    turn_block(b + 1, step)
                if step == SHARED_RANK:
                    ranks()
                if step == SHARED - 1:
                    turn_group(0, step)
                if step:
                    gate_up(step, s, s, b % 2, 1)
                    if ahead:
                        logits(b + 1)
                gate_up(step, s, s, b % 2, 2)
                if step == 0:
                    logits(b + 1)
                if b == 0:
                    pe.wait_ge(dn_split, NF * (s + 1) + 2)

                def freed(j):
                    if ahead:
                        pe.wait_ge(h_split, TPB * (b + 1) + j + 1)
                        pe.wait_ge(logits_taken, b + 2)
                    elif step == SHARED_RANK:
                        pe.wait_ge(rank_taken, 1)
                    elif step == SHARED - 1:
                        pe.wait_ge(h_split, TPB * NBLK + j + 1)
                    if not ahead and step:
                        pe.wait_ge(y_taken, TPB * (step - 1) + j + 1)

                for f in range(NF):
                    down(step, s, f, freed)

            def group(g, s):
                step = SHARED + g
                last = isinstance(g, int)
                pe.wait_ge(gu_split, KC * (g + 3) + 2)
                pe.wait_ge(h_split, TPB * (NBLK + g + 1))
                gate_up(step, s, s, s, 0)
                if not last:
                    turn_group(g + 1, step)
                gate_up(step, s, s, s, 1)
                gate_up(step, s, s, s, 2)
                pe.wait_ge(dn_split, NF * (g + 3) + 2)

                def freed(j):
                    if last:
                        pe.wait_ge(y_taken, TPB * (step - 1) + j + 1)
                    else:
                        pe.wait_ge(h_split, TPB * (NBLK + g + 1) + j + 1)

                for f in range(NF):
                    down(step, s, f, freed)

            with pe.Fori(0, NPAIR) as t:
                for i in range(2):
                    group(2 * t + i, i)
            group(MAXG - 1, 0)

        @block.vector
        def _(dve):
            def statistics(n):
                s = n % 2
                dve.wait_ge(x_in[n // TPB] if n >= TPB else x_tile_in[n], 16)
                dve.bn_stats(stats[:, s, :], y[:, n, :]).then_inc(ln_stats, 1)
                dve.wait_ge(ln_stats, n + 1)
                dve.bn_aggr(mv[:, s, :], stats[:, s, :]).then_inc(ln_mv, 1)
                dve.wait_ge(ln_mv, n + 1)
                dve.tensor_scalar(rstd[:, s, :], mv[:, s, 1:2], LN_EPS, None, ALU.add).then_inc(ln_eps, 1)

            def normalise(n):
                s = n % 2
                dve.wait_ge(ln_rstd, n + 1)
                if n >= TPB:
                    dve.wait_ge(h_turned, n - TPB + 1)
                    dve.wait_ge(rows_out[n % TPB], 16 * (n // TPB))
                dve.tensor_scalar(hs[:, n % TPB, :], y[:, n, :], mv[:, s, 0:1], rstd[:, s, :], ALU.subtract, ALU.mult)\
                    .then_inc(ln_done, 1)

            def layer_norm(b):
                for j in range(TPB + 1):
                    if j < TPB:
                        statistics(TPB * b + j)
                    if j >= 1:
                        normalise(TPB * b + j - 1)

            def h_low_parts(u, s):
                for j in range(TPB):
                    dve.wait_ge(h_high, TPB * u + j + 1)
                    dve.tensor_tensor(h_hl[:, s, 1, :, j * P:(j + 1) * P],
                                      y_ps[:, j, :].rearrange("p (k n) -> p k n", k=KC),
                                      f32(h_hl[:, s, 0, :, j * P:(j + 1) * P]), ALU.subtract).then_inc(h_split, 1)

            def take_logits(b):
                dve.wait_ge(logits_ready, b + 1)
                dve.tensor_copy(logit[:, b * TPB:(b + 1) * TPB, :],
                                y_ps[:, 0, 0:TPB * E].rearrange("p (n e) -> p n e", e=E)).then_inc(logits_taken, 1)

            steps = [0]

            def step_done(ins):
                steps[0] += 1
                ins.then_inc(route, 1)
                dve.wait_ge(route, steps[0])

            every = [P, NT, E]
            spread = back[:].to_broadcast(every)

            def choose():
                dve.wait_ge(logits_taken, NBLK)
                step_done(dve.tensor_reduce(top[:], logit[:], AX.X, ALU.max))
                step_done(dve.tensor_tensor(left[:], logit[:], top[:].to_broadcast(every), ALU.subtract))
                dve.wait_ge(exp_ready, 1)
                step_done(dve.tensor_reduce(top[:], left[:], AX.X, ALU.add))
                step_done(dve.reciprocal(top[:], top[:]))
                step_done(dve.tensor_tensor(prob[:], left[:], top[:].to_broadcast(every), ALU.mult))
                for r in range(2):
                    rest = (prob, left)[r]
                    step_done(dve.tensor_reduce(weight[:, r, :].unsqueeze(2), rest[:], AX.X, ALU.max))
                    step_done(dve.tensor_tensor(hit[:], rest[:], weight[:, r, :].unsqueeze(2).to_broadcast(every),
                                                ALU.is_equal))
                    step_done(dve.tensor_tensor(hit[:], hit[:], spread, ALU.mult))
                    step_done(dve.tensor_reduce(top[:], hit[:], AX.X, ALU.min))
                    step_done(dve.tensor_tensor(pick[:, r], spread, top[:].to_broadcast(every), ALU.is_equal))
                    if r == 0:
                        step_done(dve.scalar_tensor_tensor(left[:], pick[:, 0], -2.0, prob[:], ALU.mult, ALU.add))
                dve.tensor_tensor(hit[:], pick[:, 0], pick[:, 1], ALU.add).then_inc(picks_ready, 1)
                dve.wait_ge(picks_ready, 1)
                dve.tensor_reduce(taken[:], hit[:].rearrange("p n e -> p e n"), AX.X, ALU.add).then_inc(picks_ready, 1)
                dve.wait_ge(tg_ready, 1)
                step_done(dve.tensor_scalar(weight[:], weight[:], tg[:], None, ALU.mult))

            def assign():
                dve.wait_ge(rank_ready, 1)
                count = y_ps[:, 1:2, 0:E]
                step_done(dve.tensor_scalar(groups[:], count, 0.0, None, ALU.is_gt))
                for k in range(1, NBLK):
                    step_done(dve.scalar_tensor_tensor(groups[:], count, float(BLK * k), groups[:], ALU.is_gt, ALU.add))
                step_done(dve.tensor_copy(ends[:], groups[:]))
                for e in range(1, E):
                    step_done(dve.tensor_tensor(ends[:, :, e:e + 1], ends[:, :, e:e + 1], ends[:, :, e - 1:e], ALU.add))
                step_done(dve.tensor_tensor(base[:], ends[:], groups[:], ALU.subtract))
                step_done(dve.tensor_scalar(base[:], base[:], float(BLK), None, ALU.mult))
                step_done(dve.tensor_tensor(left[:], y_ps[:, 0, 0:NT * E].rearrange("p (n e) -> p n e", e=E),
                                            base[:].to_broadcast(every), ALU.add))
                dve.sem_inc(rank_taken, 1)
                for r in range(2):
                    step_done(dve.tensor_tensor(hit[:], pick[:, r], left[:], ALU.mult))
                    step_done(dve.tensor_reduce(slot_f[:, r], hit[:], AX.X, ALU.add))
                step_done(dve.tensor_copy(slot_i[:], slot_f[:].rearrange("p r n o -> p (r n o)")))
                step_done(dve.tensor_scalar(slot_p[:], slot_i[:], P - 1, None, ALU.bitwise_and))
                step_done(dve.tensor_scalar(slot_c[:], slot_i[:], P.bit_length() - 1, None, ALU.logical_shift_right))
                dve.scalar_tensor_tensor(place[:].rearrange("p r n -> p (r n)"), slot_p[:], float(COLS), slot_c[:],
                                         ALU.mult, ALU.add).then_inc(places_ready, 1)
                lot = [P, MAXG, E]
                step_done(dve.tensor_tensor(before[:], ends[:].to_broadcast(lot), group_no[:].to_broadcast(lot),
                                            ALU.is_le))
                step_done(dve.tensor_reduce(passed[:], before[:], AX.X, ALU.add))
                dve.tensor_scalar(expert[:], passed[:, :, 0], float(E - 1), None, ALU.min).then_inc(experts_ready, 1)

            def product(step, par, f):
                w = FCH[f][1]
                n = (NF * par + f) % 2
                dve.wait_ge(silu_ready, NF * step + f + 1)
                dve.wait_ge(a_split, NF * step + f + 1)
                dve.tensor_tensor(prod[0:w, n, :], silu[0:w, n, :], gu_ps[0:w, n, 1, :], ALU.mult)\
                    .then_inc(prod_ready, 1)

            def last_low_part(m, s):
                k = KC - 1
                dve.wait_ge(gu_high, KC * m + k + 1)
                dve.wait_ge(gu_split, KC * m + k + 2)
                dve.tensor_tensor(gu_hl[:, s, 1, k, :], gu_raw[:, k % 2, :], f32(gu_hl[:, s, 0, k, :]),
                                  ALU.subtract).then_inc(gu_split, 1)

            dve.wait_ge(const_made, 7)
            layer_norm(0)
            dve.wait_ge(r_high, 1)
            dve.tensor_tensor(r_hl[:, 1], r_raw[:], f32(r_hl[:, 0]), ALU.subtract).then_inc(r_split, 1)
            h_low_parts(0, 0)
            layer_norm(1)
            take_logits(0)
            dve.wait_ge(tg_ready, 1)
            for step in range(SHARED):
                b, s = step // 2, step % 2
                product(step, s, 0)
                if step == 0:
                    product(step, s, 1)
                if s == 0 and b + 1 < NBLK:
                    h_low_parts(b + 1, (b + 1) % 2)
                elif s == 1 and b + 2 < NBLK:
                    layer_norm(b + 2)
                elif step == SHARED_RANK:
                    assign()
                elif step == SHARED - 1:
                    h_low_parts(NBLK, 0)
                if step == 0:
                    product(step, s, 2)
                    take_logits(b + 1)
                else:
                    product(step, s, 1)
                    if s == 0 and b + 1 < NBLK:
                        take_logits(b + 1)
                    if step == SHARED_RANK - 1:
                        choose()
                    product(step, s, 2)
                if step == SHARED - 1:
                    last_low_part(2, 0)
                for j in range(TPB):
                    tile = TPB * b + j
                    dve.wait_ge(y_ready, TPB * step + j + 1)
                    dve.scalar_tensor_tensor(y[:, tile, :], y_ps[:, j, :], tg[:], y[:, tile, :], ALU.mult, ALU.add)\
                        .then_inc(y_taken, 1)

            def take_group(g):
                for j in range(TPB):
                    if j == 0:
                        dve.wait_ge(yg_out, 16 * g + 16)
                    dve.wait_ge(y_ready, TPB * (SHARED + g) + j + 1)
                    dve.tensor_copy(yg[:, j, :], y_ps[:, j, :]).then_inc(y_taken, 1)

            dve.sem_inc(yg_out, 16)
            with dve.Fori(0, NPAIR) as t:
                for i in range(2):
                    product(SHARED + 2 * t + i, i, 0)
                    h_low_parts(NBLK + 2 * t + i + 1, 1 - i)
                    product(SHARED + 2 * t + i, i, 1)
                    product(SHARED + 2 * t + i, i, 2)
                    last_low_part(2 * t + i + 3, 1 - i)
                    take_group(2 * t + i)
            for f in range(NF):
                product(SHARED + MAXG - 1, 0, f)
            take_group(MAXG - 1)


def l1_projections(nc, new_sem, x_shared, expert_out, place, weight, ctxT, W, w_ffn, x2, qT, kT, v, sums):
    T, D = x2.shape
    TURN_AFTER = {1: 0, 3: 1, 4: 2, 5: 3}
    KC = D // P
    NBLK = T // BLK
    NO = 3 * KC
    RING = 4
    HALF = KC // 2 * BLK
    assert w_ffn.shape[0] == 2 * NBLK

    with ExitStack() as c:
        def sb(name, shape, dt=F32):
            return c.enter_context(nc.sbuf_tensor("p_" + name, shape, dt))

        def sem(name):
            return new_sem("p_" + name)

        def psum(name, shape):
            return c.enter_context(nc.psum_tensor("p_" + name, shape, F32))

        proj = psum("proj", [P, 4, BLK])
        tr_ps = psum("turned", [P, 2, BLK])
        w_raw = sb("w_raw", [P, 3, KC, D])
        w_hl = sb("w_hl", [P, 3, 2, KC, D], F32R)
        c_raw = sb("c_raw", [P, KC, BLK])
        c_hl = sb("c_hl", [P, 2, KC, BLK], F32R)
        a_hl = sb("a_hl", [P, 2, KC, BLK], F32R)
        xr = sb("xr", [P, TPB, D])
        routed = sb("routed", [P, TPB, 2, D])
        place_now = sb("place_now", [P, 2, TPB], I32)
        hn = sb("hn", [P, 2, D])
        w_piece = sb("w_piece", [P, 2, HALF])
        outs = sb("outs", [P, RING, BLK])
        bias = sb("bias", [P, 2, KC])
        v_b = sb("v_b", [P, D])
        ident = sb("ident", [P, P])
        ones = sb("ones", [P, P])
        mhalf = sb("mhalf", [P, 1])
        stats = sb("stats", [P, 2, 6])
        mv = sb("mv", [P, 2, 2])
        rstd = sb("rstd", [P, 2, 1])

        const_in = sem("const_in")
        const_made = sem("const_made")
        wk_in = [sem(f"wk_in{k}") for k in range(KC)]
        w_in = {n: sem(f"w_in{n}") for n in (1, 2)}
        w_high = sem("w_high")
        w_split = sem("w_split")
        c_in = [sem(f"c_in{k}") for k in range(KC)]
        c_high = sem("c_high")
        piece_in = [sem(f"piece_in{s}") for s in range(2)]
        piece_summed = sem("piece_summed")
        sums_done = sem("sums_done")
        c_split = sem("c_split")
        x_in = [sem(f"x_in{j}") for j in range(TPB)]
        got = [sem(f"got{j}") for j in range(TPB)]
        places_ready = sem("places_ready")
        gather_free = sem("gather_free")
        first_added = sem("first_added")
        x2_ready = sem("x2_ready")
        x2_out = [sem(f"x2_out{j}") for j in range(TPB)]
        ln_stats = sem("ln_stats")
        ln_seen = sem("ln_seen")
        ln_mv = sem("ln_mv")
        ln_eps = sem("ln_eps")
        ln_rstd = sem("ln_rstd")
        ln_done = sem("ln_done")
        h_turned = sem("h_turned")
        h_high = sem("h_high")
        h_split = sem("h_split")
        proj_ready = sem("proj_ready")
        kq_taken = sem("kq_taken")
        v_taken = sem("v_taken")
        stored = [sem(f"stored{s}") for s in range(RING)]

        x_t, x2_t = (a.rearrange("(b n p) d -> n b p d", p=P, n=TPB) for a in (x_shared, x2))
        ctx_t = ctxT.rearrange("(k p) (b t) -> k b p t", p=P, t=BLK)
        piece_t = w_ffn.rearrange("g (h k) p n -> h g p k n", h=2)
        k_out, q_out = (a.rearrange("(k p) (b t) -> k b p t", p=P, t=BLK) for a in (kT, qT))
        v_out = v.rearrange("(b n p) d -> n b p d", p=P, n=TPB)

        block = c.enter_context(nc.Block())

        @block.sync
        def _(sp):
            sp.dma_start(bias[:], W["kq_bias"]).then_inc(const_in, 16)
            sp.dma_start(v_b[:], W["bv"].to_broadcast([P, D])).then_inc(const_in, 16)
            for s in range(RING):
                sp.sem_inc(stored[s], 16)

            def load_ctx(b, k):
                sp.dma_start(c_raw[:, k, :], ctx_t[k][b]).then_inc(c_in[k], 16)

            for k in range(KC):
                sp.dma_start(w_raw[:, 0, k], W["wk"].rearrange("(k p) n -> k p n", p=P)[k]).then_inc(wk_in[k], 16)
                load_ctx(0, k)
            for n, name in ((1, "wv"), (2, "wq")):
                sp.dma_start(w_raw[:, n], W[name].rearrange("(k p) n -> p k n", p=P)).then_inc(w_in[n], 16)
            for j in range(TPB):
                sp.dma_start(xr[:, j, :], x_t[j][0]).then_inc(x_in[j], 16)
            with sp.Fori(0, NBLK) as t:
                def load_x(j):
                    sp.wait_ge(ln_done, TPB * t + j + 1)
                    sp.wait_ge(x2_out[j], 16 * t + 16)
                    sp.dma_start(xr[:, j, :], x_t[j][(t + 1) % NBLK]).then_inc(x_in[j], 16)

                def store_x2(j):
                    sp.wait_ge(x2_ready, TPB * t + j + 1)
                    sp.dma_start(x2_t[j][t], xr[:, j, :]).then_inc(x2_out[j], 16)

                def store(i):
                    if KC <= i < 2 * KC:
                        sp.wait_ge(v_taken, KC * t + i - KC + 1)
                    else:
                        sp.wait_ge(kq_taken, KC + 2 * KC * t + (i if i < KC else i - KC) + 1)
                    dst = (k_out, v_out, q_out)[i // KC][i % KC][t]
                    sp.dma_start(dst, outs[:, i % RING, :]).then_inc(stored[i % RING], 16)

                def load_piece(which, half):
                    sp.wait_ge(piece_summed, 4 * t + 2 * which + half + 1)
                    sp.dma_start(w_piece[:, half, :].rearrange("p (k n) -> p k n", n=BLK), piece_t[half][2 * t + which])\
                        .then_inc(piece_in[half], 16)

                for i in range(NO):
                    store(i)
                    if i in (0, 7):
                        load_piece(i // 7, 0)
                        load_piece(i // 7, 1)
                    if i in TURN_AFTER:
                        store_x2(TURN_AFTER[i])
                    if i >= NO - TPB:
                        load_x(i - NO + TPB)
                    if i == 1:
                        for k in range(KC):
                            sp.wait_ge(c_split, KC * t + k + 1)
                            load_ctx((t + 1) % NBLK, k)
            sp.wait_ge(sums_done, 1)
            for s in range(RING):
                sp.wait_ge(stored[s], 16 + 16 * NBLK * (NO // RING))
            for j in range(TPB):
                sp.wait_ge(x2_out[j], 16 * NBLK)
                sp.wait_ge(x_in[j], 16 * (NBLK + 1))
                sp.wait_ge(got[j], 32 * (NBLK + 1))

        @block.gpsimd
        def _(pool):
            pool.memset(ones[:], 1.0).then_inc(const_made, 1)
            pool.memset(mhalf[:], -0.5).then_inc(const_made, 1)
            pool.wait_ge(const_made, 2)
            pool.affine_select(out=ident[:], in_=ones[:], compare_op=ALU.is_equal, fill=0.0, base=0,
                               pattern=[[-1, P]], channel_multiplier=1).then_inc(const_made, 1)

            def c_low(n, k):
                pool.wait_ge(c_high, n + k + 1)
                pool.tensor_tensor(c_hl[:, 1, k, :], c_raw[:, k, :], f32(c_hl[:, 0, k, :]), ALU.subtract)\
                    .then_inc(c_split, 1)

            def gather(n, b):
                pool.tensor_copy(place_now[:], place[:, :, bass.ds(b * TPB, TPB)]).then_inc(places_ready, 1)
                pool.wait_ge(places_ready, n + 1)
                pool.sem_inc(gather_free, 1)
                for j in range(TPB):
                    for r in range(2):
                        pool.indirect_dma_start(routed[:, j, r, :], None, expert_out,
                                                bass.IndirectOffsetOnAxis(ap=place_now[:, r, j:j + 1], axis=0))\
                            .then_inc(got[j], 16)

            for k in range(KC):
                c_low(0, k)
            gather(0, 0)
            with pool.Fori(0, NBLK) as t:
                for j in range(TPB):
                    pool.wait_ge(ln_eps, TPB * t + j + 1)
                    pool.tensor_tensor(rstd[:, j % 2, :], rstd[:, j % 2, :], mhalf[:], ALU.pow).then_inc(ln_rstd, 1)
                pool.wait_ge(x2_ready, TPB * t + TPB)
                for j in range(TPB):
                    pool.wait_ge(got[j], 32 * t + 32)
                pool.sem_inc(gather_free, 1)
                gather(t + 1, (t + 1) % NBLK)
                for k in range(KC):
                    c_low(KC * t + KC, k)

        @block.scalar
        def _(act):
            def c_high_part(loads, k):
                act.wait_ge(c_in[k], 16 * loads)
                act.activation(c_hl[:, 0, k, :], c_raw[:, k, :], ACT.Copy).then_inc(c_high, 1)

            def w_high_part(n, chunks=range(KC)):
                if n:
                    act.wait_ge(w_in[n], 16)
                for k in chunks:
                    if n == 0:
                        act.wait_ge(wk_in[k], 16)
                    act.activation(w_hl[:, n, 0, k, :], w_raw[:, n, k, :], ACT.Copy).then_inc(w_high, 1)

            act.sem_inc(kq_taken, KC)
            act.sem_inc(piece_summed, 2)
            for k in range(KC):
                w_high_part(0, (k,))
                c_high_part(1, k)
            act.wait_ge(const_in, 32)
            w_high_part(1)
            w_high_part(2)
            with act.Fori(0, NBLK) as t:
                def take(i):
                    half = 0 if i < KC else 1
                    act.wait_ge(proj_ready, NO * t + i + 1)
                    act.wait_ge(stored[i % RING], 16 * (NO // RING * t + i // RING + 1))
                    act.activation(outs[:, i % RING, :], proj[:, i % 4, :], ACT.Identity,
                                   bias=bias[:, half, i % KC:i % KC + 1]).then_inc(kq_taken, 1)

                def h_high_part(j):
                    act.wait_ge(h_turned, TPB * t + j + 1)
                    act.activation(a_hl[:, 0, :, j * P:(j + 1) * P],
                                   tr_ps[:, j % 2, :].rearrange("p (k n) -> p k n", k=KC), ACT.Copy)\
                        .then_inc(h_high, 1)

                def sum_pieces(which):
                    for half in range(2):
                        act.wait_ge(piece_in[half], 32 * t + 16 * which + 16)
                        act.activation(w_piece[:, half, :], w_piece[:, half, :], ACT.Abs,
                                       accum_out=sums[:, which, bass.ds(2 * t + half, 1)]).then_inc(piece_summed, 1)

                for i in range(max(TURN_AFTER) + 1):
                    if i < KC:
                        take(i)
                    if i in TURN_AFTER:
                        h_high_part(TURN_AFTER[i])
                sum_pieces(0)
                act.wait_ge(proj_ready, NO * t + 2 * KC)
                for k in range(KC):
                    c_high_part(t + 2, k)
                    if k % 2:
                        take(2 * KC + k // 2)
                take(3 * KC - 2)
                sum_pieces(1)
                take(3 * KC - 1)
            act.wait_ge(piece_summed, 2 + 4 * NBLK)
            act.drain().then_inc(sums_done, 1)

        @block.tensor
        def _(pe):
            pe.wait_ge(const_made, 3)
            with pe.Fori(0, NBLK) as t:
                def project(i):
                    which, j = i // KC, i % KC
                    if i % KC == 0 and i:
                        pe.wait_ge(w_split, KC * (which + 1))
                    if i == 2 * KC:
                        pe.wait_ge(h_split, TPB * t + TPB)
                    if which == 1:
                        pe.wait_ge(kq_taken, KC + 2 * KC * t + j + 1)
                    elif which == 2:
                        pe.wait_ge(v_taken, KC * t + j + 1)
                    else:
                        pe.wait_ge(kq_taken, 2 * KC * t + j + 1)
                    a = a_hl if which == 2 else c_hl
                    own = slice(j * P, (j + 1) * P)
                    for k in range(KC):
                        if i == 0:
                            pe.wait_ge(w_split, k + 1)
                            pe.wait_ge(c_split, KC * t + k + 1)
                        for n, (wp, ap) in enumerate(PASSES):
                            tok, col = a[:, ap, k], w_hl[:, which, wp, k]
                            left, right = (tok[:, own], col) if which == 1 else (col[:, own], tok)
                            mm = pe.matmul(proj[:, j, :], left, right, start=(k == 0 and n == 0),
                                           stop=(k == KC - 1 and n == 2))
                    mm.then_inc(proj_ready, 1)

                def turn_h(j):
                    pe.wait_ge(ln_done, TPB * t + j + 1)
                    if j >= 2:
                        pe.wait_ge(h_split, TPB * t + j - 1)
                    for k in range(KC):
                        mm = pe.transpose(tr_ps[:, j % 2, k * P:(k + 1) * P], hn[:, j % 2, k * P:(k + 1) * P],
                                          ident[:])
                    mm.then_inc(h_turned, 1)

                for i in range(NO):
                    project(i)
                    if i in TURN_AFTER:
                        turn_h(TURN_AFTER[i])

        @block.vector
        def _(dve):
            dve.wait_ge(const_in, 32)
            for n in range(3):
                for k in range(KC):
                    dve.wait_ge(w_high, KC * n + k + 1)
                    dve.tensor_tensor(w_hl[:, n, 1, k, :], w_raw[:, n, k, :], f32(w_hl[:, n, 0, k, :]), ALU.subtract)\
                        .then_inc(w_split, 1)
            with dve.Fori(0, NBLK) as t:
                def normalise_x(j):
                    s = j % 2
                    n = TPB * t + j + 1
                    dve.wait_ge(x_in[j], 16 * t + 16)
                    dve.wait_ge(got[j], 32 * t + 32)
                    dve.scalar_tensor_tensor(xr[:, j, :], routed[:, j, 0, :], weight[:, 0, bass.ds(TPB * t + j, 1)],
                                             xr[:, j, :], ALU.mult, ALU.add).then_inc(first_added, 1)
                    dve.wait_ge(first_added, n)
                    dve.scalar_tensor_tensor(xr[:, j, :], routed[:, j, 1, :], weight[:, 1, bass.ds(TPB * t + j, 1)],
                                             xr[:, j, :], ALU.mult, ALU.add).then_inc(x2_ready, 1)
                    dve.wait_ge(x2_ready, n)
                    dve.bn_stats(stats[:, s, :], xr[:, j, :]).then_inc(ln_stats, 1)
                    dve.wait_ge(ln_stats, n)
                    dve.sem_inc(ln_seen, 1)
                    dve.bn_aggr(mv[:, s, :], stats[:, s, :]).then_inc(ln_mv, 1)
                    dve.wait_ge(ln_mv, n)
                    dve.tensor_scalar(rstd[:, s, :], mv[:, s, 1:2], LN_EPS, None, ALU.add).then_inc(ln_eps, 1)
                    dve.wait_ge(ln_rstd, n)
                    if j >= 2:
                        dve.wait_ge(h_turned, TPB * t + j - 1)
                    dve.tensor_scalar(hn[:, s, :], xr[:, j, :], mv[:, s, 0:1], rstd[:, s, :],
                                      ALU.subtract, ALU.mult).then_inc(ln_done, 1)

                def take_v(j):
                    i = KC + j
                    dve.wait_ge(proj_ready, NO * t + i + 1)
                    dve.wait_ge(stored[i % RING], 16 * (NO // RING * t + i // RING + 1))
                    dve.tensor_tensor(outs[:, i % RING, :], proj[:, j, :], v_b[:], ALU.add).then_inc(v_taken, 1)

                def h_low_part(j):
                    own = slice(j * P, (j + 1) * P)
                    dve.wait_ge(h_high, TPB * t + j + 1)
                    dve.tensor_tensor(a_hl[:, 1, :, own], tr_ps[:, j % 2, :].rearrange("p (k n) -> p k n", k=KC),
                                      f32(a_hl[:, 0, :, own]), ALU.subtract).then_inc(h_split, 1)

                for j in range(TPB):
                    normalise_x(j)
                    if j >= 1:
                        h_low_part(j - 1)
                take_v(0)
                h_low_part(TPB - 1)
                for j in range(1, KC):
                    take_v(j)


def l1_attention(nc, new_sem, qT, kT, v, aT, w_ffn, sums, w_t):
    D, T = qT.shape
    HD = 32
    H = D // HD
    NBLK = T // BLK
    NQ = P // HD
    TQ = BLK // NQ
    TOK = P // H
    UN = 4
    NJ = TQ // TOK // UN
    NU = NJ * NQ
    NV = BLK // TOK
    TURN_LAG, AV_LAG = 3, 4
    BIG = 1e30
    NW, KC = w_ffn.shape[0:2]
    HALF = KC // 2 * BLK
    PPB = NU // 2
    assert PPB * (NBLK // 2) == 2 * NW

    with ExitStack() as c:
        def sb(name, shape, dt=F32):
            return c.enter_context(nc.sbuf_tensor("t_" + name, shape, dt))

        def sem(name):
            return new_sem("t_" + name)

        def psum(name, shape):
            return c.enter_context(nc.psum_tensor("t_" + name, shape, F32))

        sc_ps = psum("scores", [P, 2, UN, P])
        tr_ps = psum("turned", [P, 2, UN, P])
        av_ps = psum("out", [P, 2, UN, P])
        q_sb = sb("q", [P, H, TQ])
        q_laid = sb("q_laid", [P, 2, NJ * UN, H, TOK])
        k_sb = sb("k", [P, 2, H, TQ])
        v_sb = sb("v", [P, 2, NV, HD])
        o_sb = sb("o", [P, 2, H, TQ])
        probs = sb("probs", [P, 4, UN, P])
        mask = sb("mask", [P, H, TOK])
        diff = sb("diff", [P, TOK], mybir.dt.int32)
        same = sb("same", [P, TOK], mybir.dt.int32)
        flag = sb("flag", [P, 1, TOK])
        ident = sb("ident", [P, P])
        ones = sb("ones", [P, P])
        mx = sb("mx", [P, 4, UN])
        den = sb("den", [P, 4, UN])
        rden = sb("rden", [P, 4, UN])

        m_ps = psum("means", [P, 2])
        w_raw = sb("w_raw", [P, 2, HALF])
        w_neg = sb("w_neg", [P, HALF])
        sum2 = sb("sum2", [P, 2])
        mean = sb("mean", [P, 2])
        thr = sb("thr", [P, 2, 2])

        const_made = sem("const_made")
        mean_ready = sem("mean_ready")
        thr_step = sem("thr_step")
        w_in = [sem(f"w_in{s}") for s in range(2)]
        w_neg_ready = sem("w_neg_ready")
        w_used = sem("w_used")
        masked = sem("masked")
        q_in = sem("q_in")
        k_in = [sem(f"k_in{s}") for s in range(2)]
        q_moved = sem("q_moved")
        v_in = [sem(f"v_in{s}") for s in range(2)]
        s_ready = sem("s_ready")
        s_masked = sem("s_masked")
        s_max = sem("s_max")
        s_sub = sem("s_sub")
        e_ready = sem("e_ready")
        e_sum = sem("e_sum")
        e_rec = sem("e_rec")
        p_ready = sem("p_ready")
        pt_ready = sem("pt_ready")
        pt_copied = sem("pt_copied")
        av_ready = sem("av_ready")
        o_copied = sem("o_copied")
        o_out = [sem(f"o_out{s}") for s in range(2)]

        def by_quadrant(a):
            return a.rearrange("(h d) (b q t) -> q b d h t", d=HD, q=NQ, t=TQ)

        q_src, k_src, a_out = by_quadrant(qT), by_quadrant(kT), by_quadrant(aT)
        v_src = v.rearrange("(b n t) (h d) -> h b t n d", t=TOK, n=NV, d=HD)
        IN_QK, IN_V = NQ * 16, H * 16

        piece_t = w_ffn.rearrange("g (h k) p n -> h g p k n", h=2)

        block = c.enter_context(nc.Block())

        def load(eng, n, b, s):
            eng.wait_ge(q_moved, n + 1)
            for q in range(NQ):
                rows = slice(q * HD, (q + 1) * HD)
                eng.dma_start(q_sb[rows], q_src[q][b]).then_inc(q_in, 16)
                eng.dma_start(k_sb[rows, s], k_src[q][b]).then_inc(k_in[s], 16)
            for h in range(H):
                eng.dma_start(v_sb[h * TOK:(h + 1) * TOK, s], v_src[h][b]).then_inc(v_in[s], 16)

        @block.sync
        def _(sp):
            for s in range(2):
                sp.sem_inc(o_out[s], 16 * NQ)
            sp.sem_inc(q_moved, 1)
            load(sp, 0, 0, 0)
            with sp.Fori(0, NBLK // 2) as t:
                def store(s, blocks, b):
                    sp.wait_ge(o_copied, 2 + NJ * blocks)
                    for q in range(NQ):
                        rows = slice(q * HD, (q + 1) * HD)
                        sp.dma_start(a_out[q][b], o_sb[rows, s]).then_inc(o_out[s], 16)

                load(sp, 2 * t + 1, 2 * t + 1, 1)
                store(0, 2 * t + 1, 2 * t)
                load(sp, 2 * t + 2, (2 * t + 2) % NBLK, 0)
                store(1, 2 * t + 2, 2 * t + 1)
            for s in range(2):
                sp.wait_ge(o_out[s], 16 * NQ * (NBLK // 2 + 1))
            sp.wait_ge(q_in, IN_QK * (NBLK + 1))
            sp.wait_ge(k_in[0], IN_QK * (NBLK // 2 + 1))
            sp.wait_ge(v_in[0], IN_V * (NBLK // 2 + 1))

        @block.gpsimd
        def _(pool):
            pool.memset(ones[:], 1.0).then_inc(const_made, 1)
            pool.iota(diff[:], pattern=[[-1, TOK]], base=TOK, channel_multiplier=1).then_inc(const_made, 1)
            pool.wait_ge(const_made, 2)
            pool.affine_select(out=ident[:], in_=ones[:], compare_op=ALU.is_equal, fill=0.0, base=0,
                               pattern=[[-1, P]], channel_multiplier=1).then_inc(const_made, 1)
            with pool.Fori(0, NBLK // 2) as t:
                for u in range(2 * NU):
                    pool.wait_ge(e_rec, 2 * NU * t + u + 1)
                    pool.tensor_tensor(probs[:, u % 4], probs[:, u % 4],
                                       rden[:, u % 4].unsqueeze(2).to_broadcast([P, UN, P]), ALU.mult)\
                        .then_inc(p_ready, 1)

        @block.scalar
        def _(act):
            act.sem_inc(o_copied, 2)
            act.sem_inc(av_ready, 4)
            act.sem_inc(w_used, 2)
            with act.Fori(0, NBLK // 2) as t:
                def move_queries(s):
                    act.wait_ge(q_in, IN_QK * (2 * t + s + 1))
                    act.activation(q_laid[:, s], q_sb[:].rearrange("p h (n t) -> p n h t", t=TOK), ACT.Copy)\
                        .then_inc(q_moved, 1)

                move_queries(0)
                for u in range(2 * NU + AV_LAG):
                    if u == NU - 4:
                        move_queries(1)
                    if u % 4 == 0 and u < 2 * NU:
                        m = u // 4
                        act.wait_ge(w_used, PPB * t + m + 1)
                        act.dma_start(w_raw[:, m % 2, :].rearrange("p (k n) -> p k n", n=BLK),
                                      piece_t[m % 2][PPB // 2 * t + m // 2]).then_inc(w_in[m % 2], 16)
                    if TURN_LAG <= u < 2 * NU + TURN_LAG:
                        m = u - TURN_LAG
                        act.wait_ge(pt_ready, 2 * NU * t + m + 1)
                        act.activation(probs[:, m % 4], tr_ps[:, m % 2], ACT.Copy).then_inc(pt_copied, 1)
                    if u < 2 * NU:
                        act.wait_ge(s_sub, 2 * NU * t + u + 1)
                        act.activation(probs[:, u % 4], probs[:, u % 4], ACT.Exp).then_inc(e_ready, 1)
                    m = u - AV_LAG
                    if m >= 0 and m % NQ == NQ - 1:
                        n, s = m // NQ, m // NU
                        jj = n % NJ
                        if jj == 0:
                            act.wait_ge(o_out[s], 16 * NQ * (t + 1))
                        act.wait_ge(av_ready, 4 + 2 * NU * t + m + 1)
                        dst = o_sb[:, s, :, jj * UN * TOK:(jj + 1) * UN * TOK].rearrange("p h (y t) -> p y h t", t=TOK)
                        src = av_ps[:, n % 2].rearrange("p y (h t) -> p y h t", t=TOK)
                        act.activation(dst, src, ACT.Copy).then_inc(o_copied, 1)

        @block.tensor
        def _(pe):
            pe.wait_ge(const_made, 3)
            pe.wait_ge(thr_step, 1)
            pe.matmul(m_ps[:], ones[:], sum2[:], start=True, stop=True).then_inc(mean_ready, 1)
            with pe.Fori(0, NBLK // 2) as t:
                def place(u):
                    return u // NU, u % NU // NQ, u % NQ

                def scores(u):
                    s, jj, q = place(u)
                    if u % NU == 0:
                        pe.wait_ge(k_in[s], IN_QK * (t + 1))
                        pe.wait_ge(q_moved, 1 + 2 * t + s + 1)
                    pe.wait_ge(s_masked, 2 * NU * t + u + 1)
                    rows = slice(q * HD, (q + 1) * HD)
                    for y in range(UN):
                        toks = slice((jj * UN + y) * TOK, (jj * UN + y + 1) * TOK)
                        mm = pe.matmul(sc_ps[:, u % 2, y, :], q_laid[rows, s, jj * UN + y].rearrange("p h t -> p (h t)"),
                                       k_sb[rows, s, :, toks],
                                       start=True, stop=True)
                    mm.then_inc(s_ready, 1)

                def turn(u):
                    pe.wait_ge(p_ready, 2 * NU * t + u + 1)
                    if u >= 2:
                        pe.wait_ge(pt_copied, 2 * NU * t + u - 1)
                    for y in range(UN):
                        mm = pe.transpose(tr_ps[:, u % 2, y, :], probs[:, u % 4, y, :], ident[:])
                    mm.then_inc(pt_ready, 1)

                def weigh(u):
                    s, jj, q = place(u)
                    n = u // NQ
                    if u % NU == 0:
                        pe.wait_ge(v_in[s], IN_V * (t + 1))
                    pe.wait_ge(pt_copied, 2 * NU * t + u + 1)
                    if q == 0:
                        pe.wait_ge(o_copied, 2 * NJ * t + n + 1)
                    for y in range(UN):
                        mm = pe.matmul(av_ps[q * HD:(q + 1) * HD, n % 2, y, :],
                                       v_sb[:, s, (q * NJ + jj) * UN + y, :], probs[:, u % 4, y, :],
                                       start=True, stop=True)
                    mm.then_inc(av_ready, 1)

                for u in range(2 * NU + AV_LAG):
                    if u < 2 * NU:
                        scores(u)
                    if TURN_LAG <= u < 2 * NU + TURN_LAG:
                        turn(u - TURN_LAG)
                    if u >= AV_LAG:
                        weigh(u - AV_LAG)

        @block.vector
        def _(dve):
            dve.wait_ge(const_made, 2)
            dve.tensor_scalar(same[:], diff[:], TOK - 1, None, ALU.bitwise_and).then_inc(masked, 1)
            dve.wait_ge(masked, 1)
            dve.tensor_scalar(flag[:, 0, :], same[:], 0.0, None, ALU.is_equal).then_inc(masked, 1)
            dve.wait_ge(masked, 2)
            dve.tensor_scalar(mask[:], flag[:].to_broadcast([P, H, TOK]), 1.0, BIG, ALU.subtract, ALU.mult)\
                .then_inc(masked, 1)
            dve.wait_ge(masked, 3)
            dve.tensor_reduce(sum2[:], sums[:], AX.X, ALU.add).then_inc(thr_step, 1)
            dve.wait_ge(mean_ready, 1)
            dve.tensor_scalar(mean[:], m_ps[:], 1.0 / (NW // 2 * KC * P * BLK), 1e-8, ALU.mult, ALU.max)\
                .then_inc(thr_step, 1)
            dve.wait_ge(thr_step, 2)
            dve.tensor_scalar(thr[:, :, 0], mean[:], 0.5, None, ALU.mult).then_inc(thr_step, 1)
            dve.tensor_scalar(thr[:, :, 1], mean[:], -0.5, None, ALU.mult).then_inc(thr_step, 1)
            dve.wait_ge(thr_step, 4)
            dve.sem_inc(s_masked, 2)
            with dve.Fori(0, NBLK // 2) as t:
                def round_piece(m):
                    which, raw = m // 2 % 2, w_raw[:, m % 2, :]
                    dst = w_t[:, bass.ds(PPB // 2 * t + m // 2, 1), m % 2 * (KC // 2):(m % 2 + 1) * (KC // 2), :]
                    dve.wait_ge(w_in[m % 2], 16 * (PPB // 2 * t + m // 2 + 1))
                    dve.wait_ge(w_used, PPB * t + m + 2)
                    dve.tensor_scalar(w_neg[:], raw, thr[:, which, 1:2], None, ALU.is_lt).then_inc(w_neg_ready, 1)
                    dve.wait_ge(w_neg_ready, PPB * t + m + 1)
                    dve.scalar_tensor_tensor(dst.rearrange("p g k n -> p (g k n)"), raw, thr[:, which, 0:1], w_neg[:],
                                             ALU.is_gt, ALU.subtract).then_inc(w_used, 1)

                for u in range(2 * NU + 1):
                    n = 2 * NU * t + u + 1
                    r = u % 4
                    if u < 2 * NU:
                        dve.wait_ge(s_ready, n)
                        dve.wait_ge(av_ready, n)
                        dve.tensor_tensor(probs[:, r], sc_ps[:, u % 2],
                                          mask[:].rearrange("p h t -> p (h t)").unsqueeze(1)
                                          .to_broadcast([P, UN, P]), ALU.add).then_inc(s_masked, 1)
                        dve.wait_ge(s_masked, n + 2)
                        dve.tensor_reduce(mx[:, r], probs[:, r], AX.X, ALU.max).then_inc(s_max, 1)
                        dve.wait_ge(s_max, n)
                        dve.tensor_tensor(probs[:, r], probs[:, r], mx[:, r].unsqueeze(2).to_broadcast([P, UN, P]),
                                          ALU.subtract).then_inc(s_sub, 1)
                    if u >= 1:
                        r = (u - 1) % 4
                        dve.wait_ge(e_ready, n - 1)
                        dve.tensor_reduce(den[:, r], probs[:, r], AX.X, ALU.add).then_inc(e_sum, 1)
                        dve.wait_ge(e_sum, n - 1)
                        dve.reciprocal(rden[:, r], den[:, r]).then_inc(e_rec, 1)
                    if u % 4 == 3:
                        round_piece(u // 4)


def l1_output_ffn(nc, new_sem, x2, aT, W, w_t, out):
    T, D = x2.shape
    KC = D // P
    NT = T // P
    NBLK = T // BLK
    NG = w_t.shape[1] // 2
    F = NG * BLK
    RING = 4
    FC = BLK // P
    PASSES2 = (0, 1)

    with ExitStack() as c:
        def sb(name, shape, dt=F32):
            return c.enter_context(nc.sbuf_tensor("f_" + name, shape, dt))

        def sem(name):
            return new_sem("f_" + name)

        def psum(name, shape):
            return c.enter_context(nc.psum_tensor("f_" + name, shape, F32))

        h_ps = psum("hidden", [P, 2, BLK])
        y_ps = psum("totals", [P, TPB, BLK])

        h_hl = sb("h_hl", [P, 2, KC, T], F32R)
        y = sb("y", [P, NT, D])
        a_raw = sb("a_raw", [P, RING, BLK])
        a_hl = sb("a_hl", [P, 2, KC, BLK], F32R)
        act_sb = sb("act_sb", [P, 2, BLK])
        hs = sb("hs", [P, 2, D])
        ident = sb("ident", [P, P])
        ones = sb("ones", [P, P])
        mhalf = sb("mhalf", [P, 1])
        tg_bo = sb("tg_bo", [P, D])
        tg_b2 = sb("tg_b2", [P, D])
        b1 = sb("b1", [P, F // P])
        gates = sb("gates", [P, 2])
        tgs = sb("tgs", [P, 2])
        stats = sb("stats", [P, 2, 6])
        mv = sb("mv", [P, 2, 2])
        rstd = sb("rstd", [P, 2, 1])

        gates_in = sem("gates_in")
        const_in = sem("const_in")
        const_made = sem("const_made")
        tg_ready = sem("tg_ready")
        const_done = sem("const_done")
        x_in = [sem(f"x_in{n}") for n in range(NBLK)]
        wo_in = [sem(f"wo_in{s}") for s in range(2)]
        wo_high = sem("wo_high")
        wo_split = sem("wo_split")
        bo_added = sem("bo_added")
        a_in = [sem(f"a_in{s}") for s in range(RING)]
        a_high = sem("a_high")
        a_split = sem("a_split")
        o_ready = sem("o_ready")
        o_added = sem("o_added")
        ln_stats = sem("ln_stats")
        ln_mv = sem("ln_mv")
        ln_eps = sem("ln_eps")
        ln_rstd = sem("ln_rstd")
        ln_done = sem("ln_done")
        h_turned = sem("h_turned")
        h_high = sem("h_high")
        h_split = sem("h_split")
        hid_ready = sem("hid_ready")
        gelu_ready = sem("gelu_ready")
        g_high = sem("g_high")
        g_split = sem("g_split")
        y_ready = sem("y_ready")
        y_added = sem("y_added")
        y_done = sem("y_done")
        x_out = sem("x_out")

        x2_t = x2.rearrange("(b n p) d -> b p n d", p=P, n=TPB)
        out_t = out.rearrange("(b n p) d -> n b p d", p=P, n=TPB)
        a_t = aT.rearrange("(k p) (b t) -> k b p t", p=P, t=BLK)
        wo_t = W["woT"].rearrange("(k p) (c n) -> k c p n", p=P, n=BLK)

        def chunks_beside(n):
            return range(KC + 2 * n, min(KC * NBLK, KC + 2 * n + 2))

        block = c.enter_context(nc.Block())

        @block.sync
        def _(sp):
            sp.dma_start(gates[:], W["gates"].to_broadcast([P, 2])).then_inc(gates_in, 16)
            def load_chunk(n):
                if n >= RING:
                    sp.wait_ge(a_split, n - RING + 1)
                sp.dma_start(a_raw[:, n % RING, :], a_t[n % KC][n // KC]).then_inc(a_in[n % RING], 16)

            for k in range(KC):
                load_chunk(k)
                if k >= 2:
                    sp.wait_ge(wo_split, k - 1)
                sp.dma_start(act_sb[:, k % 2, :], wo_t[k][0]).then_inc(wo_in[k % 2], 16)
            sp.dma_start(tg_bo[:], W["bo"].to_broadcast([P, D])).then_inc(const_in, 16)
            sp.dma_start(y[:, 0:TPB, :], x2_t[0]).then_inc(x_in[0], 16)
            sp.dma_start(tg_b2[:], W["b2"].to_broadcast([P, D])).then_inc(const_in, 16)
            sp.dma_start(b1[:], W["b1"]).then_inc(const_in, 16)
            for b in range(1, NBLK):
                sp.dma_start(y[:, b * TPB:(b + 1) * TPB, :], x2_t[b]).then_inc(x_in[b], 16)
                for k in range(KC):
                    load_chunk(KC * b + k)
            with sp.Fori(0, NBLK) as t:
                for j in range(TPB):
                    sp.wait_ge(y_done, TPB * t + j + 1)
                    sp.dma_start(out_t[j][t], y[:, bass.ds(TPB * t + j, 1), :]).then_inc(x_out, 16)
            sp.wait_ge(x_out, 16 * NT)

        @block.gpsimd
        def _(pool):
            pool.memset(ones[:], 1.0).then_inc(const_made, 1)
            pool.memset(mhalf[:], -0.5).then_inc(const_made, 1)
            pool.wait_ge(const_made, 2)
            pool.affine_select(out=ident[:], in_=ones[:], compare_op=ALU.is_equal, fill=0.0, base=0,
                               pattern=[[-1, P]], channel_multiplier=1).then_inc(const_made, 1)
            pool.sem_inc(g_split, 2)
            pool.sem_inc(gelu_ready, 2)

            def a_low(n):
                own = slice(n // KC * BLK, (n // KC + 1) * BLK)
                pool.wait_ge(a_high, n + 1)
                pool.tensor_tensor(h_hl[:, 1, n % KC, own], a_raw[:, n % RING, :], f32(h_hl[:, 0, n % KC, own]),
                                   ALU.subtract).then_inc(a_split, 1)

            def add_bias(n):
                pool.wait_ge(x_in[n // TPB], 16)
                pool.tensor_tensor(y[:, n, :], y[:, n, :], tg_bo[:], ALU.add).then_inc(bo_added, 1)

            for n in range(KC):
                a_low(n)
            pool.wait_ge(const_done, 2)
            add_bias(0)
            add_bias(1)
            for n in range(NT):
                pool.wait_ge(ln_eps, n + 1)
                pool.tensor_tensor(rstd[:, n % 2, :], rstd[:, n % 2, :], mhalf[:], ALU.pow).then_inc(ln_rstd, 1)
                if n + 2 < NT:
                    add_bias(n + 2)
                for m in chunks_beside(n):
                    a_low(m)
            with pool.Fori(0, NBLK) as t:
                for m in range(NG * FC):
                    pool.wait_ge(g_high, NG * FC * t + m + 1)
                    pool.tensor_tensor(a_hl[:, 1, m % FC, :], act_sb[:, m % 2, :], f32(a_hl[:, 0, m % FC, :]),
                                       ALU.subtract).then_inc(g_split, 1)

        @block.scalar
        def _(act):
            act.wait_ge(gates_in, 16)
            act.activation(tgs[:], gates[:], ACT.Tanh).then_inc(tg_ready, 1)

            def a_high_part(n):
                own = slice(n // KC * BLK, (n // KC + 1) * BLK)
                act.wait_ge(a_in[n % RING], 16 * (n // RING + 1))
                act.activation(h_hl[:, 0, n % KC, own], a_raw[:, n % RING, :], ACT.Copy).then_inc(a_high, 1)

            for k in range(KC):
                a_high_part(k)
                act.wait_ge(wo_in[k % 2], 16 * (k // 2 + 1))
                act.activation(a_hl[:, 0, k, :], act_sb[:, k % 2, :], ACT.Copy).then_inc(wo_high, 1)
            for n in range(NT):
                act.wait_ge(h_turned, n + 1)
                act.activation(h_hl[:, 0, :, n * P:(n + 1) * P],
                               y_ps[:, 2 + n % 2, :].rearrange("p (k n) -> p k n", k=KC), ACT.Copy).then_inc(h_high, 1)
                for m in chunks_beside(n):
                    a_high_part(m)
            act.wait_ge(const_in, 48)
            with act.Fori(0, NBLK) as t:
                for m in range(NG * FC):
                    n = NG * FC * t + m
                    act.wait_ge(hid_ready, n + 1)
                    act.wait_ge(g_split, n + 1)
                    act.activation(act_sb[:, m % 2, :], h_ps[:, m % 2, :], ACT.Gelu, bias=b1[:, m:m + 1])\
                        .then_inc(gelu_ready, 1)
                    act.wait_ge(gelu_ready, n + 1 + 2)
                    act.activation(a_hl[:, 0, m % FC, :], act_sb[:, m % 2, :], ACT.Copy).then_inc(g_high, 1)

        @block.tensor
        def _(pe):
            pe.wait_ge(const_made, 3)

            def project_out(n):
                if n:
                    pe.wait_ge(a_split, KC * (n // TPB + 1))
                if n >= 2:
                    pe.wait_ge(o_added, n - 1)
                own = slice(n * P, (n + 1) * P)
                for k in range(KC):
                    if n == 0:
                        pe.wait_ge(wo_split, k + 1)
                        pe.wait_ge(a_split, k + 1)
                    for m, (wp, ap) in enumerate(PASSES):
                        mm = pe.matmul(y_ps[:, n % 2, :], h_hl[:, ap, k, own], a_hl[:, wp, k, :],
                                       start=(k == 0 and m == 0), stop=(k == KC - 1 and m == 2))
                mm.then_inc(o_ready, 1)

            def turn(n):
                pe.wait_ge(ln_done, n + 1)
                if n >= 2:
                    pe.wait_ge(h_split, n - 1)
                for k in range(KC):
                    mm = pe.transpose(y_ps[:, 2 + n % 2, k * P:(k + 1) * P], hs[:, n % 2, k * P:(k + 1) * P], ident[:])
                mm.then_inc(h_turned, 1)

            for n in range(NT + 2):
                if n < NT:
                    project_out(n)
                if n >= 2:
                    turn(n - 2)
            with pe.Fori(0, NBLK) as t:
                def hidden(m):
                    g, f = m // FC, m % FC
                    if m == 0:
                        pe.wait_ge(h_split, TPB * t + TPB)
                    pe.wait_ge(gelu_ready, NG * FC * t + m + 1)
                    for k in range(KC):
                        for ap in PASSES2:
                            mm = pe.matmul(h_ps[:, m % 2, :], w_t[:, 2 * g, k, f * P:(f + 1) * P],
                                           h_hl[:, ap, k, bass.ds(BLK * t, BLK)],
                                           start=(k == 0 and ap == 0), stop=(k == KC - 1 and ap == 1))
                    mm.then_inc(hid_ready, 1)

                def down(m):
                    g, f = m // FC, m % FC
                    pe.wait_ge(g_split, 2 + NG * FC * t + m + 1)
                    for j in range(TPB):
                        if m == 0:
                            pe.wait_ge(y_added, TPB * t + j + 1)
                        for ap in PASSES2:
                            mm = pe.matmul(y_ps[:, j, :], a_hl[:, ap, f, j * P:(j + 1) * P], w_t[:, 2 * g + 1, f, :],
                                           start=(m == 0 and ap == 0), stop=(m == NG * FC - 1 and ap == 1))
                        if m == NG * FC - 1:
                            mm.then_inc(y_ready, 1)

                for g in range(NG):
                    for f in range(FC):
                        hidden(FC * g + f)
                    for f in range(FC):
                        down(FC * g + f)

        @block.vector
        def _(dve):
            for k in range(KC):
                dve.wait_ge(wo_high, k + 1)
                dve.tensor_tensor(a_hl[:, 1, k, :], act_sb[:, k % 2, :], f32(a_hl[:, 0, k, :]), ALU.subtract)\
                    .then_inc(wo_split, 1)
            dve.wait_ge(const_in, 48)
            dve.wait_ge(tg_ready, 1)
            dve.tensor_scalar(tg_bo[:], tg_bo[:], tgs[:, 0:1], None, ALU.mult).then_inc(const_done, 1)
            dve.tensor_scalar(tg_b2[:], tg_b2[:], tgs[:, 1:2], None, ALU.mult).then_inc(const_done, 1)

            def add_output(n):
                s = n % 2
                dve.wait_ge(bo_added, n + 1)
                dve.wait_ge(o_ready, n + 1)
                dve.scalar_tensor_tensor(y[:, n, :], y_ps[:, s, :], tgs[:, 0:1], y[:, n, :], ALU.mult, ALU.add)\
                    .then_inc(o_added, 1)
                dve.wait_ge(o_added, n + 1)
                dve.bn_stats(stats[:, s, :], y[:, n, :]).then_inc(ln_stats, 1)
                dve.wait_ge(ln_stats, n + 1)
                dve.bn_aggr(mv[:, s, :], stats[:, s, :]).then_inc(ln_mv, 1)
                dve.wait_ge(ln_mv, n + 1)
                dve.tensor_scalar(rstd[:, s, :], mv[:, s, 1:2], LN_EPS, None, ALU.add).then_inc(ln_eps, 1)

            def normalise(n):
                s = n % 2
                dve.wait_ge(ln_rstd, n + 1)
                if n >= 2:
                    dve.wait_ge(h_turned, n - 1)
                dve.tensor_scalar(hs[:, s, :], y[:, n, :], mv[:, s, 0:1], rstd[:, s, :], ALU.subtract, ALU.mult)\
                    .then_inc(ln_done, 1)

            def h_low_part(n):
                own = slice(n * P, (n + 1) * P)
                dve.wait_ge(h_high, n + 1)
                dve.tensor_tensor(h_hl[:, 1, :, own], y_ps[:, 2 + n % 2, :].rearrange("p (k n) -> p k n", k=KC),
                                  f32(h_hl[:, 0, :, own]), ALU.subtract).then_inc(h_split, 1)

            for n in range(NT + 2):
                if n < NT:
                    add_output(n)
                if n >= 2:
                    h_low_part(n - 2)
                if n < NT:
                    normalise(n)

            dve.wait_ge(h_split, NT)
            dve.sem_inc(y_added, TPB)
            with dve.Fori(0, NBLK) as t:
                for j in range(TPB):
                    tile = y[:, bass.ds(TPB * t + j, 1), :].rearrange("p a d -> p (a d)")
                    dve.wait_ge(y_ready, TPB * t + j + 1)
                    dve.scalar_tensor_tensor(tile, y_ps[:, j, :], tgs[:, 1:2], tile, ALU.mult, ALU.add)\
                        .then_inc(y_added, 1)
                    dve.wait_ge(y_added, TPB * t + TPB + j + 1)
                    dve.tensor_tensor(tile, tile, tg_b2[:], ALU.add).then_inc(y_done, 1)


def build(nc, a, out):
    T, D = a["x"].shape

    def scratch(name, shape, dt=F32):
        return nc.dram_tensor(name, shape, dt, kind="Internal").ap()

    x1, x_shared, x2, v = (scratch(n, [T, D]) for n in ("x1", "x_shared", "x2", "l1_v"))
    qT, kT, aT = (scratch(n, [D, T]) for n in ("l1_qT", "l1_kT", "l1_aT"))

    slots = most_groups(T, a["b_router"].shape[1]) * BLK
    rows, expert_out = scratch("l0_rows", [T, D]), scratch("l0_expert_out", [slots, D])
    slot_token = scratch("l0_slot_token", [slots, 1], I32)

    def part(prefix):
        return {k[len(prefix):]: ap for k, ap in a.items() if k.startswith(prefix)}

    last = [ExitStack()]

    def stage(run, *args):
        sems, own = ExitStack(), []

        def new_sem(name):
            own.append(sems.enter_context(nc.semaphore(name)))
            return own[-1]

        run(nc, new_sem, *args)
        nc.all_engine_barrier()
        for s in own:
            nc.gpsimd.sem_clear(s)
        last[0].close()
        last[0] = sems

    stage(l0_attention, a["x"], a["ctxT"], part("a_"), x1)
    with nc.sbuf_tensor("place", [P, 2, T // P], I32) as place, \
            nc.sbuf_tensor("weight", [P, 2, T // P], F32) as weight:
        stage(l0_experts, x1, part("b_"), x_shared, rows, slot_token, expert_out, place, weight)
        with nc.sbuf_tensor("magnitudes", [P, 2, a["w_ffn"].shape[0]], F32) as sums:
            stage(l1_projections, x_shared, expert_out, place, weight, a["ctxT"], part("c_"), a["w_ffn"], x2, qT, kT, v,
                  sums)
            with nc.sbuf_tensor("ternary", [P, *[a["w_ffn"].shape[n] for n in (0, 1, 3)]], F32R) as w_t:
                stage(l1_attention, qT, kT, v, aT, a["w_ffn"], sums, w_t)
                stage(l1_output_ffn, x2, aT, part("d_"), w_t, out)
    last[0].close()


def lay_out(i):
    import numpy as np

    def chunks(a):
        return a.reshape(-1, P).T

    B, S, D = i["x"].shape
    F = i["L0_ffn_down_weights"].shape[2]
    x = i["x"].reshape(B * S, D)
    ctx = i["ctx_2048"].reshape(B * S, D)
    shared_gu = i["L0_ffn_shared_gate_up"]
    halves = shared_gu.reshape(2, -1, F, D).transpose(1, 0, 2, 3).reshape(-1, 2 * F, D)
    g_x, g_f = i["g_xattn"], i["g_ffn"]
    w1 = i["L1_ffn_w1"].T.reshape(D // P, P, -1, BLK).transpose(2, 0, 1, 3)
    w2 = i["L1_ffn_w2"].T.reshape(-1, BLK // P, P, D)
    a = {
        "x": x, "ctxT": ctx.T,
        "a_ki_w": i["L0_xattn_ki_w"], "a_vi_w": i["L0_xattn_vi_w"], "a_q_w": i["L0_xattn_q_w"],
        "a_o_w": i["L0_xattn_o_w"], "a_o_b": i["L0_xattn_o_b"][None], "a_gate": g_x[None, 0:1],
        "a_vecs": np.stack([chunks(i["L0_xattn_" + n]) for n in ("q_b", "ki_b", "vi_b", "nki_s", "nq_s")], 1),
        "b_gate_up": np.concatenate([i["L0_ffn_gate_up_weights"], halves]).transpose(0, 2, 1),
        "b_down": np.concatenate([i["L0_ffn_down_weights"].transpose(0, 2, 1),
                                  i["L0_ffn_shared_down"].T.reshape(-1, F, D)]),
        "b_router": i["L0_ffn_gate_weight"].T, "b_gate": g_f[None, 0:1],
        "c_wk": i["L1_xattn_Wk"].T, "c_wv": i["L1_xattn_Wv"].T, "c_wq": i["L1_xattn_Wq"].T,
        "c_kq_bias": np.stack([chunks(i["L1_xattn_bk"]), chunks(i["L1_xattn_bq"])], 1),
        "c_bv": i["L1_xattn_bv"][None],
        "d_woT": i["L1_xattn_Wo"].T, "d_bo": i["L1_xattn_bo"][None],
        "w_ffn": np.stack([w1, w2], 1).reshape(-1, BLK // P, P, BLK), "d_b1": chunks(i["L1_ffn_b1"]),
        "d_b2": i["L1_ffn_b2"][None],
        "d_gates": np.concatenate([g_x[1:2], g_f[1:2]])[None],
    }
    return {k: np.ascontiguousarray(v) for k, v in a.items()}


def kernel(**inputs):
    import numpy as np
    import concourse.bacc as bacc
    from concourse.bass_utils import run_bass_kernel_spmd

    nc = bacc.Bacc("TRN2", target_bir_lowering=False, num_devices=1)
    arrays = lay_out({k: np.asarray(v) for k, v in inputs.items()})
    aps = {k: nc.dram_tensor("in_" + k, v.shape, mybir.dt.from_np(v.dtype), kind="ExternalInput").ap()
           for k, v in arrays.items()}
    shape = inputs["x"].shape
    out = nc.dram_tensor("out", shape, F32, kind="ExternalOutput").ap()
    build(nc, aps, out.rearrange("b s d -> (b s) d"))
    r = run_bass_kernel_spmd(nc, [{"in_" + k: v for k, v in arrays.items()}], core_ids=[0])
    return r.results[0]["out"]
```
